# Optimizing a Trainium2 kernel written in Bass

```python
import numpy as np
import jax
import jax.numpy as jnp

def _softmax(x, axis=-1):
    return jax.nn.softmax(x, axis=axis)

def _gelu(x):
    return jax.nn.gelu(x, approximate=True)

def _silu(x):
    return jax.nn.silu(x)

def _sigmoid(x):
    return jax.nn.sigmoid(x)

def _layernorm(x, axis=-1, eps=1e-05):
    m = jnp.mean(x, axis=axis, keepdims=True)
    v = jnp.var(x, axis=axis, keepdims=True)
    return (x - m) / jnp.sqrt(v + eps)

def _scatter_add(tgt, idx, src, axis=0):
    return tgt.at[idx].add(src)

def _segment_sum(src, seg, n):
    return jax.ops.segment_sum(src, seg, n)
kernel_name = 'mk_cond_resid_d4_seqx_r8_063930'

def setup_inputs(seed: int=0):
    np.random.seed(seed)
    _w = jnp.asarray

    def _rec_inputs():
        import jax
        import jax.numpy as jnp
        _rk = jax.random.key(seed)
        x = -7.109e-05 + 0.9999 * jax.random.normal(jax.random.fold_in(_rk, 1), (64, 32, 512), jnp.float32)
        _lenS = 32 - jax.random.randint(jax.random.fold_in(_rk, 7), (64,), 0, max(1, 32 // 4) + 1, jnp.int32)
        _lenS2 = 32 - jax.random.randint(jax.random.fold_in(_rk, 8), (64,), 0, max(1, 32 // 4) + 1, jnp.int32)
        itok_B_0_15 = jax.random.randint(jax.random.fold_in(_rk, 11), (64,), 0, 16, jnp.int32)
        itok_B_0_31 = jax.random.randint(jax.random.fold_in(_rk, 12), (64,), 0, 32, jnp.int32)
        itok_Bx16_0_63 = jax.random.randint(jax.random.fold_in(_rk, 13), (64, 16), 0, 64, jnp.int32)
        itok_B_207_1644 = jax.random.randint(jax.random.fold_in(_rk, 14), (64,), 207, 1645, jnp.int32)
        return (x, itok_B_0_15, itok_B_0_31, itok_Bx16_0_63, itok_B_207_1644)
    x, itok_B_0_15, itok_B_0_31, itok_Bx16_0_63, itok_B_207_1644 = _rec_inputs()

    def _L0_cond_setup():
        import jax, jax.numpy as jnp
        import numpy as np
        NUM_CONDITIONS = 16
        IN_CH = 32
        OUT_CH = 32
        B = 64
        T = 512
        key = jax.random.key(seed)
        k_x, k_w, k_c = jax.random.split(key, 3)
        x = jax.random.normal(k_x, (B, IN_CH, T), dtype=jnp.float32)
        bound = float(np.sqrt(6.0 / IN_CH))
        weights = jax.random.uniform(k_w, (NUM_CONDITIONS, IN_CH, OUT_CH), dtype=jnp.float32, minval=-bound, maxval=bound)
        condition = jax.random.randint(k_c, (B,), 0, NUM_CONDITIONS, dtype=jnp.int64)
        return {'x': x, 'weights': weights, 'condition': condition}
    _L0_cond_all = _L0_cond_setup()
    _L0_cond_in = {k: v for k, v in _L0_cond_all.items() if k in ('weights',)}
    del _L0_cond_all

    def _L1_cond_setup():
        import jax, jax.numpy as jnp
        import numpy as np
        MAX_LORAS = 16
        IN, OUT = (512, 512)
        B, S = (8, 256)
        key = jax.random.key(seed)
        k1, k2, k3 = jax.random.split(key, 3)
        x = jax.random.normal(k1, (B, S, IN), dtype=jnp.float32)
        adapter_ids = jax.random.randint(k2, (B,), 0, MAX_LORAS)
        weight = jax.random.normal(k3, (MAX_LORAS, OUT, IN), dtype=jnp.float32) * 0.02
        return {'x': x, 'adapter_ids': adapter_ids, 'weight': weight}
    _L1_cond_all = _L1_cond_setup()
    _L1_cond_in = {k: v for k, v in _L1_cond_all.items() if k in ('weight',)}
    del _L1_cond_all

    def _L2_cond_setup():
        import jax, jax.numpy as jnp
        import numpy as np
        S, C, D = (32, 32, 32)
        B, T = (64, 512)
        key = jax.random.key(seed)
        k_x, k_w, k_s = jax.random.split(key, 3)
        x = jax.random.normal(k_x, (B, C, T), dtype=jnp.float32)
        subjects = jax.random.randint(k_s, (B,), 0, S, dtype=jnp.int64)
        std = float(np.sqrt(2.0 / (C + D)))
        weights = jax.random.normal(k_w, (S, C, D), dtype=jnp.float32) * std * (1.0 / np.sqrt(C))
        biases = jnp.zeros((S, 1, D), dtype=jnp.float32)
        return {'x': x, 'subjects': subjects, 'weights': weights, 'biases': biases}
    _L2_cond_all = _L2_cond_setup()
    _L2_cond_in = {k: v for k, v in _L2_cond_all.items() if k in ('weights', 'biases')}
    del _L2_cond_all

    def _L3_cond_setup():
        import jax, jax.numpy as jnp
        import numpy as np
        B, S, HID = (4, 128, 512)
        D, HQ, HK = (128, 32, 8)
        PAGES, PSIZE, NPP = (64, 32, 16)
        THETA = 10000.0
        EPS = 1e-06
        SCALE = 1.0 / float(np.sqrt(D))

        def _rmsnorm(t, w):
            var = jnp.mean(t * t, axis=-1, keepdims=True)
            return t * jax.lax.rsqrt(var + EPS) * w

        def _rope(t, pos):
            inv_freq = 1.0 / THETA ** (jnp.arange(0, D, 2, dtype=jnp.float32) / D)
            freqs = pos[..., None].astype(jnp.float32) * inv_freq
            cos = jnp.cos(freqs)[:, :, None, :]
            sin = jnp.sin(freqs)[:, :, None, :]
            t1, t2 = (t[..., :D // 2], t[..., D // 2:])
            return jnp.concatenate([t1 * cos - t2 * sin, t2 * cos + t1 * sin], axis=-1)
        key = jax.random.key(seed)
        ks = jax.random.split(key, 10)
        x = jax.random.normal(ks[0], (B, S, HID), jnp.float32)
        Wq = jax.random.normal(ks[1], (HQ * D, HID), jnp.float32) * 0.02
        Wk = jax.random.normal(ks[2], (HK * D, HID), jnp.float32) * 0.02
        Wv = jax.random.normal(ks[3], (HK * D, HID), jnp.float32) * 0.02
        Wo = jax.random.normal(ks[4], (HID, HQ * D), jnp.float32) * 0.02
        q_norm_w = jax.random.uniform(ks[5], (D,), jnp.float32)
        k_norm_w = jax.random.uniform(ks[6], (D,), jnp.float32)
        k_cache = jax.random.normal(ks[7], (PAGES, PSIZE, HK, D), jnp.float32)
        v_cache = jax.random.normal(ks[8], (PAGES, PSIZE, HK, D), jnp.float32)
        block_table = jnp.arange(B * NPP, dtype=jnp.int32).reshape(B, NPP)
        cache_seqlens = jax.random.randint(ks[9], (B,), 0, 475).astype(jnp.int32)
        return dict(x=x, Wq=Wq, Wk=Wk, Wv=Wv, Wo=Wo, q_norm_w=q_norm_w, k_norm_w=k_norm_w, k_cache=k_cache, v_cache=v_cache, block_table=block_table, cache_seqlens=cache_seqlens)
    _L3_cond_all = _L3_cond_setup()
    _L3_cond_in = {k: v for k, v in _L3_cond_all.items() if k in ('Wq', 'Wk', 'Wv', 'Wo', 'q_norm_w', 'k_norm_w', 'k_cache', 'v_cache')}
    del _L3_cond_all
    return {'x': x, 'itok_B_0_15': itok_B_0_15, 'itok_B_0_31': itok_B_0_31, 'itok_Bx16_0_63': itok_Bx16_0_63, 'itok_B_207_1644': itok_B_207_1644, 'L0_cond_weights': _L0_cond_in['weights'], 'L1_cond_weight': _L1_cond_in['weight'], 'L2_cond_weights': _L2_cond_in['weights'], 'L2_cond_biases': _L2_cond_in['biases'], 'L3_cond_Wq': _L3_cond_in['Wq'], 'L3_cond_Wk': _L3_cond_in['Wk'], 'L3_cond_Wv': _L3_cond_in['Wv'], 'L3_cond_Wo': _L3_cond_in['Wo'], 'L3_cond_q_norm_w': _L3_cond_in['q_norm_w'], 'L3_cond_k_norm_w': _L3_cond_in['k_norm_w'], 'L3_cond_k_cache': _L3_cond_in['k_cache'], 'L3_cond_v_cache': _L3_cond_in['v_cache']}

def reference(x, itok_B_0_15, itok_B_0_31, itok_Bx16_0_63, itok_B_207_1644, L0_cond_weights, L1_cond_weight, L2_cond_weights, L2_cond_biases, L3_cond_Wq, L3_cond_Wk, L3_cond_Wv, L3_cond_Wo, L3_cond_q_norm_w, L3_cond_k_norm_w, L3_cond_k_cache, L3_cond_v_cache):
    import jax
    import jax.numpy as jnp

    def _L0_cond_ref(x, weights, condition):
        import jax, jax.numpy as jnp
        import numpy as np
        NUM_CONDITIONS = 16
        IN_CH = 32
        OUT_CH = 32
        B = 64
        T = 512
        W = weights[condition]
        return jnp.einsum('bct,bcd->bdt', x, W)

    def _L1_cond_ref(x, adapter_ids, weight):
        import jax, jax.numpy as jnp
        import numpy as np
        MAX_LORAS = 16
        IN, OUT = (512, 512)
        B, S = (8, 256)
        w = weight[adapter_ids]
        return jnp.einsum('bsi,boi->bso', x, w)

    def _L2_cond_ref(x, subjects, weights, biases):
        import jax, jax.numpy as jnp
        import numpy as np
        S, C, D = (32, 32, 32)
        B, T = (64, 512)
        w = weights[subjects]
        b = biases[subjects]
        out = jnp.einsum('bct,bcd->bdt', x, w)
        return out + jnp.transpose(b, (0, 2, 1))

    def _L3_cond_ref(x, Wq, Wk, Wv, Wo, q_norm_w, k_norm_w, k_cache, v_cache, block_table, cache_seqlens):
        import jax, jax.numpy as jnp
        import numpy as np
        B, S, HID = (4, 128, 512)
        D, HQ, HK = (128, 32, 8)
        PAGES, PSIZE, NPP = (64, 32, 16)
        THETA = 10000.0
        EPS = 1e-06
        SCALE = 1.0 / float(np.sqrt(D))

        def _rmsnorm(t, w):
            var = jnp.mean(t * t, axis=-1, keepdims=True)
            return t * jax.lax.rsqrt(var + EPS) * w

        def _rope(t, pos):
            inv_freq = 1.0 / THETA ** (jnp.arange(0, D, 2, dtype=jnp.float32) / D)
            freqs = pos[..., None].astype(jnp.float32) * inv_freq
            cos = jnp.cos(freqs)[:, :, None, :]
            sin = jnp.sin(freqs)[:, :, None, :]
            t1, t2 = (t[..., :D // 2], t[..., D // 2:])
            return jnp.concatenate([t1 * cos - t2 * sin, t2 * cos + t1 * sin], axis=-1)
        bsz, seqlen, _ = x.shape
        q = jnp.einsum('bsd,ed->bse', x, Wq).reshape(bsz, seqlen, HQ, D)
        k = jnp.einsum('bsd,ed->bse', x, Wk).reshape(bsz, seqlen, HK, D)
        v = jnp.einsum('bsd,ed->bse', x, Wv).reshape(bsz, seqlen, HK, D)
        q = _rmsnorm(q, q_norm_w)
        k = _rmsnorm(k, k_norm_w)
        pos = cache_seqlens[:, None] + jnp.arange(seqlen)[None, :]
        q = _rope(q, pos)
        k = _rope(k, pos)
        L = NPP * PSIZE
        kc = k_cache[block_table].reshape(bsz, L, HK, D)
        vc = v_cache[block_table].reshape(bsz, L, HK, D)
        k_all = jnp.concatenate([kc, k], axis=1)
        v_all = jnp.concatenate([vc, v], axis=1)
        valid_c = jnp.arange(L)[None, :] < cache_seqlens[:, None]
        valid = jnp.concatenate([valid_c, jnp.ones((bsz, seqlen), dtype=bool)], axis=1)
        rep = HQ // HK
        k_all = jnp.repeat(k_all, rep, axis=2)
        v_all = jnp.repeat(v_all, rep, axis=2)
        scores = jnp.einsum('bqhd,bkhd->bhqk', q, k_all) * SCALE
        scores = jnp.where(valid[:, None, None, :], scores, -1e+30)
        probs = jax.nn.softmax(scores, axis=-1)
        o = jnp.einsum('bhqk,bkhd->bqhd', probs, v_all)
        o = o.reshape(bsz, seqlen, HQ * D)
        return jnp.einsum('bse,de->bsd', o, Wo)
    x = x + _L0_cond_ref(x, L0_cond_weights, itok_B_0_15)
    x = x + _L1_cond_ref(x, itok_B_0_15, L1_cond_weight)
    x = x + _L2_cond_ref(x, itok_B_0_31, L2_cond_weights, L2_cond_biases)
    x = x + _L3_cond_ref(x, L3_cond_Wq, L3_cond_Wk, L3_cond_Wv, L3_cond_Wo, L3_cond_q_norm_w, L3_cond_k_norm_w, L3_cond_k_cache, L3_cond_v_cache, itok_Bx16_0_63, itok_B_207_1644)
    return x

_drawn_inputs = setup_inputs


def setup_inputs(seed=0):
    import zlib

    import numpy as np

    out = dict(_drawn_inputs(seed))
    spreads = {'L2_cond_biases': (0.0, 0.1)}
    factors = {'L3_cond_Wq': 2.731,
     'L3_cond_Wk': 8.0,
     'L3_cond_Wv': 8.0,
     'L3_cond_q_norm_w': 4.741,
     'L3_cond_k_norm_w': 8.0,
     'L3_cond_k_cache': 2.75}
    for name, (base, spread) in spreads.items():
        noise = np.random.default_rng([zlib.crc32(name.encode()), seed]).standard_normal(out[name].shape)
        drawn = base * np.exp(spread * noise) if base else spread * noise
        out[name] = jnp.asarray(drawn.astype(out[name].dtype))
    for name, factor in factors.items():
        out[name] = (out[name] * factor).astype(out[name].dtype)
    return out
```

```python
from contextlib import ExitStack

import numpy as np

import concourse.bass as bass
import concourse.mybir as mybir

ALU = mybir.AluOpType
ACT = mybir.ActivationFunctionType
F32 = mybir.dt.float32
I32 = mybir.dt.int32

P = 128
B, S, HID = 64, 32, 512
ROWS = B * S
GB = P // S
G = B // GB
IC = HID // P
CONDS, SUBJ = 16, 32
D, HQ, HK = 128, 32, 8
REP = HQ // HK
PAGES, PSIZE, NPP = 64, 32, 16
L = NPP * PSIZE
KEYS = L + S
PPT = P // PSIZE
KVD = HK * D
RC = ROWS // 512
CB = B // RC
THETA, EPS = 10000.0, 1e-6
SCALE = 1.0 / float(np.sqrt(D))
MASKED = -1e30
PI = float(np.float32(3.1415925))
TWO_PI = (6.28125, float(np.float32(0.0019353071795864769 // 2**-21 * 2**-21)))
TWO_PI += (2 * np.pi - TWO_PI[0] - TWO_PI[1],)
ROUND = 1.5 * 2**23


def rope_frequencies():
    exponent = np.arange(0, D, 2, dtype=np.float32) / np.float32(D)
    f = (1.0 / THETA ** exponent.astype(np.float64)).astype(np.float32)
    return np.concatenate([f, f]).reshape(P, 1)


class Alloc:

    def __init__(self, nc, ctx, stage):
        self.nc, self.ctx, self.stage = nc, ctx, stage

    def sb(self, name, shape, dt=F32):
        return self.ctx.enter_context(self.nc.sbuf_tensor(f"{self.stage}_{name}", shape, dt))

    def ps(self, name, cols=512):
        return self.ctx.enter_context(self.nc.psum_tensor(f"{self.stage}_{name}", [P, cols], F32))

    def sem(self, name, n=None):
        if n is None:
            return self.ctx.enter_context(self.nc.semaphore(f"{self.stage}_{name}"))
        return [self.ctx.enter_context(self.nc.semaphore(f"{self.stage}_{name}{i}")) for i in range(n)]


def stage_prep(nc, weight1, ident, adapters):
    R = 4
    with ExitStack() as ctx:
        a_ = Alloc(nc, ctx, "prep")
        natural = [a_.sb(f"natural{r}", [P, IC, HID]) for r in range(R)]
        turned = [a_.ps(f"turned{c}") for c in range(IC)]
        ident_zero = a_.sem("ident_zero")
        ident_ready = a_.sem("ident_ready")
        loaded = a_.sem("loaded", R)
        transposed = a_.sem("transposed", IC)
        evacuated = a_.sem("evacuated", IC)
        block = ctx.enter_context(nc.Block())

        def load(sp, r, a):
            sp.dma_start(natural[r][:], weight1[bass.ds(a, 1)].rearrange(
                "a (oc p) i -> p (a oc) i", p=P)).then_inc(loaded[r], 16)

        @block.sync
        def _(sp):
            for r in range(R):
                load(sp, r, r)
            with sp.Fori(0, CONDS // R - 1) as i:
                for r in range(R):
                    sp.wait_ge(transposed[IC - 1], i * R + r + 1)
                    load(sp, r, i * R + (r + R))

        @block.gpsimd
        def _(pool):
            nc.gpsimd.memset(ident[:], 0.0).then_inc(ident_zero, 1)
            pool.wait_ge(ident_zero, 1)
            nc.gpsimd.affine_select(out=ident[:], in_=ident[:], compare_op=ALU.not_equal, fill=1.0,
                                    base=0, pattern=[[-1, P]], channel_multiplier=1).then_inc(ident_ready, 1)

        @block.tensor
        def _(pe):
            pe.wait_ge(ident_ready, 1)
            with pe.Fori(0, CONDS // R) as i:
                for r in range(R):
                    pe.wait_ge(loaded[r], i * 16 + 16)
                    for c in range(IC):
                        pe.wait_ge(evacuated[c], i * R + r)
                        for oc in range(IC):
                            last = nc.tensor.transpose(turned[c][:, oc * P:(oc + 1) * P],
                                                       natural[r][:, oc, c * P:(c + 1) * P], ident[:])
                        last.then_inc(transposed[c], 1)

        @block.vector
        def _(dve):
            with dve.Fori(0, CONDS) as a:
                for c in (0, 2):
                    dve.wait_ge(transposed[c], a + 1)
                    nc.vector.tensor_copy(adapters[:, bass.ds(a * IC + c, 1), :].rearrange("p a o -> p (a o)"),
                                          turned[c][:]).then_inc(evacuated[c], 1)

        @block.scalar
        def _(act):
            with act.Fori(0, CONDS) as a:
                for c in (1, 3):
                    act.wait_ge(transposed[c], a + 1)
                    nc.scalar.activation(adapters[:, bass.ds(a * IC + c, 1), :].rearrange("p a o -> p (a o)"),
                                         turned[c][:], ACT.Copy).then_inc(evacuated[c], 1)


def stage_maps(nc, x, cond, subj, w0, w2, bias2, k_cache, ident, adapters, x3_dram, x3t_dram, kt_dram):
    U = 2
    with ExitStack() as ctx:
        a_ = Alloc(nc, ctx, "maps")
        cond_sb = a_.sb("cond", [1, B], I32)
        subj_sb = a_.sb("subj", [1, B], I32)
        w0_all = a_.sb("w0_all", [P, CONDS, S])
        w2_all = a_.sb("w2_all", [P, SUBJ, S])
        bias_rows = a_.sb("bias_rows", [SUBJ, GB, S])
        bias_all = a_.sb("bias_all", [P, SUBJ])
        diag0 = [a_.sb(f"diag0_{u}", [P, P]) for u in range(U)]
        diag2 = [a_.sb(f"diag2_{u}", [P, P]) for u in range(U)]
        bias = [a_.sb(f"bias{u}", [P, 1]) for u in range(U)]
        slots = a_.sb("slots", [P, GB, IC, HID])
        xin = [a_.sb(f"xin{u}", [P, HID]) for u in range(U)]
        xs = [a_.sb(f"xs{u}", [P, HID]) for u in range(U)]
        xt = [a_.sb(f"xt{u}", [P, IC, P]) for u in range(U)]
        k_nat = a_.sb("k_nat", [P, KVD])
        k_turned = [a_.sb(f"k_turned{q}", [P, PPT, HK // 2, PSIZE]) for q in range(2)]
        row_ps = [a_.ps(f"row{u}") for u in range(U)]
        col_ps = [a_.ps(f"col{u}") for u in range(U)]
        k_ps = [a_.ps(f"k{q}") for q in range(2)]

        tables_loaded = a_.sem("tables_loaded")
        ids_loaded = a_.sem("ids_loaded")
        bias_turned = a_.sem("bias_turned")
        bias_ready = a_.sem("bias_ready")
        diag_zero = a_.sem("diag_zero")
        diag_ready = a_.sem("diag_ready", U)
        xin_loaded = a_.sem("xin_loaded", U)
        l0_done = a_.sem("l0_done", U)
        x1_ready = a_.sem("x1_ready", U)
        x1_turned = a_.sem("x1_turned", U)
        x1t_ready = a_.sem("x1t_ready", U)
        slots_ready = a_.sem("slots_ready")
        l1_done = a_.sem("l1_done", U)
        x2_ready = a_.sem("x2_ready", U)
        l2_done = a_.sem("l2_done", U)
        x3_ready = a_.sem("x3_ready", U)
        x3_turned = a_.sem("x3_turned", U)
        x3t_ready = a_.sem("x3t_ready", U)
        x3_stored = a_.sem("x3_stored", U)
        x3t_stored = a_.sem("x3t_stored", U)
        k_loaded = a_.sem("k_loaded")
        k_transposed = a_.sem("k_transposed", 2)
        k_evacuated = a_.sem("k_evacuated", 2)
        k_stored = a_.sem("k_stored", 2)
        block = ctx.enter_context(nc.Block())

        x_rows = x.rearrange("b s t -> (b s) t")
        k_rows = k_cache.rearrange("n k h d -> (n k) (h d)")

        @block.sync
        def _(sp):
            sp.dma_start(cond_sb[:], cond.rearrange("(o b) -> o b", o=1)).then_inc(ids_loaded, 16)
            sp.dma_start(subj_sb[:], subj.rearrange("(o b) -> o b", o=1)).then_inc(ids_loaded, 16)
            for q in range(GB):
                sp.dma_start(w0_all[q * S:(q + 1) * S], w0.rearrange("n c d -> c n d")).then_inc(tables_loaded, 16)
                sp.dma_start(w2_all[q * S:(q + 1) * S], w2.rearrange("n c d -> c n d")).then_inc(tables_loaded, 16)
                sp.dma_start(bias_rows[:, q, :], bias2.rearrange("n o d -> n (o d)")).then_inc(tables_loaded, 16)
            for u in range(U):
                sp.dma_start(xin[u][:], x_rows[u * P:(u + 1) * P]).then_inc(xin_loaded[u], 16)

            def pair(i, more):
                for u in range(U):
                    g = i * U + u
                    sp.wait_ge(k_transposed[1], g)
                    sp.dma_start(k_nat[:], k_rows[bass.ds(g * P, P)]).then_inc(k_loaded, 16)
                    if more:
                        sp.wait_ge(x1_ready[u], i + 1)
                        sp.dma_start(xin[u][:], x_rows[bass.ds((g + U) * P, P)]).then_inc(xin_loaded[u], 16)
                    for q in range(2):
                        sp.wait_ge(k_evacuated[q], g + 1)
                        sp.dma_start(
                            kt_dram[bass.ds(g * PPT, PPT), :, q * (HK // 2):(q + 1) * (HK // 2), :]
                            .rearrange("n d h k -> d n (h k)"),
                            k_turned[q].rearrange("d n h k -> d n (h k)")).then_inc(k_stored[q], 16)
                for u in range(U):
                    g = i * U + u
                    sp.wait_ge(x3_ready[u], i + 1)
                    sp.dma_start(x3_dram[bass.ds(g * P, P)], xs[u][:]).then_inc(x3_stored[u], 16)
                    sp.wait_ge(ids_loaded, 32)
                    sp.wait_ge(x3t_ready[u], i + 1)
                    sp.dma_start(x3t_dram[:, :, bass.ds(g * P, P)], xt[u][:]).then_inc(x3t_stored[u], 16)

            with sp.Fori(0, G // U - 1) as i:
                pair(i, True)
            pair(G // U - 1, False)
            for u in range(U):
                sp.wait_ge(x3_stored[u], 16 * (G // U))
                sp.wait_ge(x3t_stored[u], 16 * (G // U))
            for q in range(2):
                sp.wait_ge(k_stored[q], 16 * G)

        @block.gpsimd
        def _(pool):
            for n, t in enumerate((diag0[0], diag0[1], diag2[0], diag2[1])):
                nc.gpsimd.memset(t[:], 0.0).then_inc(diag_zero, 1)
            pool.wait_ge(diag_zero, 4)
            pool.wait_ge(ids_loaded, 32)
            pool.wait_ge(tables_loaded, 16 * 3 * GB)
            pool.wait_ge(bias_ready, 1)
            with pool.Fori(0, G // U) as i:
                for u in range(U):
                    g = i * U + u
                    _, ids = nc.values_load_multi_w_load_instructions(
                        cond_sb[0:1, bass.ds(g * GB, GB)], engines=(mybir.EngineType.Pool,), min_val=0, max_val=CONDS - 1)
                    _, subs = nc.values_load_multi_w_load_instructions(
                        subj_sb[0:1, bass.ds(g * GB, GB)], engines=(mybir.EngineType.Pool,), min_val=0, max_val=SUBJ - 1)
                    pool.wait_ge(x3_ready[u], i)
                    for q in range(GB):
                        rows = slice(q * S, (q + 1) * S)
                        nc.gpsimd.tensor_copy(diag0[u][rows, q * S:(q + 1) * S],
                                              w0_all[rows, bass.ds(ids[q], 1), :].rearrange("p n d -> p (n d)"))
                        nc.gpsimd.tensor_copy(diag2[u][rows, q * S:(q + 1) * S],
                                              w2_all[rows, bass.ds(subs[q], 1), :].rearrange("p n d -> p (n d)"))
                        last = nc.gpsimd.tensor_copy(bias[u][rows, :], bias_all[rows, bass.ds(subs[q], 1)])
                    last.then_inc(diag_ready[u], 1)

        def adapter_slot(engine, etype, copy, g, qs):
            _, ids = nc.values_load_multi_w_load_instructions(
                cond_sb[0:1, bass.ds(g * GB + qs[0], len(qs))], engines=(etype,), min_val=0, max_val=CONDS - 1)
            for a, q in zip(ids, qs):
                copy(slots[:, q].rearrange("p c o -> p (c o)"),
                     adapters[:, bass.ds(a * IC, IC), :].rearrange("p c o -> p (c o)")).then_inc(slots_ready, 1)

        @block.vector
        def _(dve):
            dve.wait_ge(bias_turned, 1)
            nc.vector.tensor_copy(bias_all[:], k_ps[0][:, 0:SUBJ]).then_inc(bias_ready, 1)
            dve.wait_ge(ids_loaded, 32)

            def evacuate_k(g):
                dve.wait_ge(k_transposed[0], g + 1)
                dve.wait_ge(k_stored[0], g * 16)
                nc.vector.tensor_copy(k_turned[0].rearrange("d n h k -> d h n k"),
                                      k_ps[0].rearrange("d (h n k) -> d h n k", h=HK // 2, n=PPT)
                                      ).then_inc(k_evacuated[0], 1)

            copy = nc.vector.tensor_copy
            with dve.Fori(0, G // U) as i:
                dve.wait_ge(l1_done[1], i)
                adapter_slot(dve, mybir.EngineType.DVE, copy, i * U, (0, 1))
                for u in range(U):
                    dve.wait_ge(l0_done[u], i + 1)
                    dve.wait_ge(xin_loaded[u], i * 16 + 16)
                    dve.wait_ge(x3_stored[u], i * 16)
                    nc.vector.tensor_tensor(xs[u][:], row_ps[u][:], xin[u][:], ALU.add).then_inc(x1_ready[u], 1)
                evacuate_k(i * U)
                dve.wait_ge(l1_done[0], i + 1)
                nc.vector.tensor_tensor(xs[0][:], row_ps[0][:], xs[0][:], ALU.add).then_inc(x2_ready[0], 1)
                adapter_slot(dve, mybir.EngineType.DVE, copy, i * U + 1, (0, 1))
                evacuate_k(i * U + 1)
                dve.wait_ge(l2_done[0], i + 1)
                nc.vector.scalar_tensor_tensor(xs[0][:], row_ps[0][:], bias[0][:, 0:1], xs[0][:],
                                               ALU.add, ALU.add).then_inc(x3_ready[0], 1)
                dve.wait_ge(l1_done[1], i + 1)
                nc.vector.tensor_tensor(xs[1][:], row_ps[1][:], xs[1][:], ALU.add).then_inc(x2_ready[1], 1)
                dve.wait_ge(l2_done[1], i + 1)
                nc.vector.scalar_tensor_tensor(xs[1][:], row_ps[1][:], bias[1][:, 0:1], xs[1][:],
                                               ALU.add, ALU.add).then_inc(x3_ready[1], 1)

        @block.scalar
        def _(act):
            act.wait_ge(ids_loaded, 32)

            def evacuate_k(g):
                act.wait_ge(k_transposed[1], g + 1)
                act.wait_ge(k_stored[1], g * 16)
                nc.scalar.activation(k_turned[1].rearrange("d n h k -> d h n k"),
                                     k_ps[1].rearrange("d (h n k) -> d h n k", h=HK // 2, n=PPT),
                                     ACT.Copy).then_inc(k_evacuated[1], 1)

            def copy(out, in_):
                return nc.scalar.activation(out, in_, ACT.Copy)

            with act.Fori(0, G // U) as i:
                act.wait_ge(l1_done[1], i)
                adapter_slot(act, mybir.EngineType.Activation, copy, i * U, (2, 3))
                for u in range(U):
                    act.wait_ge(x1_turned[u], i + 1)
                    act.wait_ge(x3t_stored[u], i * 16)
                    nc.scalar.activation(xt[u].rearrange("p c r -> p (c r)"), col_ps[u][:],
                                         ACT.Copy).then_inc(x1t_ready[u], 1)
                evacuate_k(i * U)
                act.wait_ge(l1_done[0], i + 1)
                adapter_slot(act, mybir.EngineType.Activation, copy, i * U + 1, (2, 3))
                evacuate_k(i * U + 1)
                for u in range(U):
                    act.wait_ge(x3_turned[u], i + 1)
                    nc.scalar.activation(xt[u].rearrange("p c r -> p (c r)"), col_ps[u][:],
                                         ACT.Copy).then_inc(x3t_ready[u], 1)

        @block.tensor
        def _(pe):
            pe.wait_ge(tables_loaded, 16 * 3 * GB)
            nc.tensor.transpose(k_ps[0][:, 0:SUBJ], bias_rows.rearrange("n q d -> n (q d)"),
                                ident[0:SUBJ, 0:SUBJ]).then_inc(bias_turned, 1)
            pe.wait_ge(bias_ready, 1)

            def turn_x(u, done):
                for c in range(IC):
                    last = nc.tensor.transpose(col_ps[u][:, c * P:(c + 1) * P], xs[u][:, c * P:(c + 1) * P], ident[:])
                last.then_inc(done[u], 1)

            def turn_k(g):
                pe.wait_ge(k_loaded, g * 16 + 16)
                for q in range(2):
                    pe.wait_ge(k_evacuated[q], g)
                    for h in range(HK // 2):
                        col = (q * (HK // 2) + h) * D
                        last = nc.tensor.transpose(k_ps[q][:, h * P:(h + 1) * P], k_nat[:, col:col + D], ident[:])
                    last.then_inc(k_transposed[q], 1)

            def layer1(u, i):
                pe.wait_ge(x1t_ready[u], i + 1)
                pe.wait_ge(slots_ready, i * (U * GB) + (u + 1) * GB)
                for c in range(IC):
                    for q in range(GB):
                        last = nc.tensor.matmul(row_ps[u][q * S:(q + 1) * S, :], xt[u][:, c, q * S:(q + 1) * S],
                                                slots[:, q, c, :], start=(c == 0), stop=(c == IC - 1))
                last.then_inc(l1_done[u], 1)

            with pe.Fori(0, G // U) as i:
                for u in range(U):
                    pe.wait_ge(diag_ready[u], i + 1)
                    pe.wait_ge(xin_loaded[u], i * 16 + 16)
                    pe.wait_ge(x3_ready[u], i)
                    nc.tensor.matmul(row_ps[u][:], diag0[u][:], xin[u][:], start=True, stop=True).then_inc(l0_done[u], 1)
                for u in range(U):
                    pe.wait_ge(x1_ready[u], i + 1)
                    pe.wait_ge(x3t_ready[u], i)
                    turn_x(u, x1_turned)
                turn_k(i * U)
                layer1(0, i)
                turn_k(i * U + 1)
                pe.wait_ge(x2_ready[0], i + 1)
                nc.tensor.matmul(row_ps[0][:], diag2[0][:], xs[0][:], start=True, stop=True).then_inc(l2_done[0], 1)
                layer1(1, i)
                pe.wait_ge(x3_ready[0], i + 1)
                turn_x(0, x3_turned)
                pe.wait_ge(x2_ready[1], i + 1)
                nc.tensor.matmul(row_ps[1][:], diag2[1][:], xs[1][:], start=True, stop=True).then_inc(l2_done[1], 1)
                pe.wait_ge(x3_ready[1], i + 1)
                turn_x(1, x3_turned)


def stage_values(nc, wv, table, seqlens, freq, qw, kw, ident, x3t, rope, stat, v_index, x3t_dram, vn_dram):
    U = 2
    with ExitStack() as ctx:
        a_ = Alloc(nc, ctx, "values")
        wv_nat = a_.sb("wv_nat", [P, HK, HID])
        wvt = a_.sb("wvt", [P, IC, KVD])
        slot = [a_.sb(f"slot{u}", [P, IC, P]) for u in range(U)]
        v_out = [a_.sb(f"v_out{u}", [P, KVD]) for u in range(U)]
        freq_sb = a_.sb("freq", [P, 1])
        wcol = a_.sb("wcol", [P, 4])
        seq_i = a_.sb("seq_i", [P, B], I32)
        seq_f = a_.sb("seq_f", [P, B])
        step_i = a_.sb("step_i", [P, S], I32)
        step_f = a_.sb("step_f", [P, S])
        turns, angle, cosine, sine = (rope[:, n, :] for n in range(4))
        pages_i = a_.sb("pages_i", [P, B, NPP], I32)
        row_i = a_.sb("row_i", [P, 1], I32)
        row_f = a_.sb("row_f", [P, 1])
        w_ps = [a_.ps(f"w{n}") for n in range(2)]
        v_ps = [a_.ps(f"v{u}{n}") for u in range(U) for n in range(2)]

        wv_loaded = a_.sem("wv_loaded")
        x3t_loaded = a_.sem("x3t_loaded")
        small_loaded = a_.sem("small_loaded")
        w_turned = a_.sem("w_turned", 2)
        w_ready = a_.sem("w_ready", 2)
        slot_ready = a_.sem("slot_ready", U)
        v_done = a_.sem("v_done", U)
        v_ready = a_.sem("v_ready", U)
        v_stored = a_.sem("v_stored", U)
        iotas = a_.sem("iotas")
        chain = a_.sem("chain")
        reduced = a_.sem("reduced")
        sines = a_.sem("sines")
        block = ctx.enter_context(nc.Block())

        @block.sync
        def _(sp):
            sp.dma_start(wv_nat[:], wv.rearrange("(h p) i -> p h i", p=P)).then_inc(wv_loaded, 16)
            sp.dma_start(x3t[:], x3t_dram).then_inc(x3t_loaded, 16)
            sp.dma_start(seq_i[:], seqlens.rearrange("(o b) -> o b", o=1).to_broadcast([P, B])).then_inc(small_loaded, 16)
            sp.dma_start(pages_i[:], table.rearrange("(o b) n -> o b n", o=1).to_broadcast([P, B, NPP])).then_inc(small_loaded, 16)
            sp.dma_start(freq_sb[:], freq).then_inc(small_loaded, 16)
            sp.dma_start(wcol[:, 0:1], qw.rearrange("(p o) -> p o", o=1)).then_inc(small_loaded, 16)
            sp.dma_start(wcol[:, 1:2], kw.rearrange("(p o) -> p o", o=1)).then_inc(small_loaded, 16)
            with sp.Fori(0, G // U) as i:
                for u in range(U):
                    sp.wait_ge(v_ready[u], (i + 1) * 2)
                    sp.dma_start(vn_dram[bass.ds((i * U + u) * P, P)], v_out[u][:]).then_inc(v_stored[u], 16)
            for u in range(U):
                sp.wait_ge(v_stored[u], 16 * (G // U))

        @block.gpsimd
        def _(pool):
            nc.gpsimd.iota(step_i[:], pattern=[[1, S]], base=0, channel_multiplier=0).then_inc(iotas, 1)
            pool.wait_ge(iotas, 1)
            for c in range(PPT):
                nc.gpsimd.iota(row_i[c * PSIZE:(c + 1) * PSIZE], pattern=[[1, 1]], base=0,
                               channel_multiplier=1).then_inc(iotas, 1)
            pool.wait_ge(iotas, 1 + PPT)
            pool.wait_ge(x3t_loaded, 16)
            with pool.Fori(0, G // U) as i:
                for u in range(U):
                    pool.wait_ge(v_done[u], i)
                    nc.gpsimd.tensor_copy(slot[u][:], x3t[:, :, bass.ds((i * U + u) * P, P)]).then_inc(slot_ready[u], 1)

        @block.tensor
        def _(pe):
            pe.wait_ge(wv_loaded, 16)
            for h in range(HK):
                n = h % 2
                pe.wait_ge(w_ready[n], h // 2)
                for c in range(IC):
                    last = nc.tensor.transpose(w_ps[n][:, c * P:(c + 1) * P], wv_nat[:, h, c * P:(c + 1) * P], ident[:])
                last.then_inc(w_turned[n], 1)
            for n in range(2):
                pe.wait_ge(w_ready[n], HK // 2)
            with pe.Fori(0, G // U) as i:
                for u in range(U):
                    pe.wait_ge(slot_ready[u], i + 1)
                    pe.wait_ge(v_ready[u], i * 2)
                    for n in range(2):
                        for c in range(IC):
                            last = nc.tensor.matmul(v_ps[2 * u + n][:], slot[u][:, c, :], wvt[:, c, n * 512:(n + 1) * 512],
                                                    start=(c == 0), stop=(c == IC - 1))
                    last.then_inc(v_done[u], 1)

        @block.scalar
        def _(act):
            for h in range(HK):
                act.wait_ge(w_turned[h % 2], h // 2 + 1)
                nc.scalar.activation(wvt[:, :, h * D:(h + 1) * D], w_ps[h % 2].rearrange("p (c e) -> p c e", c=IC),
                                     ACT.Copy).then_inc(w_ready[h % 2], 1)
            act.wait_ge(reduced, 2)
            nc.scalar.activation(sine, angle, ACT.Sin).then_inc(sines, 1)
            nc.scalar.activation(cosine, turns, ACT.Sin).then_inc(sines, 1)
            with act.Fori(0, G // U) as i:
                for u in range(U):
                    act.wait_ge(v_done[u], i + 1)
                    act.wait_ge(v_stored[u], i * 16)
                    for n in range(2):
                        nc.scalar.activation(v_out[u][:, n * 512:(n + 1) * 512], v_ps[2 * u + n][:],
                                             ACT.Copy).then_inc(v_ready[u], 1)

        @block.vector
        def _(dve):
            dve.wait_ge(small_loaded, 16 * 5)
            dve.wait_ge(iotas, 1 + PPT)
            steps = [0]

            def then(instruction):
                steps[0] += 1
                instruction.then_inc(chain, 1)
                dve.wait_ge(chain, steps[0])

            nc_v = nc.vector
            then(nc_v.tensor_copy(seq_f[:], seq_i[:]))
            then(nc_v.tensor_copy(step_f[:], step_i[:]))
            then(nc_v.tensor_copy(row_f[:], row_i[:]))
            then(nc_v.tensor_scalar(wcol[0:64, 2:4], wcol[0:64, 0:2], 1.0, None, ALU.mult))
            then(nc_v.tensor_scalar(wcol[64:P, 2:4], wcol[64:P, 0:2], -1.0, None, ALU.mult))
            shape = [P, B, S]
            then(nc_v.tensor_tensor(angle.rearrange("p (b s) -> p b s", b=B), seq_f.rearrange("p (b o) -> p b o", o=1).to_broadcast(shape),
                                    step_f.rearrange("p (o s) -> p o s", o=1).to_broadcast(shape), ALU.add))
            then(nc_v.tensor_scalar(angle, angle, freq_sb[:, 0:1], None, ALU.mult))
            then(nc_v.tensor_scalar(turns, angle, float(1 / (2 * np.pi)), ROUND, ALU.mult, ALU.add))
            then(nc_v.tensor_scalar(turns, turns, ROUND, None, ALU.subtract))
            for part in TWO_PI:
                then(nc_v.scalar_tensor_tensor(angle, turns, -part, angle, ALU.mult, ALU.add))
            then(nc_v.tensor_scalar(turns, angle, float(np.pi / 2), float(-2 * np.pi), ALU.is_gt, ALU.mult))
            then(nc_v.scalar_tensor_tensor(turns, angle, float(np.pi / 2), turns, ALU.add, ALU.add))
            for t in (angle, turns):
                steps[0] += 1
                nc_v.tensor_scalar(t, t, PI, -PI, ALU.min, ALU.max).then_inc(chain, 1)
                dve.wait_ge(chain, steps[0])
                dve.sem_inc(reduced, 1)
            for c in range(PPT):
                rows = slice(c * PSIZE, (c + 1) * PSIZE)
                then(nc_v.tensor_scalar(v_index[rows, :, :], pages_i[rows, :, :].rearrange("p b (t c) -> p b t c", c=PPT)[:, :, :, c],
                                        float(PSIZE), row_f[rows, 0:1], ALU.mult, ALU.add))
            then(nc_v.tensor_copy(stat[:, :, HK], seq_f[:]))
            dve.wait_ge(sines, 2)
            for n, (src, w) in enumerate(((cosine, 0), (sine, 2), (cosine, 1), (sine, 3))):
                then(nc_v.tensor_scalar(rope[:, n, :], src, wcol[:, w:w + 1], None, ALU.mult))


def stage_projection(nc, wq, wk, wo, ident, x3t, rope, stat, wot, qt_dram, kn_dram):
    with ExitStack() as ctx:
        a_ = Alloc(nc, ctx, "proj")
        M = 1 + REP
        w_nat = a_.sb("w_nat", [P, M, HID])
        w_t = a_.sb("w_t", [P, M, IC, P])
        wo_nat = a_.sb("wo_nat", [P, IC, REP * D])
        ones = a_.sb("ones", [P, P])
        raw = [a_.sb(f"raw{n}", [P, 512]) for n in range(2)]
        squares = [a_.sb(f"squares{m}", [P, 512]) for m in range(M)]
        by_cos = [a_.sb(f"by_cos{n}", [P, 512]) for n in range(2)]
        by_sin = [a_.sb(f"by_sin{n}", [P, 512]) for n in range(2)]
        q_out = [a_.sb(f"q_out{n}", [P, CB, REP, S]) for n in range(2)]
        k_rms = a_.sb("k_rms", [P, 512])
        stat_t = a_.sb("stat_t", [P, CB, S])
        w_ps = [a_.ps(f"w{n}") for n in range(2)]
        proj_ps = [a_.ps(f"proj{n}") for n in range(2)]
        ksum_ps = a_.ps("ksum")
        qsum_ps = a_.ps("qsum")

        w_loaded = a_.sem("w_loaded")
        wo_loaded = a_.sem("wo_loaded")
        w_turned = a_.sem("w_turned", 2)
        w_ready = a_.sem("w_ready", 2)
        wo_turned = a_.sem("wo_turned", 2)
        wo_ready = a_.sem("wo_ready", 2)
        ones_ready = a_.sem("ones_ready")
        proj_done = a_.sem("proj_done")
        raw_ready = a_.sem("raw_ready")
        squared = a_.sem("squared")
        ksum_done = a_.sem("ksum_done")
        k_mean = a_.sem("k_mean")
        k_root = a_.sem("k_root")
        k_scaled = a_.sem("k_scaled")
        inverted = a_.sem("inverted")
        qsum_done = a_.sem("qsum_done")
        stat_turned = a_.sem("stat_turned")
        stat_ready = a_.sem("stat_ready")
        products = a_.sem("products")
        rotated = a_.sem("rotated")
        q_stored = a_.sem("q_stored", 2)
        k_stored = a_.sem("k_stored", 2)
        k_out = [a_.sb(f"k_out{n}", [P, CB, S]) for n in range(2)]
        block = ctx.enter_context(nc.Block())
        TPH = RC * M

        @block.sync
        def _(sp):
            def load_weights(h):
                sp.dma_start(w_nat[:, 0, :], wk[bass.ds(h * D, D)]).then_inc(w_loaded, 16)
                sp.dma_start(w_nat[:, 1:M, :], wq[bass.ds(h * (REP * D), REP * D)]
                             .rearrange("(m p) i -> p m i", p=P)).then_inc(w_loaded, 16)

            def load_wo(h):
                sp.dma_start(wo_nat[:], wo.rearrange("(c p) e -> p c e", p=P)[:, :, bass.ds(h * (REP * D), REP * D)]
                             ).then_inc(wo_loaded, 16)

            def store_k(h, rc):
                sp.wait_ge(k_scaled, h * RC + rc + 1)
                sp.dma_start(kn_dram[rc * CB:(rc + 1) * CB, :, bass.ds(h, 1), :].rearrange("b d h s -> d b (h s)"),
                             k_out[rc % 2][:]).then_inc(k_stored[rc % 2], 16)

            def head(h, more):
                for rc in range(RC):
                    sp.wait_ge(rotated, h * TPH + (rc + 1) * M)
                    sp.dma_start(qt_dram[bass.ds(h, 1), :, rc * CB:(rc + 1) * CB, :].rearrange("h d b n -> d (h b n)"),
                                 q_out[rc % 2].rearrange("d b r s -> d (b r s)")).then_inc(q_stored[rc % 2], 16)
                    if rc > 0:
                        store_k(h, rc - 1)
                    if rc == 1 and more:
                        sp.wait_ge(w_turned[0], h * 3 + 3)
                        sp.wait_ge(w_turned[1], h * 2 + 2)
                        load_weights(h + 1)
                        sp.wait_ge(w_loaded, 32)
                        for n in range(2):
                            sp.wait_ge(wo_turned[n], h * 2 + 2)
                        load_wo(h + 1)
                store_k(h, RC - 1)

            load_weights(0)
            load_wo(0)
            with sp.Fori(0, HK - 1) as h:
                head(h, True)
            head(HK - 1, False)
            for n in range(2):
                sp.wait_ge(q_stored[n], 16 * HK * (RC // 2))
                sp.wait_ge(k_stored[n], 16 * HK * (RC // 2))

        @block.tensor
        def _(pe):
            pe.wait_ge(ones_ready, 1)
            with pe.Fori(0, HK) as h:
                pe.wait_ge(w_loaded, h * 32 + 32)
                for m in range(M):
                    pe.wait_ge(w_ready[m % 2], h * (3 if m % 2 == 0 else 2) + m // 2)
                    for c in range(IC):
                        last = nc.tensor.transpose(w_ps[m % 2][:, c * P:(c + 1) * P], w_nat[:, m, c * P:(c + 1) * P], ident[:])
                    last.then_inc(w_turned[m % 2], 1)

                def sums(rc):
                    pe.wait_ge(squared, h * TPH + (rc + 1) * M)
                    pe.wait_ge(k_mean, h * RC + rc)
                    nc.tensor.matmul(ksum_ps[:], ones[:], squares[0][:], start=True, stop=True).then_inc(ksum_done, 1)
                    pe.wait_ge(stat_turned, h * RC + rc)
                    for r in range(REP):
                        last = nc.tensor.matmul(qsum_ps[r * S:(r + 1) * S, :], ones[:, 0:S], squares[1 + r][:],
                                                start=True, stop=True)
                    last.then_inc(qsum_done, 1)

                for rc in range(RC):
                    for m in range(M):
                        t = rc * M + m
                        if rc == 0:
                            pe.wait_ge(w_ready[m % 2], h * (3 if m % 2 == 0 else 2) + m // 2 + 1)
                        if t >= 2:
                            pe.wait_ge(raw_ready, h * TPH + t - 1)
                        else:
                            pe.wait_ge(raw_ready, h * TPH)
                        for c in range(IC):
                            last = nc.tensor.matmul(proj_ps[t % 2][:], w_t[:, m, c, :], x3t[:, c, rc * 512:(rc + 1) * 512],
                                                    start=(c == 0), stop=(c == IC - 1))
                        last.then_inc(proj_done, 1)
                        if m == 1 and rc > 0:
                            sums(rc - 1)
                    if rc == 0:
                        pe.wait_ge(wo_loaded, h * 16 + 16)
                        for r in range(REP):
                            pe.wait_ge(w_ready[0], h * 3 + 3)
                            pe.wait_ge(w_ready[1], h * 2 + 2)
                            pe.wait_ge(wo_ready[r % 2], h * 2 + r // 2)
                            for c in range(IC):
                                last = nc.tensor.transpose(w_ps[r % 2][:, c * P:(c + 1) * P],
                                                           wo_nat[:, c, r * D:(r + 1) * D], ident[:])
                            last.then_inc(wo_turned[r % 2], 1)
                pe.wait_ge(wo_ready[0], h * 2 + 2)
                pe.wait_ge(wo_ready[1], h * 2 + 2)
                sums(RC - 1)

        @block.scalar
        def _(act):
            with act.Fori(0, HK) as h:
                for m in range(M):
                    act.wait_ge(w_turned[m % 2], h * (3 if m % 2 == 0 else 2) + m // 2 + 1)
                    act.wait_ge(proj_done, h * TPH)
                    nc.scalar.activation(w_t[:, m].rearrange("p c e -> p (c e)"), w_ps[m % 2][:], ACT.Copy).then_inc(w_ready[m % 2], 1)

                def root(rc):
                    act.wait_ge(k_mean, h * RC + rc + 1)
                    nc.scalar.activation(k_rms[:], k_rms[:], ACT.Sqrt).then_inc(k_root, 1)

                for rc in range(RC):
                    for m in range(M):
                        t = rc * M + m
                        act.wait_ge(proj_done, h * TPH + t + 1)
                        if t >= 2:
                            act.wait_ge(products, h * TPH + t - 1)
                        else:
                            act.wait_ge(products, h * TPH)
                        nc.scalar.activation(raw[t % 2][:], proj_ps[t % 2][:], ACT.Copy).then_inc(raw_ready, 1)
                        act.wait_ge(raw_ready, h * TPH + t + 1)
                        act.wait_ge(qsum_done, h * RC + rc)
                        nc.scalar.activation(squares[m][:], raw[t % 2][:], ACT.Square).then_inc(squared, 1)
                        if m == 2 and rc > 0:
                            root(rc - 1)
                    if rc == 0:
                        for r in range(REP):
                            act.wait_ge(wo_turned[r % 2], h * 2 + r // 2 + 1)
                            nc.scalar.activation(wot[:, bass.ds(h * REP + r, 1), :].rearrange("p a e -> p (a e)"),
                                                 w_ps[r % 2][:], ACT.Copy).then_inc(wo_ready[r % 2], 1)

                root(RC - 1)
            act.wait_ge(k_mean, HK * RC + 1)
            nc.scalar.activation(stat[:, :, 0:HK], stat[:, :, 0:HK], ACT.Sqrt).then_inc(k_root, 1)

        @block.vector
        def _(dve):
            with dve.Fori(0, HK) as h:
                def rotate(t):
                    rc, m = divmod(t, M)
                    cols = slice(rc * 512, (rc + 1) * 512)
                    cos, sin = (2, 3) if m == 0 else (0, 1)
                    n = t % 2
                    dve.wait_ge(raw_ready, h * TPH + t + 1)
                    dve.wait_ge(rotated, h * TPH + (t - 1 if t >= 2 else 0))
                    nc.vector.tensor_tensor(by_cos[n][:], raw[n][:], rope[:, cos, cols], ALU.mult)
                    nc.vector.tensor_tensor(by_sin[n][0:64], raw[n][64:P], rope[64:P, sin, cols], ALU.mult)
                    nc.vector.tensor_tensor(by_sin[n][64:P], raw[n][0:64], rope[0:64, sin, cols],
                                            ALU.mult).then_inc(products, 1)

                def statistics(rc):
                    dve.wait_ge(ksum_done, h * RC + rc + 1)
                    dve.wait_ge(k_scaled, h * RC + rc)
                    nc.vector.tensor_scalar(k_rms[:], ksum_ps[:], 1.0 / D, EPS, ALU.mult, ALU.add).then_inc(k_mean, 1)
                    dve.wait_ge(qsum_done, h * RC + rc + 1)
                    dve.wait_ge(stat_ready, h * RC + rc)
                    nc.vector.transpose(stat_t.rearrange("p b s -> p (b s)"), qsum_ps[:]).then_inc(stat_turned, 1)
                    dve.wait_ge(stat_turned, h * RC + rc + 1)
                    nc.vector.tensor_copy(stat[:, rc * CB:(rc + 1) * CB, bass.ds(h, 1)], stat_t[:, :, 0:1]).then_inc(stat_ready, 1)

                def scale_k(rc):
                    dve.wait_ge(k_root, h * RC + rc + 1)
                    nc.vector.reciprocal(k_rms[:], k_rms[:]).then_inc(inverted, 1)
                    dve.wait_ge(inverted, h * RC + rc + 1)
                    dve.wait_ge(rotated, h * TPH + rc * M + 1)
                    kf = k_out[rc % 2].rearrange("d b s -> d (b s)")
                    nc.vector.tensor_tensor(kf, kf, k_rms[:], ALU.mult).then_inc(k_scaled, 1)

                for t in range(TPH):
                    rc, m = divmod(t, M)
                    if rc > 0 and m == 3:
                        statistics(rc - 1)
                    rotate(t)
                    if rc > 0 and m == 4:
                        scale_k(rc - 1)
                statistics(RC - 1)
                scale_k(RC - 1)
            dve.wait_ge(stat_ready, HK * RC)
            qs = stat[:, :, 0:HK]
            nc.vector.tensor_scalar(qs, qs, 1.0 / D, EPS, ALU.mult, ALU.add).then_inc(k_mean, 1)
            dve.wait_ge(k_root, HK * RC + 1)
            nc.vector.reciprocal(qs, qs).then_inc(inverted, 1)
            dve.wait_ge(inverted, HK * RC + 1)
            nc.vector.tensor_scalar(qs, qs, -SCALE, None, ALU.mult).then_inc(inverted, 1)

        @block.gpsimd
        def _(pool):
            nc.gpsimd.memset(ones[:], 1.0).then_inc(ones_ready, 1)
            with pool.Fori(0, HK) as h:
                for t in range(TPH):
                    rc, m = divmod(t, M)
                    pool.wait_ge(products, h * TPH + t + 1)
                    if m == 0:
                        pool.wait_ge(k_stored[rc % 2], h * 32 + (rc // 2) * 16)
                        out = k_out[rc % 2][:]
                    else:
                        if m == 1:
                            pool.wait_ge(q_stored[rc % 2], h * 32 + (rc // 2) * 16)
                        out = q_out[rc % 2][:, :, m - 1, :]
                    n = t % 2
                    nc.gpsimd.tensor_tensor(out, by_cos[n].rearrange("d (b s) -> d b s", s=S),
                                            by_sin[n].rearrange("d (b s) -> d b s", s=S), ALU.add).then_inc(rotated, 1)


def stage_attention(nc, table, v_cache, ident, stat, wot, v_index, kt_dram, kn_dram, qt_dram, vn_dram, x3_dram, out):
    N = GB * HK
    RING = 4
    with ExitStack() as ctx:
        a_ = Alloc(nc, ctx, "att")
        pages_sb = a_.sb("pages", [1, B * NPP], I32)
        keys = [a_.sb(f"keys{v}", [P, NPP + 1, HK, PSIZE]) for v in range(2)]
        queries = [a_.sb(f"queries{v}", [P, HK, P]) for v in range(2)]
        values = [a_.sb(f"values{v}", [P, PPT, KVD]) for v in range(2)]
        new_values = [a_.sb(f"new_values{v}", [P, KVD]) for v in range(2)]
        v_rows_of = [a_.sb(f"v_rows_of{v}", [P, PPT], I32) for v in range(2)]
        key_no_i = a_.sb("key_no_i", [P, L], I32)
        key_no = a_.sb("key_no", [P, L])
        batch_cols = a_.sb("batch_cols", [P, HK + 1])
        mask = a_.sb("mask", [P, KEYS])
        probs = [a_.sb(f"probs{k}", [P, KEYS]) for k in range(RING)]
        low = [a_.sb(f"low{k}", [P, 1]) for k in range(RING)]
        total = [a_.sb(f"total{k}", [P, 1]) for k in range(RING)]
        inverse = [a_.sb(f"inverse{k}", [P, 1]) for k in range(RING)]
        probs_t = [a_.sb(f"probs_t{n}", [P, L]) for n in range(2)]
        new_probs_t = [a_.sb(f"new_probs_t{n}", [P, P]) for n in range(2)]
        heads_out = a_.sb("heads_out", [P, HK, REP, GB, S])
        x3 = a_.sb("x3", [P, HID])
        y = a_.sb("y", [P, HID])
        score_ps = [a_.ps(f"score{n}", 1024) for n in range(2)]
        turn_ps = [a_.ps(f"turn{n}") for n in range(2)]
        o_ps = a_.ps("o")
        last_ps = a_.ps("last")

        pages_loaded = a_.sem("pages_loaded")
        kq_loaded = a_.sem("kq_loaded", 2)
        v_loaded = a_.sem("v_loaded", 2)
        zeroed = a_.sem("zeroed")
        index_ready = a_.sem("index_ready")
        iota_done = a_.sem("iota_done")
        setup = a_.sem("setup")
        cols_ready = a_.sem("cols_ready")
        mask_ready = a_.sem("mask_ready")
        scores_done = a_.sem("scores_done", 2)
        scores_masked = a_.sem("scores_masked", 2)
        exp_done = a_.sem("exp_done")
        inverse_ready = a_.sem("inverse_ready")
        probs_ready = a_.sem("probs_ready")
        main_turned = a_.sem("main_turned", 2)
        all_turned = a_.sem("all_turned", RING)
        main_ready = a_.sem("main_ready", 2)
        new_ready = a_.sem("new_ready")
        o_done = a_.sem("o_done", 2)
        o_ready = a_.sem("o_ready")
        y_done = a_.sem("y_done")
        x3_loaded = a_.sem("x3_loaded")
        y_ready = a_.sem("y_ready")
        y_stored = a_.sem("y_stored")
        block = ctx.enter_context(nc.Block())

        KQ = 16 * (NPP + 2)
        VN = 16 * (PPT + 1)

        @block.sync
        def _(sp):
            sp.dma_start(pages_sb[:], table.rearrange("(o b) n -> o (b n)", o=1)).then_inc(pages_loaded, 16)
            sp.wait_ge(pages_loaded, 16)

            def load(v, b):
                sp.dma_start(queries[v][:], qt_dram[:, :, bass.ds(b, 1), :].rearrange("h d b n -> d h (b n)")).then_inc(kq_loaded[v], 16)
                sp.dma_start(keys[v][:, NPP], kn_dram[bass.ds(b, 1)].rearrange("b d h s -> d (b h) s")).then_inc(kq_loaded[v], 16)
                _, pages = nc.values_load_multi_w_load_instructions(
                    pages_sb[0:1, bass.ds(b * NPP, NPP)], engines=(mybir.EngineType.SP,), min_val=0, max_val=PAGES - 1)
                for n in range(NPP):
                    sp.dma_start(keys[v][:, n], kt_dram[bass.ds(pages[n], 1)].rearrange("n d h k -> d (n h) k")).then_inc(kq_loaded[v], 16)

            for v in range(2):
                load(v, v)
            with sp.Fori(0, B // 2 - 1) as i:
                for v in range(2):
                    sp.wait_ge(scores_done[1], i * HK + (v + 1) * (HK // 2))
                    load(v, i * 2 + (v + 2))

        @block.gpsimd
        def _(pool):
            nc.gpsimd.iota(key_no_i[:], pattern=[[1, L]], base=0, channel_multiplier=0).then_inc(iota_done, 1)
            for v in range(2):
                nc.gpsimd.memset(new_values[v][:], 0.0).then_inc(zeroed, 1)
                nc.gpsimd.memset(new_probs_t[v][:], 0.0).then_inc(zeroed, 1)
            pool.wait_ge(zeroed, 4)
            v_rows = v_cache.rearrange("n k h d -> (n k) (h d)")

            def load(v, b, parts):
                if 0 in parts:
                    nc.gpsimd.dma_start(new_values[v][0:S, :], vn_dram[bass.ds(b * S, S)]).then_inc(v_loaded[v], 16)
                    load_index(v, b)
                for t in range(PPT):
                    if t + 1 in parts:
                        nc.gpsimd.indirect_dma_start(
                            values[v][:, t, :], None, v_rows,
                            bass.IndirectOffsetOnAxis(ap=v_rows_of[v][:, t:t + 1], axis=0)).then_inc(v_loaded[v], 16)

            def load_index(v, b):
                nc.gpsimd.tensor_copy(v_rows_of[v][:], v_index[:, bass.ds(b, 1), :].rearrange("p b t -> p (b t)")).then_inc(index_ready, 1)
                pool.lower_val(b + 1)
                pool.wait_ge(zeroed, 4)
                pool.wait_ge(index_ready, b + 1)

            def group(g, last_group):
                for n in range(N):
                    j, h = divmod(n, HK)
                    if h >= 3 and not (last_group and j == GB - 1):
                        if h == 3:
                            pool.wait_ge(o_done[1], g * (N // 2) + j * (HK // 2))
                        load((j + 1) % 2, g * GB + (j + 1), [h - 3])
                    pool.wait_ge(inverse_ready, g * N + n + 1)
                    k = n % RING
                    nc.gpsimd.tensor_tensor(probs[k][:], probs[k][:], inverse[k][:, 0:1].to_broadcast([P, KEYS]),
                                            ALU.mult).then_inc(probs_ready, 1)

            load(0, 0, range(1 + PPT))
            with pool.Fori(0, G - 1) as g:
                group(g, False)
            group(G - 1, True)

        @block.tensor
        def _(pe):
            with pe.Fori(0, G) as g:
                def scores(n):
                    j, h = divmod(n, HK)
                    if h == 0:
                        pe.wait_ge(kq_loaded[j % 2], g * (2 * KQ) + (j // 2 + 1) * KQ)
                    pe.wait_ge(scores_masked[n % 2], g * (N // 2) + n // 2)
                    nc.tensor.matmul(score_ps[n % 2][:, 0:L], queries[j % 2][:, h, :], keys[j % 2][:, 0:NPP, h, :], start=True, stop=True)
                    nc.tensor.matmul(score_ps[n % 2][:, L:KEYS], queries[j % 2][:, h, :], keys[j % 2][:, NPP, h, :],
                                     start=True, stop=True).then_inc(scores_done[n % 2], 1)

                def turn(n):
                    pe.wait_ge(probs_ready, g * N + n + 1)
                    pe.wait_ge(main_ready[n % 2], g * (N // 2) + n // 2)
                    for t in range(PPT):
                        last = nc.tensor.transpose(turn_ps[n % 2][:, t * P:(t + 1) * P], probs[n % RING][:, t * P:(t + 1) * P], ident[:])
                    last.then_inc(main_turned[n % 2], 1)
                    pe.wait_ge(new_ready, g * N + n)
                    if n == 0:
                        pe.wait_ge(y_ready, g)
                    nc.tensor.transpose(last_ps[0:S, 0:P], probs[n % RING][:, L:KEYS], ident[:]).then_inc(all_turned[n % RING], 1)

                def weigh(n):
                    j, h = divmod(n, HK)
                    if h == 0:
                        pe.wait_ge(v_loaded[j % 2], g * (2 * VN) + (j // 2 + 1) * VN)
                    pe.wait_ge(main_ready[n % 2], g * (N // 2) + n // 2 + 1)
                    pe.wait_ge(new_ready, g * N + n + 1)
                    pe.wait_ge(o_ready, g * N + n)
                    for t in range(PPT):
                        nc.tensor.matmul(o_ps[:, 0:P], values[j % 2][:, t, h * D:(h + 1) * D], probs_t[n % 2][:, t * P:(t + 1) * P],
                                         start=(t == 0), stop=False)
                    nc.tensor.matmul(o_ps[:, 0:P], new_values[j % 2][:, h * D:(h + 1) * D], new_probs_t[n % 2][:],
                                     start=False, stop=True).then_inc(o_done[n % 2], 1)

                def project(h):
                    pe.wait_ge(o_ready, g * N + (N - HK) + h + 1)
                    for r in range(REP):
                        last = nc.tensor.matmul(last_ps[:], heads_out[:, h, r].rearrange("d j s -> d (j s)"), wot[:, h * REP + r, :],
                                                start=(h == 0 and r == 0), stop=(h == HK - 1 and r == REP - 1))
                    return last

                for n in range(N):
                    scores(n)
                    if n >= 2:
                        turn(n - 2)
                    if n >= 3:
                        weigh(n - 3)
                turn(N - 2)
                weigh(N - 3)
                turn(N - 1)
                weigh(N - 2)
                pe.wait_ge(new_ready, g * N + N)
                for h in range(HK - 4):
                    project(h)
                weigh(N - 1)
                for h in range(HK - 4, HK):
                    last = project(h)
                last.then_inc(y_done, 1)

        @block.scalar
        def _(act):
            act.wait_ge(zeroed, 4)
            with act.Fori(0, G) as g:
                def softmax(n):
                    act.wait_ge(scores_masked[n % 2], g * (N // 2) + n // 2 + 1)
                    k = n % RING
                    nc.scalar.activation(probs[k][:], probs[k][:], ACT.Exp, bias=low[k][:, 0:1], scale=-1.0,
                                         accum_out=total[k][:, 0:1]).then_inc(exp_done, 1)

                def new_part(n):
                    act.wait_ge(all_turned[n % RING], g * (N // RING) + n // RING + 1)
                    act.wait_ge(o_done[n % 2], g * (N // 2) + n // 2)
                    nc.scalar.activation(new_probs_t[n % 2][0:S, :], last_ps[0:S, 0:P], ACT.Copy).then_inc(new_ready, 1)

                def keep_o(n):
                    j, h = divmod(n, HK)
                    act.wait_ge(o_done[n % 2], g * (N // 2) + n // 2 + 1)
                    if n == 0:
                        act.wait_ge(y_done, g)
                    nc.scalar.activation(heads_out[:, h, :, j, :], o_ps[:, 0:P].rearrange("d (r s) -> d r s", r=REP),
                                         ACT.Copy).then_inc(o_ready, 1)

                act.wait_ge(y_ready, g)
                act.dma_start(x3[:], x3_dram[bass.ds(g * P, P)]).then_inc(x3_loaded, 16)
                for n in range(N + 3):
                    if n < N:
                        softmax(n)
                    if 2 <= n < N + 2:
                        new_part(n - 2)
                    if n >= 3:
                        keep_o(n - 3)
                act.wait_ge(y_ready, g + 1)
                act.dma_start(out[bass.ds(g * P, P)], y[:]).then_inc(y_stored, 16)
            act.wait_ge(y_stored, 16 * G)

        @block.vector
        def _(dve):
            dve.wait_ge(iota_done, 1)
            nc.vector.tensor_copy(key_no[:], key_no_i[:]).then_inc(setup, 1)
            nc.vector.memset(mask[:, L:KEYS], 0.0).then_inc(setup, 1)
            dve.wait_ge(setup, 2)
            with dve.Fori(0, G) as g:
                def begin_batch(j):
                    dve.wait_ge(scores_masked[1], g * (N // 2) + j * (HK // 2))
                    nc.vector.tensor_copy(batch_cols[:], stat[:, bass.ds(g * GB + j, 1), :].rearrange("p b c -> p (b c)")).then_inc(cols_ready, 1)
                    dve.wait_ge(cols_ready, g * GB + j + 1)
                    nc.vector.tensor_scalar(mask[:, 0:L], key_no[:], batch_cols[:, HK:HK + 1], MASKED, ALU.is_ge, ALU.mult).then_inc(mask_ready, 1)
                    dve.wait_ge(mask_ready, g * GB + j + 1)

                def mask_scores(n):
                    h = n % HK
                    k = n % RING
                    dve.lower_val(g * (N // 2) + (n // 2 + 1))
                    dve.lower_val(g * (N // RING) + n // RING)
                    dve.wait_ge(setup, 2)
                    dve.wait_ge(scores_done[n % 2], g * (N // 2) + n // 2 + 1)
                    dve.wait_ge(all_turned[k], g * (N // RING) + n // RING)
                    nc.vector.tensor_tensor_reduce(out=probs[k][:], in0=score_ps[n % 2][:, 0:KEYS], in1=mask[:],
                                                   scale=batch_cols[:, h:h + 1], scalar=3e38, op0=ALU.add, op1=ALU.min,
                                                   accum_out=low[k][:, 0:1]).then_inc(scores_masked[n % 2], 1)

                def invert(n):
                    dve.wait_ge(exp_done, g * N + n + 1)
                    nc.vector.reciprocal(inverse[n % RING][:], total[n % RING][:]).then_inc(inverse_ready, 1)

                def main_part(n):
                    dve.wait_ge(main_turned[n % 2], g * (N // 2) + n // 2 + 1)
                    dve.wait_ge(o_done[n % 2], g * (N // 2) + n // 2)
                    nc.vector.tensor_copy(probs_t[n % 2][:], turn_ps[n % 2][:]).then_inc(main_ready[n % 2], 1)

                for n in range(N + 2):
                    if n < N:
                        if n % HK == 0:
                            begin_batch(n // HK)
                        mask_scores(n)
                    if 1 <= n < N + 1:
                        invert(n - 1)
                    if n >= 2:
                        main_part(n - 2)
                dve.wait_ge(y_done, g + 1)
                dve.wait_ge(x3_loaded, g * 16 + 16)
                dve.wait_ge(y_stored, g * 16)
                nc.vector.tensor_tensor(y[:], last_ps[:], x3[:], ALU.add).then_inc(y_ready, 1)


INPUTS = ["x", "itok_B_0_15", "itok_B_0_31", "itok_Bx16_0_63", "itok_B_207_1644", "L0_cond_weights",
          "L1_cond_weight", "L2_cond_weights", "L2_cond_biases", "L3_cond_Wq", "L3_cond_Wk", "L3_cond_Wv",
          "L3_cond_Wo", "L3_cond_q_norm_w", "L3_cond_k_norm_w", "L3_cond_k_cache", "L3_cond_v_cache"]


def program(nc, ins, freq, out):
    (x, cond, subj, table, seqlens, w0, w1, w2, b2, wq, wk, wv, wo, qw, kw, kc, vc) = ins

    def scratch(name, shape):
        return nc.dram_tensor(name, shape, F32, kind="Internal").ap()

    x3_dram = scratch("x3_rows", [ROWS, HID])
    x3t_dram = scratch("x3_cols", [P, IC, ROWS])
    kt_dram = scratch("k_cache_t", [PAGES, D, HK, PSIZE])
    vn_dram = scratch("v_new", [ROWS, KVD])
    kn_dram = scratch("k_new_t", [B, D, HK, S])
    qt_dram = scratch("q_t", [HK, D, B, REP * S])

    with ExitStack() as ctx:
        ident = ctx.enter_context(nc.sbuf_tensor("ident", [P, P], F32))
        with nc.sbuf_tensor("adapters", [P, CONDS * IC, HID], F32) as adapters:
            stage_prep(nc, w1, ident, adapters)
            stage_maps(nc, x, cond, subj, w0, w2, b2, kc, ident, adapters, x3_dram, x3t_dram, kt_dram)
        stat = ctx.enter_context(nc.sbuf_tensor("stat", [P, B, HK + 1], F32))
        v_index = ctx.enter_context(nc.sbuf_tensor("v_index", [P, B, PPT], I32))
        wot = ctx.enter_context(nc.sbuf_tensor("wot", [P, HQ, HID], F32))
        with nc.sbuf_tensor("x3t", [P, IC, ROWS], F32) as x3t, nc.sbuf_tensor("rope", [P, 4, ROWS], F32) as rope:
            stage_values(nc, wv, table, seqlens, freq, qw, kw, ident, x3t, rope, stat, v_index, x3t_dram, vn_dram)
            stage_projection(nc, wq, wk, wo, ident, x3t, rope, stat, wot, qt_dram, kn_dram)
        stage_attention(nc, table, vc, ident, stat, wot, v_index, kt_dram, kn_dram, qt_dram, vn_dram, x3_dram,
                        out.rearrange("b s t -> (b s) t"))


def kernel(**inputs):
    import concourse.bacc as bacc
    from concourse.bass_utils import run_bass_kernel_spmd

    nc = bacc.Bacc("TRN2", target_bir_lowering=False, num_devices=1)
    arrays, ins = {}, []
    for name in INPUTS:
        a = np.ascontiguousarray(inputs[name])
        arrays[name] = a
        ins.append(nc.dram_tensor(name, a.shape, mybir.dt.from_np(a.dtype), kind="ExternalInput").ap())
    arrays["rope_freq"] = rope_frequencies()
    freq = nc.dram_tensor("rope_freq", (P, 1), F32, kind="ExternalInput").ap()
    out = nc.dram_tensor("out", (B, S, HID), F32, kind="ExternalOutput").ap()
    program(nc, ins, freq, out)
    r = run_bass_kernel_spmd(nc, [arrays], core_ids=[0])
    return r.results[0]["out"]
```

```python
from contextlib import ExitStack

import numpy as np

import concourse.bass as bass
import concourse.mybir as mybir

ALU = mybir.AluOpType
ACT = mybir.ActivationFunctionType
F32 = mybir.dt.float32
F32R = mybir.dt.float32r
I32 = mybir.dt.int32

P = 128
B, S, HID = 64, 32, 512
ROWS = B * S
GB = P // S
G = B // GB
IC = HID // P
CONDS, SUBJ = 16, 32
D, HQ, HK = 128, 32, 8
REP = HQ // HK
PAGES, PSIZE, NPP = 64, 32, 16
L = NPP * PSIZE
KEYS = L + S
PPT = P // PSIZE
KVD = HK * D
RC = ROWS // 512
CB = B // RC
THETA, EPS = 10000.0, 1e-6
SCALE = 1.0 / float(np.sqrt(D))
MASKED = -1e30
PI = float(np.float32(3.1415925))
TWO_PI = (6.28125, float(np.float32(0.0019353071795864769 // 2**-21 * 2**-21)))
TWO_PI += (2 * np.pi - TWO_PI[0] - TWO_PI[1],)
ROUND = 1.5 * 2**23


def rope_frequencies():
    exponent = np.arange(0, D, 2, dtype=np.float32) / np.float32(D)
    f = (1.0 / THETA ** exponent.astype(np.float64)).astype(np.float32)
    return np.concatenate([f, f]).reshape(P, 1)


class Alloc:

    def __init__(self, nc, ctx, stage):
        self.nc, self.ctx, self.stage = nc, ctx, stage

    def sb(self, name, shape, dt=F32):
        return self.ctx.enter_context(self.nc.sbuf_tensor(f"{self.stage}_{name}", shape, dt))

    def ps(self, name, cols=512):
        return self.ctx.enter_context(self.nc.psum_tensor(f"{self.stage}_{name}", [P, cols], F32))

    def sem(self, name, n=None):
        if n is None:
            return self.ctx.enter_context(self.nc.semaphore(f"{self.stage}_{name}"))
        return [self.ctx.enter_context(self.nc.semaphore(f"{self.stage}_{name}{i}")) for i in range(n)]


def f32(ap):
    return ap.bitcast(F32)




def stage_prep(nc, weight1, ident, adapters):
    R = 4
    with ExitStack() as ctx:
        a_ = Alloc(nc, ctx, "prep")
        natural = [a_.sb(f"natural{r}", [P, IC, HID]) for r in range(R)]
        turned = [a_.ps(f"turned{c}") for c in range(IC)]
        ident_steps = a_.sem("ident_steps")
        loaded = a_.sem("loaded", R)
        transposed = a_.sem("transposed")
        evacuated = a_.sem("evacuated", IC)
        block = ctx.enter_context(nc.Block())

        def load(sp, r, a):
            sp.dma_start(natural[r][:], weight1[bass.ds(a, 1)].rearrange(
                "a (oc p) i -> p (a oc) i", p=P)).then_inc(loaded[r], 16)

        @block.sync
        def _(sp):
            for r in range(R):
                load(sp, r, r)
            with sp.Fori(0, CONDS // R - 1) as i:
                for r in range(R):
                    sp.wait_ge(transposed, (i * R + (r + 1)) * IC)
                    load(sp, r, i * R + (r + R))

        @block.gpsimd
        def _(pool):
            nc.gpsimd.memset(ident[:], 0.0).then_inc(ident_steps, 1)
            pool.wait_ge(ident_steps, 1)
            nc.gpsimd.affine_select(out=ident[:], in_=ident[:], compare_op=ALU.not_equal, fill=1.0,
                                    base=0, pattern=[[-1, P]], channel_multiplier=1).then_inc(ident_steps, 1)

        @block.tensor
        def _(pe):
            pe.wait_ge(ident_steps, 2)
            with pe.Fori(0, CONDS // R) as i:
                for r in range(R):
                    pe.wait_ge(loaded[r], i * 16 + 16)
                    for c in range(IC):
                        pe.wait_ge(evacuated[c], i * R + r)
                        for oc in range(IC):
                            last = nc.tensor.transpose(turned[c][:, oc * P:(oc + 1) * P],
                                                       natural[r][:, oc, c * P:(c + 1) * P], ident[:])
                        last.then_inc(transposed, 1)

        @block.vector
        def _(dve):
            with dve.Fori(0, CONDS) as a:
                for c in (0, 2):
                    dve.wait_ge(transposed, a * IC + (c + 1))
                    nc.vector.tensor_copy(adapters[:, bass.ds(a * IC + c, 1), :].rearrange("p a o -> p (a o)"),
                                          turned[c][:]).then_inc(evacuated[c], 1)

        @block.scalar
        def _(act):
            with act.Fori(0, CONDS) as a:
                for c in (1, 3):
                    act.wait_ge(transposed, a * IC + (c + 1))
                    nc.scalar.activation(adapters[:, bass.ds(a * IC + c, 1), :].rearrange("p a o -> p (a o)"),
                                         turned[c][:], ACT.Copy).then_inc(evacuated[c], 1)


def stage_maps(nc, x, cond, subj, w0, w2, bias2, k_cache, ident, adapters, x3_dram, x3t_dram, kt_dram):
    U = 2
    with ExitStack() as ctx:
        a_ = Alloc(nc, ctx, "maps")
        cond_sb = a_.sb("cond", [1, B], I32)
        subj_sb = a_.sb("subj", [1, B], I32)
        w0_all = a_.sb("w0_all", [P, CONDS, S])
        w2_all = a_.sb("w2_all", [P, SUBJ, S])
        bias_rows = a_.sb("bias_rows", [SUBJ, GB, S])
        bias_all = a_.sb("bias_all", [P, SUBJ])
        diag0 = [a_.sb(f"diag0_{u}", [P, P]) for u in range(U)]
        diag2 = [a_.sb(f"diag2_{u}", [P, P]) for u in range(U)]
        bias = [a_.sb(f"bias{u}", [P, 1]) for u in range(U)]
        slots = a_.sb("slots", [P, GB, IC, HID])
        xin = [a_.sb(f"xin{u}", [P, HID]) for u in range(U)]
        xs = [a_.sb(f"xs{u}", [P, HID]) for u in range(U)]
        xt = [a_.sb(f"xt{u}", [P, IC, P]) for u in range(U)]
        k_nat = a_.sb("k_nat", [P, KVD])
        k_turned = [a_.sb(f"k_turned{q}", [P, PPT, HK // 2, PSIZE]) for q in range(2)]
        row_ps = [a_.ps(f"row{u}") for u in range(U)]
        col_ps = [a_.ps(f"col{u}") for u in range(U)]
        k_ps = [a_.ps(f"k{q}") for q in range(2)]

        tables_loaded = a_.sem("tables_loaded")
        ids_loaded = a_.sem("ids_loaded")
        bias_steps = a_.sem("bias_steps")
        diag_zero = a_.sem("diag_zero")
        diag_ready = a_.sem("diag_ready", U)
        xin_loaded = a_.sem("xin_loaded", U)
        l0_done = a_.sem("l0_done", U)
        x1_ready = a_.sem("x1_ready", U)
        x1_turned = a_.sem("x1_turned", U)
        x1t_ready = a_.sem("x1t_ready", U)
        slots_ready = a_.sem("slots_ready")
        l1_done = a_.sem("l1_done", U)
        x2_ready = a_.sem("x2_ready", U)
        l2_done = a_.sem("l2_done", U)
        x3_ready = a_.sem("x3_ready", U)
        x3_turned = a_.sem("x3_turned", U)
        x3t_ready = a_.sem("x3t_ready", U)
        x3_stored = a_.sem("x3_stored", U)
        k_loaded = a_.sem("k_loaded")
        k_transposed = a_.sem("k_transposed")
        k_evacuated = a_.sem("k_evacuated", 2)
        k_stored = a_.sem("k_stored", 2)
        block = ctx.enter_context(nc.Block())

        x_rows = x.rearrange("b s t -> (b s) t")
        k_rows = k_cache.rearrange("n k h d -> (n k) (h d)")

        @block.sync
        def _(sp):
            sp.dma_start(cond_sb[:], cond.rearrange("(o b) -> o b", o=1)).then_inc(ids_loaded, 16)
            sp.dma_start(subj_sb[:], subj.rearrange("(o b) -> o b", o=1)).then_inc(ids_loaded, 16)
            for q in range(GB):
                sp.dma_start(w0_all[q * S:(q + 1) * S], w0.rearrange("n c d -> c n d")).then_inc(tables_loaded, 16)
                sp.dma_start(w2_all[q * S:(q + 1) * S], w2.rearrange("n c d -> c n d")).then_inc(tables_loaded, 16)
                sp.dma_start(bias_rows[:, q, :], bias2.rearrange("n o d -> n (o d)")).then_inc(tables_loaded, 16)
            for u in range(U):
                sp.dma_start(xin[u][:], x_rows[u * P:(u + 1) * P]).then_inc(xin_loaded[u], 16)

            def pair(i, more):
                for u in range(U):
                    g = i * U + u
                    sp.wait_ge(k_transposed, g * 2)
                    sp.dma_start(k_nat[:], k_rows[bass.ds(g * P, P)]).then_inc(k_loaded, 16)
                    if more:
                        sp.wait_ge(x1_ready[u], i + 1)
                        sp.dma_start(xin[u][:], x_rows[bass.ds((g + U) * P, P)]).then_inc(xin_loaded[u], 16)
                    for q in range(2):
                        sp.wait_ge(k_evacuated[q], g + 1)
                        sp.dma_start(
                            kt_dram[bass.ds(g * PPT, PPT), :, q * (HK // 2):(q + 1) * (HK // 2), :]
                            .rearrange("n d h k -> d n (h k)"),
                            k_turned[q].rearrange("d n h k -> d n (h k)")).then_inc(k_stored[q], 16)
                for u in range(U):
                    g = i * U + u
                    sp.wait_ge(x3_ready[u], i + 1)
                    sp.dma_start(x3_dram[bass.ds(g * P, P)], xs[u][:]).then_inc(x3_stored[u], 16)
                    sp.wait_ge(ids_loaded, 32)
                    sp.wait_ge(x3t_ready[u], i + 1)
                    sp.dma_start(x3t_dram[:, :, bass.ds(g * P, P)], xt[u][:]).then_inc(x3_stored[u], 16)

            with sp.Fori(0, G // U - 1) as i:
                pair(i, True)
            pair(G // U - 1, False)
            for u in range(U):
                sp.wait_ge(x3_stored[u], 32 * (G // U))
            for q in range(2):
                sp.wait_ge(k_stored[q], 16 * G)

        @block.gpsimd
        def _(pool):
            for n, t in enumerate((diag0[0], diag0[1], diag2[0], diag2[1])):
                nc.gpsimd.memset(t[:], 0.0).then_inc(diag_zero, 1)
            pool.wait_ge(diag_zero, 4)
            pool.wait_ge(ids_loaded, 32)
            pool.wait_ge(tables_loaded, 16 * 3 * GB)
            pool.wait_ge(bias_steps, 2)
            with pool.Fori(0, G // U) as i:
                for u in range(U):
                    g = i * U + u
                    _, ids = nc.values_load_multi_w_load_instructions(
                        cond_sb[0:1, bass.ds(g * GB, GB)], engines=(mybir.EngineType.Pool,), min_val=0, max_val=CONDS - 1)
                    _, subs = nc.values_load_multi_w_load_instructions(
                        subj_sb[0:1, bass.ds(g * GB, GB)], engines=(mybir.EngineType.Pool,), min_val=0, max_val=SUBJ - 1)
                    pool.wait_ge(x3_ready[u], i)
                    for q in range(GB):
                        rows = slice(q * S, (q + 1) * S)
                        nc.gpsimd.tensor_copy(diag0[u][rows, q * S:(q + 1) * S],
                                              w0_all[rows, bass.ds(ids[q], 1), :].rearrange("p n d -> p (n d)"))
                        nc.gpsimd.tensor_copy(diag2[u][rows, q * S:(q + 1) * S],
                                              w2_all[rows, bass.ds(subs[q], 1), :].rearrange("p n d -> p (n d)"))
                        last = nc.gpsimd.tensor_copy(bias[u][rows, :], bias_all[rows, bass.ds(subs[q], 1)])
                    last.then_inc(diag_ready[u], 1)

        def adapter_slot(engine, etype, copy, g, qs):
            _, ids = nc.values_load_multi_w_load_instructions(
                cond_sb[0:1, bass.ds(g * GB + qs[0], len(qs))], engines=(etype,), min_val=0, max_val=CONDS - 1)
            for a, q in zip(ids, qs):
                copy(slots[:, q].rearrange("p c o -> p (c o)"),
                     adapters[:, bass.ds(a * IC, IC), :].rearrange("p c o -> p (c o)")).then_inc(slots_ready, 1)

        @block.vector
        def _(dve):
            dve.wait_ge(bias_steps, 1)
            nc.vector.tensor_copy(bias_all[:], k_ps[0][:, 0:SUBJ]).then_inc(bias_steps, 1)
            dve.wait_ge(ids_loaded, 32)

            def evacuate_k(g):
                dve.wait_ge(k_transposed, g * 2 + 1)
                dve.wait_ge(k_stored[0], g * 16)
                nc.vector.tensor_copy(k_turned[0].rearrange("d n h k -> d h n k"),
                                      k_ps[0].rearrange("d (h n k) -> d h n k", h=HK // 2, n=PPT)
                                      ).then_inc(k_evacuated[0], 1)

            copy = nc.vector.tensor_copy
            with dve.Fori(0, G // U) as i:
                dve.wait_ge(l1_done[1], i)
                adapter_slot(dve, mybir.EngineType.DVE, copy, i * U, (0, 1))
                for u in range(U):
                    dve.wait_ge(l0_done[u], i + 1)
                    dve.wait_ge(xin_loaded[u], i * 16 + 16)
                    dve.wait_ge(x3_stored[u], i * 32)
                    nc.vector.tensor_tensor(xs[u][:], row_ps[u][:], xin[u][:], ALU.add).then_inc(x1_ready[u], 1)
                evacuate_k(i * U)
                dve.wait_ge(l1_done[0], i + 1)
                nc.vector.tensor_tensor(xs[0][:], row_ps[0][:], xs[0][:], ALU.add).then_inc(x2_ready[0], 1)
                adapter_slot(dve, mybir.EngineType.DVE, copy, i * U + 1, (0, 1))
                evacuate_k(i * U + 1)
                dve.wait_ge(l2_done[0], i + 1)
                nc.vector.scalar_tensor_tensor(xs[0][:], row_ps[0][:], bias[0][:, 0:1], xs[0][:],
                                               ALU.add, ALU.add).then_inc(x3_ready[0], 1)
                dve.wait_ge(l1_done[1], i + 1)
                nc.vector.tensor_tensor(xs[1][:], row_ps[1][:], xs[1][:], ALU.add).then_inc(x2_ready[1], 1)
                dve.wait_ge(l2_done[1], i + 1)
                nc.vector.scalar_tensor_tensor(xs[1][:], row_ps[1][:], bias[1][:, 0:1], xs[1][:],
                                               ALU.add, ALU.add).then_inc(x3_ready[1], 1)

        @block.scalar
        def _(act):
            act.wait_ge(ids_loaded, 32)

            def evacuate_k(g):
                act.wait_ge(k_transposed, g * 2 + 2)
                act.wait_ge(k_stored[1], g * 16)
                nc.scalar.activation(k_turned[1].rearrange("d n h k -> d h n k"),
                                     k_ps[1].rearrange("d (h n k) -> d h n k", h=HK // 2, n=PPT),
                                     ACT.Copy).then_inc(k_evacuated[1], 1)

            def copy(out, in_):
                return nc.scalar.activation(out, in_, ACT.Copy)

            with act.Fori(0, G // U) as i:
                act.wait_ge(l1_done[1], i)
                adapter_slot(act, mybir.EngineType.Activation, copy, i * U, (2, 3))
                for u in range(U):
                    act.wait_ge(x1_turned[u], i + 1)
                    act.wait_ge(x3_stored[u], i * 32)
                    nc.scalar.activation(xt[u].rearrange("p c r -> p (c r)"), col_ps[u][:],
                                         ACT.Copy).then_inc(x1t_ready[u], 1)
                evacuate_k(i * U)
                act.wait_ge(l1_done[0], i + 1)
                adapter_slot(act, mybir.EngineType.Activation, copy, i * U + 1, (2, 3))
                evacuate_k(i * U + 1)
                for u in range(U):
                    act.wait_ge(x3_turned[u], i + 1)
                    nc.scalar.activation(xt[u].rearrange("p c r -> p (c r)"), col_ps[u][:],
                                         ACT.Copy).then_inc(x3t_ready[u], 1)

        @block.tensor
        def _(pe):
            pe.wait_ge(tables_loaded, 16 * 3 * GB)
            nc.tensor.transpose(k_ps[0][:, 0:SUBJ], bias_rows.rearrange("n q d -> n (q d)"),
                                ident[0:SUBJ, 0:SUBJ]).then_inc(bias_steps, 1)
            pe.wait_ge(bias_steps, 2)

            def turn_x(u, done):
                for c in range(IC):
                    last = nc.tensor.transpose(col_ps[u][:, c * P:(c + 1) * P], xs[u][:, c * P:(c + 1) * P], ident[:])
                last.then_inc(done[u], 1)

            def turn_k(g):
                pe.wait_ge(k_loaded, g * 16 + 16)
                for q in range(2):
                    pe.wait_ge(k_evacuated[q], g)
                    for h in range(HK // 2):
                        col = (q * (HK // 2) + h) * D
                        last = nc.tensor.transpose(k_ps[q][:, h * P:(h + 1) * P], k_nat[:, col:col + D], ident[:])
                    last.then_inc(k_transposed, 1)

            def layer1(u, i):
                pe.wait_ge(x1t_ready[u], i + 1)
                pe.wait_ge(slots_ready, i * (U * GB) + (u + 1) * GB)
                for c in range(IC):
                    for q in range(GB):
                        last = nc.tensor.matmul(row_ps[u][q * S:(q + 1) * S, :], xt[u][:, c, q * S:(q + 1) * S],
                                                slots[:, q, c, :], start=(c == 0), stop=(c == IC - 1))
                last.then_inc(l1_done[u], 1)

            with pe.Fori(0, G // U) as i:
                for u in range(U):
                    pe.wait_ge(diag_ready[u], i + 1)
                    pe.wait_ge(xin_loaded[u], i * 16 + 16)
                    pe.wait_ge(x3_ready[u], i)
                    nc.tensor.matmul(row_ps[u][:], diag0[u][:], xin[u][:], start=True, stop=True).then_inc(l0_done[u], 1)
                for u in range(U):
                    pe.wait_ge(x1_ready[u], i + 1)
                    pe.wait_ge(x3t_ready[u], i)
                    turn_x(u, x1_turned)
                turn_k(i * U)
                layer1(0, i)
                turn_k(i * U + 1)
                pe.wait_ge(x2_ready[0], i + 1)
                nc.tensor.matmul(row_ps[0][:], diag2[0][:], xs[0][:], start=True, stop=True).then_inc(l2_done[0], 1)
                layer1(1, i)
                pe.wait_ge(x3_ready[0], i + 1)
                turn_x(0, x3_turned)
                pe.wait_ge(x2_ready[1], i + 1)
                nc.tensor.matmul(row_ps[1][:], diag2[1][:], xs[1][:], start=True, stop=True).then_inc(l2_done[1], 1)
                pe.wait_ge(x3_ready[1], i + 1)
                turn_x(1, x3_turned)


def stage_values(nc, wv, table, seqlens, freq, qw, kw, ident, x3t_hi, x3t_lo, rope, stat, v_index, x3t_dram, vn_dram):
    U = 2
    with ExitStack() as ctx:
        a_ = Alloc(nc, ctx, "values")
        wv_nat = a_.sb("wv_nat", [P, HK, HID])
        wvt_hi = a_.sb("wvt_hi", [P, IC, KVD], F32R)
        wvt_lo = a_.sb("wvt_lo", [P, IC, KVD], F32R)
        slot_hi = [a_.sb(f"slot_hi{u}", [P, IC, P], F32R) for u in range(U)]
        slot_lo = [a_.sb(f"slot_lo{u}", [P, IC, P], F32R) for u in range(U)]
        v_out = [a_.sb(f"v_out{u}", [P, KVD]) for u in range(U)]
        freq_sb = a_.sb("freq", [P, 1])
        wcol = a_.sb("wcol", [P, 4])
        seq_i = a_.sb("seq_i", [P, B], I32)
        seq_f = a_.sb("seq_f", [P, B])
        step_i = a_.sb("step_i", [P, S], I32)
        step_f = a_.sb("step_f", [P, S])
        turns, angle, cosine, sine = (rope[:, n, :] for n in range(4))
        pages_i = a_.sb("pages_i", [P, B, NPP], I32)
        row_i = a_.sb("row_i", [P, 1], I32)
        row_f = a_.sb("row_f", [P, 1])
        w_ps = [a_.ps(f"w{n}") for n in range(2)]
        v_ps = [a_.ps(f"v{u}{n}") for u in range(U) for n in range(2)]

        wv_loaded = a_.sem("wv_loaded")
        x3t_loaded = a_.sem("x3t_loaded", IC)
        x3t_hi_ready = a_.sem("x3t_hi_ready")
        x3t_lo_ready = a_.sem("x3t_lo_ready")
        wv_hi_ready = a_.sem("wv_hi_ready")
        small_loaded = a_.sem("small_loaded")
        w_turned = a_.sem("w_turned")
        w_ready = a_.sem("w_ready", 2)
        slot_ready = a_.sem("slot_ready", U)
        v_done = a_.sem("v_done", U)
        v_ready = a_.sem("v_ready", U)
        v_stored = a_.sem("v_stored", U)
        iotas = a_.sem("iotas")
        chain = a_.sem("chain")
        reduced = a_.sem("reduced")
        sines = a_.sem("sines")
        block = ctx.enter_context(nc.Block())

        @block.sync
        def _(sp):
            sp.dma_start(wv_nat[:], wv.rearrange("(h p) i -> p h i", p=P)).then_inc(wv_loaded, 16)
            for c in range(IC):
                sp.dma_start(f32(x3t_lo[:, c, :]), x3t_dram[:, c, :]).then_inc(x3t_loaded[c], 16)
            sp.dma_start(seq_i[:], seqlens.rearrange("(o b) -> o b", o=1).to_broadcast([P, B])).then_inc(small_loaded, 16)
            sp.dma_start(pages_i[:], table.rearrange("(o b) n -> o b n", o=1).to_broadcast([P, B, NPP])).then_inc(small_loaded, 16)
            sp.dma_start(freq_sb[:], freq).then_inc(small_loaded, 16)
            sp.dma_start(wcol[:, 0:1], qw.rearrange("(p o) -> p o", o=1)).then_inc(small_loaded, 16)
            sp.dma_start(wcol[:, 1:2], kw.rearrange("(p o) -> p o", o=1)).then_inc(small_loaded, 16)
            with sp.Fori(0, G // U) as i:
                for u in range(U):
                    sp.wait_ge(v_ready[u], (i + 1) * 2)
                    sp.dma_start(vn_dram[bass.ds((i * U + u) * P, P)], v_out[u][:]).then_inc(v_stored[u], 16)
            for u in range(U):
                sp.wait_ge(v_stored[u], 16 * (G // U))

        @block.gpsimd
        def _(pool):
            nc.gpsimd.iota(step_i[:], pattern=[[1, S]], base=0, channel_multiplier=0).then_inc(iotas, 1)
            pool.wait_ge(iotas, 1)
            for c in range(PPT):
                nc.gpsimd.iota(row_i[c * PSIZE:(c + 1) * PSIZE], pattern=[[1, 1]], base=0,
                               channel_multiplier=1).then_inc(iotas, 1)
            pool.wait_ge(iotas, 1 + PPT)
            pool.wait_ge(x3t_lo_ready, IC)
            with pool.Fori(0, G // U) as i:
                for u in range(U):
                    pool.wait_ge(v_done[u], i)
                    for part, x in ((slot_hi, x3t_hi), (slot_lo, x3t_lo)):
                        nc.gpsimd.tensor_copy(part[u][:], f32(x[:, :, bass.ds((i * U + u) * P, P)])).then_inc(slot_ready[u], 1)

        @block.tensor
        def _(pe):
            pe.wait_ge(wv_loaded, 16)
            for h in range(HK):
                n = h % 2
                pe.wait_ge(w_ready[n], h // 2)
                for c in range(IC):
                    last = nc.tensor.transpose(w_ps[n][:, c * P:(c + 1) * P], wv_nat[:, h, c * P:(c + 1) * P], ident[:])
                last.then_inc(w_turned, 1)
            for n in range(2):
                pe.wait_ge(w_ready[n], HK // 2)
            with pe.Fori(0, G // U) as i:
                for u in range(U):
                    pe.wait_ge(slot_ready[u], i * 2 + 2)
                    pe.wait_ge(v_ready[u], i * 2)
                    for n in range(2):
                        for c in range(IC):
                            for k, (x, w) in enumerate(((slot_hi, wvt_hi), (slot_hi, wvt_lo), (slot_lo, wvt_hi))):
                                last = nc.tensor.matmul(v_ps[2 * u + n][:], x[u][:, c, :], w[:, c, n * 512:(n + 1) * 512],
                                                        start=(c == 0 and k == 0), stop=(c == IC - 1 and k == 2))
                    last.then_inc(v_done[u], 1)

        @block.scalar
        def _(act):
            for h in range(HK):
                act.wait_ge(w_turned, h + 1)
                nc.scalar.activation(wvt_hi[:, :, h * D:(h + 1) * D], w_ps[h % 2].rearrange("p (c e) -> p c e", c=IC),
                                     ACT.Copy).then_inc(wv_hi_ready, 1)
            for c in range(IC):
                act.wait_ge(x3t_loaded[c], 16)
                nc.scalar.activation(x3t_hi[:, c, :], f32(x3t_lo[:, c, :]), ACT.Copy).then_inc(x3t_hi_ready, 1)
            act.wait_ge(reduced, 2)
            nc.scalar.activation(sine, angle, ACT.Sin).then_inc(sines, 1)
            nc.scalar.activation(cosine, turns, ACT.Sin).then_inc(sines, 1)
            with act.Fori(0, G // U) as i:
                for u in range(U):
                    act.wait_ge(v_done[u], i + 1)
                    act.wait_ge(v_stored[u], i * 16)
                    for n in range(2):
                        nc.scalar.activation(v_out[u][:, n * 512:(n + 1) * 512], v_ps[2 * u + n][:],
                                             ACT.Copy).then_inc(v_ready[u], 1)

        @block.vector
        def _(dve):
            for h in range(HK):
                dve.wait_ge(wv_hi_ready, h + 1)
                cols = slice(h * D, (h + 1) * D)
                nc.vector.tensor_tensor(wvt_lo[:, :, cols], w_ps[h % 2].rearrange("p (c e) -> p c e", c=IC),
                                        f32(wvt_hi[:, :, cols]), ALU.subtract).then_inc(w_ready[h % 2], 1)
            for c in range(IC):
                dve.wait_ge(x3t_hi_ready, c + 1)
                nc.vector.tensor_tensor(x3t_lo[:, c, :], f32(x3t_lo[:, c, :]), f32(x3t_hi[:, c, :]),
                                        ALU.subtract).then_inc(x3t_lo_ready, 1)
            dve.wait_ge(small_loaded, 16 * 5)
            dve.wait_ge(iotas, 1 + PPT)
            steps = [0]

            def then(instruction):
                steps[0] += 1
                instruction.then_inc(chain, 1)
                dve.wait_ge(chain, steps[0])

            nc_v = nc.vector
            then(nc_v.tensor_copy(seq_f[:], seq_i[:]))
            then(nc_v.tensor_copy(step_f[:], step_i[:]))
            then(nc_v.tensor_copy(row_f[:], row_i[:]))
            then(nc_v.tensor_scalar(wcol[0:64, 2:4], wcol[0:64, 0:2], 1.0, None, ALU.mult))
            then(nc_v.tensor_scalar(wcol[64:P, 2:4], wcol[64:P, 0:2], -1.0, None, ALU.mult))
            shape = [P, B, S]
            then(nc_v.tensor_tensor(angle.rearrange("p (b s) -> p b s", b=B), seq_f.rearrange("p (b o) -> p b o", o=1).to_broadcast(shape),
                                    step_f.rearrange("p (o s) -> p o s", o=1).to_broadcast(shape), ALU.add))
            then(nc_v.tensor_scalar(angle, angle, freq_sb[:, 0:1], None, ALU.mult))
            then(nc_v.tensor_scalar(turns, angle, float(1 / (2 * np.pi)), ROUND, ALU.mult, ALU.add))
            then(nc_v.tensor_scalar(turns, turns, ROUND, None, ALU.subtract))
            for part in TWO_PI:
                then(nc_v.scalar_tensor_tensor(angle, turns, -part, angle, ALU.mult, ALU.add))
            then(nc_v.tensor_scalar(turns, angle, float(np.pi / 2), float(-2 * np.pi), ALU.is_gt, ALU.mult))
            then(nc_v.scalar_tensor_tensor(turns, angle, float(np.pi / 2), turns, ALU.add, ALU.add))
            for t in (angle, turns):
                steps[0] += 1
                nc_v.tensor_scalar(t, t, PI, -PI, ALU.min, ALU.max).then_inc(chain, 1)
                dve.wait_ge(chain, steps[0])
                dve.sem_inc(reduced, 1)
            for c in range(PPT):
                rows = slice(c * PSIZE, (c + 1) * PSIZE)
                then(nc_v.tensor_scalar(v_index[rows, :, :], pages_i[rows, :, :].rearrange("p b (t c) -> p b t c", c=PPT)[:, :, :, c],
                                        float(PSIZE), row_f[rows, 0:1], ALU.mult, ALU.add))
            then(nc_v.tensor_copy(stat[:, :, HK], seq_f[:]))
            dve.wait_ge(sines, 2)
            for n, (src, w) in enumerate(((cosine, 0), (sine, 2), (cosine, 1), (sine, 3))):
                then(nc_v.tensor_scalar(rope[:, n, :], src, wcol[:, w:w + 1], None, ALU.mult))


def stage_projection(nc, wq, wk, ident, x3t_hi, x3t_lo, rope, stat, qt_dram, kn_dram):
    with ExitStack() as ctx:
        a_ = Alloc(nc, ctx, "proj")
        M = 1 + REP
        w_nat = a_.sb("w_nat", [P, M, HID])
        w_hi = a_.sb("w_hi", [P, M, IC, P], F32R)
        w_lo = a_.sb("w_lo", [P, M, IC, P], F32R)
        ones = a_.sb("ones", [P, P])
        raw = [a_.sb(f"raw{n}", [P, 512]) for n in range(2)]
        squares = [a_.sb(f"squares{m}", [P, 512]) for m in range(M)]
        by_cos = [a_.sb(f"by_cos{n}", [P, 512]) for n in range(2)]
        by_sin = [a_.sb(f"by_sin{n}", [P, 512]) for n in range(2)]
        q_out = [a_.sb(f"q_out{n}", [P, CB, REP, S]) for n in range(2)]
        k_rms = a_.sb("k_rms", [P, 512])
        stat_t = a_.sb("stat_t", [P, CB, S])
        w_ps = [a_.ps(f"w{n}") for n in range(2)]
        proj_ps = [a_.ps(f"proj{n}") for n in range(2)]
        ksum_ps = a_.ps("ksum")
        qsum_ps = a_.ps("qsum")

        w_loaded = a_.sem("w_loaded")
        w_turned = a_.sem("w_turned", 2)
        w_hi_ready = a_.sem("w_hi_ready")
        w_ready = a_.sem("w_ready", 2)
        ones_ready = a_.sem("ones_ready")
        proj_done = a_.sem("proj_done")
        raw_ready = a_.sem("raw_ready")
        squared = a_.sem("squared")
        ksum_done = a_.sem("ksum_done")
        k_mean = a_.sem("k_mean")
        k_root = a_.sem("k_root")
        k_scaled = a_.sem("k_scaled")
        inverted = a_.sem("inverted")
        qsum_done = a_.sem("qsum_done")
        stat_turned = a_.sem("stat_turned")
        stat_ready = a_.sem("stat_ready")
        products = a_.sem("products")
        rotated = a_.sem("rotated")
        q_stored = a_.sem("q_stored", 2)
        k_stored = a_.sem("k_stored", 2)
        k_out = [a_.sb(f"k_out{n}", [P, CB, S]) for n in range(2)]
        block = ctx.enter_context(nc.Block())
        TPH = RC * M

        @block.sync
        def _(sp):
            def load_weights(h):
                sp.dma_start(w_nat[:, 0, :], wk[bass.ds(h * D, D)]).then_inc(w_loaded, 16)
                sp.dma_start(w_nat[:, 1:M, :], wq[bass.ds(h * (REP * D), REP * D)]
                             .rearrange("(m p) i -> p m i", p=P)).then_inc(w_loaded, 16)

            def store_k(h, rc):
                sp.wait_ge(k_scaled, h * RC + rc + 1)
                sp.dma_start(kn_dram[rc * CB:(rc + 1) * CB, :, bass.ds(h, 1), :].rearrange("b d h s -> d b (h s)"),
                             k_out[rc % 2][:]).then_inc(k_stored[rc % 2], 16)

            def head(h, more):
                for rc in range(RC):
                    sp.wait_ge(rotated, h * TPH + (rc + 1) * M)
                    sp.dma_start(qt_dram[bass.ds(h, 1), :, rc * CB:(rc + 1) * CB, :].rearrange("h d b n -> d (h b n)"),
                                 q_out[rc % 2].rearrange("d b r s -> d (b r s)")).then_inc(q_stored[rc % 2], 16)
                    if rc > 0:
                        store_k(h, rc - 1)
                    if rc == 1 and more:
                        sp.wait_ge(w_loaded, 32)
                        sp.wait_ge(w_turned[0], h * 3 + 3)
                        sp.wait_ge(w_turned[1], h * 2 + 2)
                        load_weights(h + 1)
                store_k(h, RC - 1)

            load_weights(0)
            with sp.Fori(0, HK - 1) as h:
                head(h, True)
            head(HK - 1, False)
            for n in range(2):
                sp.wait_ge(q_stored[n], 16 * HK * (RC // 2))
                sp.wait_ge(k_stored[n], 16 * HK * (RC // 2))

        @block.tensor
        def _(pe):
            pe.wait_ge(ones_ready, 1)
            with pe.Fori(0, HK) as h:
                pe.wait_ge(w_loaded, h * 32 + 32)
                for m in range(M):
                    pe.wait_ge(w_ready[m % 2], h * (3 if m % 2 == 0 else 2) + m // 2)
                    for c in range(IC):
                        last = nc.tensor.transpose(w_ps[m % 2][:, c * P:(c + 1) * P], w_nat[:, m, c * P:(c + 1) * P], ident[:])
                    last.then_inc(w_turned[m % 2], 1)

                def sums(rc):
                    pe.wait_ge(squared, h * TPH + (rc + 1) * M)
                    pe.wait_ge(k_mean, h * RC + rc)
                    nc.tensor.matmul(ksum_ps[:], ones[:], squares[0][:], start=True, stop=True).then_inc(ksum_done, 1)
                    pe.wait_ge(stat_turned, h * RC + rc)
                    for r in range(REP):
                        last = nc.tensor.matmul(qsum_ps[r * S:(r + 1) * S, :], ones[:, 0:S], squares[1 + r][:],
                                                start=True, stop=True)
                    last.then_inc(qsum_done, 1)

                for rc in range(RC):
                    for m in range(M):
                        t = rc * M + m
                        if rc == 0:
                            pe.wait_ge(w_ready[m % 2], h * (3 if m % 2 == 0 else 2) + m // 2 + 1)
                        if t >= 2:
                            pe.wait_ge(raw_ready, h * TPH + t - 1)
                        else:
                            pe.wait_ge(raw_ready, h * TPH)
                        for c in range(IC):
                            for k, (w, x) in enumerate(((w_hi, x3t_hi), (w_hi, x3t_lo), (w_lo, x3t_hi))):
                                last = nc.tensor.matmul(proj_ps[t % 2][:], w[:, m, c, :], x[:, c, rc * 512:(rc + 1) * 512],
                                                        start=(c == 0 and k == 0), stop=(c == IC - 1 and k == 2))
                        last.then_inc(proj_done, 1)
                        if m == 1 and rc > 0:
                            sums(rc - 1)
                sums(RC - 1)

        @block.scalar
        def _(act):
            with act.Fori(0, HK) as h:
                for m in range(M):
                    act.wait_ge(w_turned[m % 2], h * (3 if m % 2 == 0 else 2) + m // 2 + 1)
                    act.wait_ge(proj_done, h * TPH)
                    nc.scalar.activation(w_hi[:, m].rearrange("p c e -> p (c e)"), w_ps[m % 2][:], ACT.Copy).then_inc(w_hi_ready, 1)

                def root(rc):
                    act.wait_ge(k_mean, h * RC + rc + 1)
                    nc.scalar.activation(k_rms[:], k_rms[:], ACT.Sqrt).then_inc(k_root, 1)

                for rc in range(RC):
                    for m in range(M):
                        t = rc * M + m
                        act.wait_ge(proj_done, h * TPH + t + 1)
                        if t >= 2:
                            act.wait_ge(products, h * TPH + t - 1)
                        else:
                            act.wait_ge(products, h * TPH)
                        nc.scalar.activation(raw[t % 2][:], proj_ps[t % 2][:], ACT.Copy).then_inc(raw_ready, 1)
                        act.wait_ge(raw_ready, h * TPH + t + 1)
                        act.wait_ge(qsum_done, h * RC + rc)
                        nc.scalar.activation(squares[m][:], raw[t % 2][:], ACT.Square).then_inc(squared, 1)
                        if m == 2 and rc > 0:
                            root(rc - 1)

                root(RC - 1)
            act.wait_ge(k_mean, HK * RC + 1)
            nc.scalar.activation(stat[:, :, 0:HK], stat[:, :, 0:HK], ACT.Sqrt).then_inc(k_root, 1)

        @block.vector
        def _(dve):
            with dve.Fori(0, HK) as h:
                def rotate(t):
                    rc, m = divmod(t, M)
                    cols = slice(rc * 512, (rc + 1) * 512)
                    cos, sin = (2, 3) if m == 0 else (0, 1)
                    n = t % 2
                    dve.wait_ge(raw_ready, h * TPH + t + 1)
                    dve.wait_ge(rotated, h * TPH + (t - 1 if t >= 2 else 0))
                    nc.vector.tensor_tensor(by_cos[n][:], raw[n][:], rope[:, cos, cols], ALU.mult)
                    nc.vector.tensor_tensor(by_sin[n][0:64], raw[n][64:P], rope[64:P, sin, cols], ALU.mult)
                    nc.vector.tensor_tensor(by_sin[n][64:P], raw[n][0:64], rope[0:64, sin, cols],
                                            ALU.mult).then_inc(products, 1)

                def statistics(rc):
                    dve.wait_ge(ksum_done, h * RC + rc + 1)
                    dve.wait_ge(k_scaled, h * RC + rc)
                    nc.vector.tensor_scalar(k_rms[:], ksum_ps[:], 1.0 / D, EPS, ALU.mult, ALU.add).then_inc(k_mean, 1)
                    dve.wait_ge(qsum_done, h * RC + rc + 1)
                    dve.wait_ge(stat_ready, h * RC + rc)
                    nc.vector.transpose(stat_t.rearrange("p b s -> p (b s)"), qsum_ps[:]).then_inc(stat_turned, 1)
                    dve.wait_ge(stat_turned, h * RC + rc + 1)
                    nc.vector.tensor_copy(stat[:, rc * CB:(rc + 1) * CB, bass.ds(h, 1)], stat_t[:, :, 0:1]).then_inc(stat_ready, 1)

                def scale_k(rc):
                    dve.wait_ge(k_root, h * RC + rc + 1)
                    nc.vector.reciprocal(k_rms[:], k_rms[:]).then_inc(inverted, 1)
                    dve.wait_ge(inverted, h * RC + rc + 1)
                    dve.wait_ge(rotated, h * TPH + rc * M + 1)
                    kf = k_out[rc % 2].rearrange("d b s -> d (b s)")
                    nc.vector.tensor_tensor(kf, kf, k_rms[:], ALU.mult).then_inc(k_scaled, 1)

                for m in range(M):
                    dve.wait_ge(w_hi_ready, h * M + m + 1)
                    nc.vector.tensor_tensor(w_lo[:, m].rearrange("p c e -> p (c e)"), w_ps[m % 2][:],
                                            f32(w_hi[:, m]).rearrange("p c e -> p (c e)"), ALU.subtract).then_inc(w_ready[m % 2], 1)
                for t in range(TPH):
                    rc, m = divmod(t, M)
                    if rc > 0 and m == 3:
                        statistics(rc - 1)
                    rotate(t)
                    if rc > 0 and m == 4:
                        scale_k(rc - 1)
                statistics(RC - 1)
                scale_k(RC - 1)
            dve.wait_ge(stat_ready, HK * RC)
            qs = stat[:, :, 0:HK]
            nc.vector.tensor_scalar(qs, qs, 1.0 / D, EPS, ALU.mult, ALU.add).then_inc(k_mean, 1)
            dve.wait_ge(k_root, HK * RC + 1)
            nc.vector.reciprocal(qs, qs).then_inc(inverted, 1)
            dve.wait_ge(inverted, HK * RC + 1)
            nc.vector.tensor_scalar(qs, qs, -SCALE, None, ALU.mult).then_inc(inverted, 1)

        @block.gpsimd
        def _(pool):
            nc.gpsimd.memset(ones[:], 1.0).then_inc(ones_ready, 1)
            with pool.Fori(0, HK) as h:
                for t in range(TPH):
                    rc, m = divmod(t, M)
                    pool.wait_ge(products, h * TPH + t + 1)
                    if m == 0:
                        pool.wait_ge(k_stored[rc % 2], h * 32 + (rc // 2) * 16)
                        out = k_out[rc % 2][:]
                    else:
                        if m == 1:
                            pool.wait_ge(q_stored[rc % 2], h * 32 + (rc // 2) * 16)
                        out = q_out[rc % 2][:, :, m - 1, :]
                    n = t % 2
                    nc.gpsimd.tensor_tensor(out, by_cos[n].rearrange("d (b s) -> d b s", s=S),
                                            by_sin[n].rearrange("d (b s) -> d b s", s=S), ALU.add).then_inc(rotated, 1)


def stage_attention(nc, table, v_cache, ident, stat, v_index, kt_dram, kn_dram, qt_dram, vn_dram, ot_dram):
    N = 2 * HK
    RING = 4
    PAIRS = B // 2
    CHUNKS = HK
    EXTRAS = 5
    FIRST = NPP // 2 + 1
    LEFT = 512 - FIRST * PSIZE
    with ExitStack() as ctx:
        a_ = Alloc(nc, ctx, "att")
        pages_sb = a_.sb("pages", [1, B * NPP], I32)
        keys_raw = a_.sb("keys_raw", [P, NPP + 1, HK, PSIZE])
        queries_raw = a_.sb("queries_raw", [P, HK, P])
        keys_hi = [a_.sb(f"keys_hi{v}", [P, NPP + 1, HK, PSIZE], F32R) for v in range(2)]
        keys_lo = [a_.sb(f"keys_lo{v}", [P, NPP + 1, HK, PSIZE], F32R) for v in range(2)]
        queries_hi = [a_.sb(f"queries_hi{v}", [P, HK, P], F32R) for v in range(2)]
        queries_lo = [a_.sb(f"queries_lo{v}", [P, HK, P], F32R) for v in range(2)]
        values = [a_.sb(f"values{v}", [P, PPT, KVD]) for v in range(2)]
        new_values = [a_.sb(f"new_values{v}", [P, KVD]) for v in range(2)]
        v_rows_of = [a_.sb(f"v_rows_of{v}", [P, PPT], I32) for v in range(2)]
        key_no_i = a_.sb("key_no_i", [P, L], I32)
        key_no = a_.sb("key_no", [P, L])
        batch_cols = a_.sb("batch_cols", [P, HK + 1])
        mask = a_.sb("mask", [P, KEYS])
        probs = [a_.sb(f"probs{k}", [P, KEYS]) for k in range(RING)]
        low = [a_.sb(f"low{k}", [P, 1]) for k in range(RING)]
        total = [a_.sb(f"total{k}", [P, 1]) for k in range(RING)]
        inverse = [a_.sb(f"inverse{k}", [P, 1]) for k in range(RING)]
        probs_t = [a_.sb(f"probs_t{n}", [P, L]) for n in range(2)]
        new_probs_t = [a_.sb(f"new_probs_t{n}", [P, P]) for n in range(2)]
        heads_out = [a_.sb(f"heads_out{v}", [P, HK, P]) for v in range(2)]
        score_ps = [a_.ps(f"score{n}", 1024) for n in range(2)]
        turn_ps = [a_.ps(f"turn{n}") for n in range(2)]
        o_ps = a_.ps("o")
        new_ps = a_.ps("new")

        pages_loaded = a_.sem("pages_loaded")
        raw_loaded = a_.sem("raw_loaded", CHUNKS)
        raw_extra_loaded = a_.sem("raw_extra_loaded")
        hi_ready = a_.sem("hi_ready")
        hi_extra_ready = a_.sem("hi_extra_ready")
        lo_ready = a_.sem("lo_ready")
        lo_extra_ready = a_.sem("lo_extra_ready")
        v_loaded = a_.sem("v_loaded", 2)
        zeroed = a_.sem("zeroed")
        index_ready = a_.sem("index_ready")
        iota_done = a_.sem("iota_done")
        setup = a_.sem("setup")
        cols_ready = a_.sem("cols_ready")
        mask_ready = a_.sem("mask_ready")
        scores_done = a_.sem("scores_done", 2)
        scores_masked = a_.sem("scores_masked", 2)
        exp_done = a_.sem("exp_done")
        inverse_ready = a_.sem("inverse_ready")
        probs_ready = a_.sem("probs_ready")
        main_turned = a_.sem("main_turned", 2)
        all_turned = a_.sem("all_turned", RING)
        main_ready = a_.sem("main_ready", 2)
        new_ready = a_.sem("new_ready")
        o_done = a_.sem("o_done", 2)
        o_ready = a_.sem("o_ready")
        o_stored = a_.sem("o_stored", 2)
        block = ctx.enter_context(nc.Block())

        VN = 16 * (PPT + 1)

        def pages_of(c):
            return slice(2 * c, 2 * c + 2)

        @block.sync
        def _(sp):
            sp.dma_start(pages_sb[:], table.rearrange("(o b) n -> o (b n)", o=1)).then_inc(pages_loaded, 16)
            sp.wait_ge(pages_loaded, 16)

            def load(b, first):
                _, pages = nc.values_load_multi_w_load_instructions(
                    pages_sb[0:1, bass.ds(b * NPP, NPP)], engines=(mybir.EngineType.SP,), min_val=0, max_val=PAGES - 1)
                for c in range(CHUNKS):
                    if not first:
                        sp.wait_ge(pages_loaded, 16)
                        sp.wait_ge(lo_ready, (b - 1) * CHUNKS + (c + 1))
                    for n in (2 * c, 2 * c + 1):
                        sp.dma_start(keys_raw[:, n], kt_dram[bass.ds(pages[n], 1)].rearrange("n d h k -> d (n h) k")).then_inc(raw_loaded[c], 16)
                    if c == EXTRAS - 1:
                        if not first:
                            sp.wait_ge(pages_loaded, 16)
                            sp.wait_ge(lo_extra_ready, b * EXTRAS)
                        sp.dma_start(queries_raw[:], qt_dram[:, :, bass.ds(b, 1), :].rearrange("h d b n -> d h (b n)")).then_inc(raw_extra_loaded, 16)
                        sp.dma_start(keys_raw[:, NPP], kn_dram[bass.ds(b, 1)].rearrange("b d h s -> d (b h) s")).then_inc(raw_extra_loaded, 16)

            load(0, True)
            with sp.Fori(1, B) as b:
                load(b, False)

        @block.gpsimd
        def _(pool):
            nc.gpsimd.iota(key_no_i[:], pattern=[[1, L]], base=0, channel_multiplier=0).then_inc(iota_done, 1)
            for v in range(2):
                nc.gpsimd.memset(new_values[v][:], 0.0).then_inc(zeroed, 1)
                nc.gpsimd.memset(new_probs_t[v][:], 0.0).then_inc(zeroed, 1)
            pool.wait_ge(zeroed, 4)
            v_rows = v_cache.rearrange("n k h d -> (n k) (h d)")

            def load(v, b, parts):
                if 0 in parts:
                    nc.gpsimd.dma_start(new_values[v][0:S, :], vn_dram[bass.ds(b * S, S)]).then_inc(v_loaded[v], 16)
                    nc.gpsimd.tensor_copy(v_rows_of[v][:], v_index[:, bass.ds(b, 1), :].rearrange("p b t -> p (b t)")).then_inc(index_ready, 1)
                    pool.lower_val(b + 1)
                    pool.wait_ge(zeroed, 4)
                    pool.wait_ge(index_ready, b + 1)
                for t in range(PPT):
                    if t + 1 in parts:
                        nc.gpsimd.indirect_dma_start(
                            values[v][:, t, :], None, v_rows,
                            bass.IndirectOffsetOnAxis(ap=v_rows_of[v][:, t:t + 1], axis=0)).then_inc(v_loaded[v], 16)

            def pair(i, last_pair):
                for n in range(N):
                    j, h = divmod(n, HK)
                    if h >= 3 and not (last_pair and j == 1):
                        if h == 3:
                            pool.wait_ge(o_done[1], i * (N // 2) + j * (HK // 2))
                        load((j + 1) % 2, i * 2 + (j + 1), [h - 3])
                    pool.wait_ge(inverse_ready, i * N + n + 1)
                    k = n % RING
                    nc.gpsimd.tensor_tensor(probs[k][:], probs[k][:], inverse[k][:, 0:1].to_broadcast([P, KEYS]),
                                            ALU.mult).then_inc(probs_ready, 1)

            load(0, 0, range(1 + PPT))
            with pool.Fori(0, PAIRS - 1) as i:
                pair(i, False)
            pair(PAIRS - 1, True)

        @block.tensor
        def _(pe):
            def scores(i, n):
                j, h = divmod(n, HK)
                if h == 0:
                    pe.wait_ge(lo_ready, i * (2 * CHUNKS) + (j + 1) * CHUNKS)
                    pe.wait_ge(lo_extra_ready, i * (2 * EXTRAS) + (j + 1) * EXTRAS)
                pe.wait_ge(scores_masked[n % 2], i * (N // 2) + n // 2)
                for pages, cols in ((slice(0, FIRST), slice(LEFT, 512)), (slice(FIRST, NPP + 1), slice(512, LEFT + KEYS))):
                    for k, (q, kt) in enumerate(((queries_hi, keys_hi), (queries_hi, keys_lo), (queries_lo, keys_hi))):
                        last = nc.tensor.matmul(score_ps[n % 2][:, cols], q[j][:, h, :], kt[j][:, pages, h, :],
                                                start=(k == 0), stop=(k == 2))
                last.then_inc(scores_done[n % 2], 1)

            def turn(i, n):
                pe.wait_ge(probs_ready, i * N + (n + 1))
                pe.wait_ge(main_ready[n % 2], i * (N // 2) + n // 2)
                for t in range(PPT):
                    last = nc.tensor.transpose(turn_ps[n % 2][:, t * P:(t + 1) * P], probs[n % RING][:, t * P:(t + 1) * P], ident[:])
                last.then_inc(main_turned[n % 2], 1)
                pe.wait_ge(new_ready, i * N + n)
                nc.tensor.transpose(new_ps[0:S, 0:P], probs[n % RING][:, L:KEYS], ident[:]).then_inc(all_turned[n % RING], 1)

            def weigh(i, n):
                j, h = (n // HK) % 2, n % HK
                if h == 0:
                    pe.wait_ge(v_loaded[j], i * VN + VN)
                pe.wait_ge(main_ready[n % 2], i * (N // 2) + (n // 2 + 1))
                pe.wait_ge(new_ready, i * N + (n + 1))
                pe.wait_ge(o_ready, i * N + n)
                for t in range(PPT):
                    nc.tensor.matmul(o_ps[:, 0:P], values[j][:, t, h * D:(h + 1) * D], probs_t[n % 2][:, t * P:(t + 1) * P],
                                     start=(t == 0), stop=False)
                nc.tensor.matmul(o_ps[:, 0:P], new_values[j][:, h * D:(h + 1) * D], new_probs_t[n % 2][:],
                                 start=False, stop=True).then_inc(o_done[n % 2], 1)

            def pair(i, first):
                for n in range(N):
                    scores(i, n)
                    if n >= 2 or not first:
                        turn(i, n - 2)
                    if n >= 3 or not first:
                        weigh(i, n - 3)

            pair(0, True)
            with pe.Fori(1, PAIRS) as i:
                pair(i, False)
            turn(PAIRS, -2)
            weigh(PAIRS, -3)
            turn(PAIRS, -1)
            weigh(PAIRS, -2)
            weigh(PAIRS, -1)

        @block.scalar
        def _(act):
            def split(b, c, v):
                act.wait_ge(raw_loaded[c], b * 32 + 32)
                nc.scalar.activation(keys_hi[v][:, pages_of(c)], keys_raw[:, pages_of(c)], ACT.Copy).then_inc(hi_ready, 1)
                if c < EXTRAS:
                    if c == 0:
                        act.wait_ge(raw_extra_loaded, b * 32 + 32)
                    if c < EXTRAS - 1:
                        nc.scalar.activation(queries_hi[v][:, 2 * c:2 * c + 2], queries_raw[:, 2 * c:2 * c + 2], ACT.Copy).then_inc(hi_extra_ready, 1)
                    else:
                        nc.scalar.activation(keys_hi[v][:, NPP], keys_raw[:, NPP], ACT.Copy).then_inc(hi_extra_ready, 1)

            def softmax(i, n):
                act.wait_ge(scores_masked[n % 2], i * (N // 2) + (n // 2 + 1))
                k = n % RING
                nc.scalar.activation(probs[k][:], probs[k][:], ACT.Exp, bias=low[k][:, 0:1], scale=-1.0,
                                     accum_out=total[k][:, 0:1]).then_inc(exp_done, 1)

            def new_part(i, n):
                act.wait_ge(all_turned[n % RING], i * (N // RING) + (n // RING + 1))
                act.wait_ge(o_done[n % 2], i * (N // 2) + n // 2)
                nc.scalar.activation(new_probs_t[n % 2][0:S, :], new_ps[0:S, 0:P], ACT.Copy).then_inc(new_ready, 1)

            def keep_o(i, n):
                j, h = (n // HK) % 2, n % HK
                act.wait_ge(o_done[n % 2], i * (N // 2) + (n // 2 + 1))
                before = n // N
                if h == 0:
                    act.wait_ge(o_stored[j], (i + before) * 16)
                nc.scalar.activation(heads_out[j][:, h], o_ps[:, 0:P], ACT.Copy).then_inc(o_ready, 1)
                if h == HK - 1:
                    act.wait_ge(o_ready, i * N + (n + 1))
                    act.dma_start(ot_dram[bass.ds(i * 2 + n // HK, 1)].rearrange("b d h n -> d (b h n)"),
                                  heads_out[j].rearrange("d h n -> d (h n)")).then_inc(o_stored[j], 16)

            def pair(i, first, last_pair):
                for n in range(N):
                    j, h = divmod(n, HK)
                    if not (last_pair and j == 1):
                        if h == 0:
                            act.wait_ge(scores_done[1], i * (N // 2) + j * (HK // 2))
                        split(i * 2 + (j + 1), h, (j + 1) % 2)
                    softmax(i, n)
                    if n >= 2 or not first:
                        new_part(i, n - 2)
                    if n >= 3 or not first:
                        keep_o(i, n - 3)

            act.wait_ge(zeroed, 4)
            for c in range(CHUNKS):
                split(0, c, 0)
            pair(0, True, False)
            with act.Fori(1, PAIRS - 1) as i:
                pair(i, False, False)
            pair(PAIRS - 1, False, True)
            new_part(PAIRS, -2)
            keep_o(PAIRS, -3)
            new_part(PAIRS, -1)
            keep_o(PAIRS, -2)
            keep_o(PAIRS, -1)
            for v in range(2):
                act.wait_ge(o_stored[v], 16 * PAIRS)

        @block.vector
        def _(dve):
            def split(b, c, v):
                dve.wait_ge(hi_ready, b * CHUNKS + (c + 1))
                nc.vector.tensor_tensor(keys_lo[v][:, pages_of(c)], keys_raw[:, pages_of(c)], f32(keys_hi[v][:, pages_of(c)]),
                                        ALU.subtract).then_inc(lo_ready, 1)
                if c < EXTRAS:
                    dve.wait_ge(hi_extra_ready, b * EXTRAS + (c + 1))
                    if c < EXTRAS - 1:
                        two = slice(2 * c, 2 * c + 2)
                        nc.vector.tensor_tensor(queries_lo[v][:, two], queries_raw[:, two], f32(queries_hi[v][:, two]),
                                                ALU.subtract).then_inc(lo_extra_ready, 1)
                    else:
                        nc.vector.tensor_tensor(keys_lo[v][:, NPP], keys_raw[:, NPP], f32(keys_hi[v][:, NPP]),
                                                ALU.subtract).then_inc(lo_extra_ready, 1)

            def begin_batch(i, j):
                dve.wait_ge(scores_masked[1], i * (N // 2) + j * (HK // 2))
                nc.vector.tensor_copy(batch_cols[:], stat[:, bass.ds(i * 2 + j, 1), :].rearrange("p b c -> p (b c)")).then_inc(cols_ready, 1)
                dve.wait_ge(cols_ready, i * 2 + (j + 1))
                nc.vector.tensor_scalar(mask[:, 0:L], key_no[:], batch_cols[:, HK:HK + 1], MASKED, ALU.is_ge, ALU.mult).then_inc(mask_ready, 1)
                dve.wait_ge(mask_ready, i * 2 + (j + 1))

            def mask_scores(i, n):
                h = n % HK
                k = n % RING
                dve.lower_val(i * (N // 2) + (n // 2 + 1))
                dve.lower_val(i * (N // RING) + n // RING)
                dve.wait_ge(setup, 2)
                dve.wait_ge(scores_done[n % 2], i * (N // 2) + (n // 2 + 1))
                dve.wait_ge(all_turned[k], i * (N // RING) + n // RING)
                nc.vector.tensor_tensor_reduce(out=probs[k][:], in0=score_ps[n % 2][:, LEFT:LEFT + KEYS], in1=mask[:],
                                               scale=batch_cols[:, h:h + 1], scalar=3e38, op0=ALU.add, op1=ALU.min,
                                               accum_out=low[k][:, 0:1]).then_inc(scores_masked[n % 2], 1)

            def main_part(i, n):
                dve.wait_ge(main_turned[n % 2], i * (N // 2) + (n // 2 + 1))
                dve.wait_ge(o_done[n % 2], i * (N // 2) + n // 2)
                nc.vector.tensor_copy(probs_t[n % 2][:], turn_ps[n % 2][:]).then_inc(main_ready[n % 2], 1)

            def invert(i, n):
                dve.wait_ge(exp_done, i * N + (n + 1))
                nc.vector.reciprocal(inverse[n % RING][:], total[n % RING][:]).then_inc(inverse_ready, 1)

            def pair(i, first, last_pair):
                for n in range(N):
                    j, h = divmod(n, HK)
                    if h == 0:
                        begin_batch(i, j)
                    mask_scores(i, n)
                    if n >= 2 or not first:
                        main_part(i, n - 2)
                    if not (last_pair and j == 1):
                        split(i * 2 + (j + 1), h, (j + 1) % 2)
                    invert(i, n)

            dve.wait_ge(iota_done, 1)
            nc.vector.tensor_copy(key_no[:], key_no_i[:]).then_inc(setup, 1)
            nc.vector.memset(mask[:, L:KEYS], 0.0).then_inc(setup, 1)
            dve.wait_ge(setup, 2)
            for c in range(CHUNKS):
                split(0, c, 0)
            pair(0, True, False)
            with dve.Fori(1, PAIRS - 1) as i:
                pair(i, False, False)
            pair(PAIRS - 1, False, True)
            main_part(PAIRS, -2)
            main_part(PAIRS, -1)


def stage_output(nc, wo, ident, ot_dram, x3_dram, out):
    HALF = HQ // 2
    with ExitStack() as ctx:
        a_ = Alloc(nc, ctx, "out")
        wo_nat = [a_.sb(f"wo_nat{v}", [P, IC, REP * D]) for v in range(2)]
        wot_hi = a_.sb("wot_hi", [P, HQ, HID], F32R)
        wot_lo = a_.sb("wot_lo", [P, HQ, HID], F32R)
        o_raw = [a_.sb(f"o_raw{v}", [P, GB, HALF, S]) for v in range(2)]
        o_hi = [a_.sb(f"o_hi{v}", [P, HALF, GB, S], F32R) for v in range(2)]
        o_lo = [a_.sb(f"o_lo{v}", [P, HALF, GB, S], F32R) for v in range(2)]
        x3 = a_.sb("x3", [P, HID])
        y = a_.sb("y", [P, HID])
        w_ps = [a_.ps(f"w{n}") for n in range(4)]
        y_ps = [a_.ps(f"y{n}") for n in range(2)]

        wo_loaded = a_.sem("wo_loaded", 2)
        turned = a_.sem("turned")
        w_hi_ready = a_.sem("w_hi_ready")
        w_ready = a_.sem("w_ready", 4)
        o_loaded = a_.sem("o_loaded", 2)
        o_hi_ready = a_.sem("o_hi_ready", 2)
        o_lo_ready = a_.sem("o_lo_ready", 2)
        half_done = a_.sem("half_done", 2)
        x3_loaded = a_.sem("x3_loaded")
        y_ready = a_.sem("y_ready")
        y_stored = a_.sem("y_stored")
        block = ctx.enter_context(nc.Block())

        @block.sync
        def _(sp):
            def load_wo(v, h):
                sp.dma_start(wo_nat[v][:], wo.rearrange("(c p) e -> p c e", p=P)[:, :, bass.ds(h * (REP * D), REP * D)]
                             ).then_inc(wo_loaded[v], 16)

            def load_o(v, g):
                sp.dma_start(o_raw[v].rearrange("d j h s -> d j (h s)"),
                             ot_dram[bass.ds(g * GB, GB), :, v * (HK // 2):(v + 1) * (HK // 2), :].rearrange("b d h n -> d b (h n)")
                             ).then_inc(o_loaded[v], 16)

            for v in range(2):
                load_wo(v, v)
            with sp.Fori(0, HK // 2 - 1) as i:
                for v in range(2):
                    sp.wait_ge(wo_loaded[0], 16)
                    sp.wait_ge(turned, (i * 2 + (v + 1)) * REP)
                    load_wo(v, i * 2 + (v + 2))
            sp.dma_start(x3[:], x3_dram[0:P]).then_inc(x3_loaded, 16)
            for v in range(2):
                load_o(v, 0)
            with sp.Fori(0, G - 1) as g:
                for v in range(2):
                    sp.wait_ge(o_loaded[0], 16)
                    sp.wait_ge(o_lo_ready[v], g + 1)
                    load_o(v, g + 1)
                sp.wait_ge(y_ready, g + 1)
                sp.dma_start(out[bass.ds(g * P, P)], y[:]).then_inc(y_stored, 16)
                sp.dma_start(x3[:], x3_dram[bass.ds(g * P + P, P)]).then_inc(x3_loaded, 16)
            sp.wait_ge(y_ready, G)
            sp.dma_start(out[(G - 1) * P:G * P], y[:]).then_inc(y_stored, 16)
            sp.wait_ge(y_stored, 16 * G)

        @block.tensor
        def _(pe):
            with pe.Fori(0, HK // 2) as i:
                for v in range(2):
                    pe.wait_ge(wo_loaded[v], i * 16 + 16)
                    for r in range(REP):
                        pe.wait_ge(w_ready[r], i * 2 + v)
                        for c in range(IC):
                            last = nc.tensor.transpose(w_ps[r][:, c * P:(c + 1) * P], wo_nat[v][:, c, r * D:(r + 1) * D], ident[:])
                        last.then_inc(turned, 1)
            for r in range(REP):
                pe.wait_ge(w_ready[r], HK)

            def group(g2, u):
                for v in range(2):
                    pe.wait_ge(o_lo_ready[v], g2 * 2 + (u + 1))
                    if v == 0:
                        pe.wait_ge(y_ready, g2 * 2 + u - 1 if u else g2 * 2)
                    for m in range(HALF):
                        hq = v * HALF + m
                        for k, (o, w) in enumerate(((o_hi, wot_hi), (o_hi, wot_lo), (o_lo, wot_hi))):
                            last = nc.tensor.matmul(y_ps[u][:], o[v][:, m].rearrange("d j s -> d (j s)"), w[:, hq, :],
                                                    start=(hq == 0 and k == 0), stop=(hq == HQ - 1 and k == 2))
                    last.then_inc(half_done[v], 1)

            with pe.Fori(0, G // 2) as g2:
                for u in range(2):
                    group(g2, u)

        @block.scalar
        def _(act):
            with act.Fori(0, HK) as h:
                for r in range(REP):
                    act.wait_ge(turned, h * REP + (r + 1))
                    nc.scalar.activation(wot_hi[:, bass.ds(h * REP + r, 1), :].rearrange("p a e -> p (a e)"), w_ps[r][:],
                                         ACT.Copy).then_inc(w_hi_ready, 1)
            with act.Fori(0, G) as g:
                for v in range(2):
                    act.wait_ge(o_loaded[v], g * 16 + 16)
                    act.wait_ge(half_done[v], g)
                    nc.scalar.activation(o_hi[v][:], o_raw[v].rearrange("d j h s -> d h j s"), ACT.Copy).then_inc(o_hi_ready[v], 1)

        @block.vector
        def _(dve):
            with dve.Fori(0, HK) as h:
                for r in range(REP):
                    dve.wait_ge(w_hi_ready, h * REP + (r + 1))
                    row = bass.ds(h * REP + r, 1)
                    nc.vector.tensor_tensor(wot_lo[:, row, :].rearrange("p a e -> p (a e)"), w_ps[r][:],
                                            f32(wot_hi[:, row, :]).rearrange("p a e -> p (a e)"), ALU.subtract).then_inc(w_ready[r], 1)

            def split(v, g):
                dve.wait_ge(o_hi_ready[v], g + 1)
                nc.vector.tensor_tensor(o_lo[v][:], o_raw[v].rearrange("d j h s -> d h j s"), f32(o_hi[v][:]), ALU.subtract).then_inc(o_lo_ready[v], 1)

            def finish(g, u):
                dve.wait_ge(half_done[1], g + 1)
                dve.wait_ge(x3_loaded, g * 16 + 16)
                dve.wait_ge(y_stored, g * 16)
                nc.vector.tensor_tensor(y[:], y_ps[u][:], x3[:], ALU.add).then_inc(y_ready, 1)

            split(0, 0)
            split(1, 0)
            with dve.Fori(0, G // 2 - 1) as g2:
                for u in range(2):
                    g = g2 * 2 + u
                    split(0, g + 1)
                    finish(g, u)
                    split(1, g + 1)
            split(0, G - 1)
            finish(G - 2, 0)
            split(1, G - 1)
            finish(G - 1, 1)


INPUTS = ["x", "itok_B_0_15", "itok_B_0_31", "itok_Bx16_0_63", "itok_B_207_1644", "L0_cond_weights",
          "L1_cond_weight", "L2_cond_weights", "L2_cond_biases", "L3_cond_Wq", "L3_cond_Wk", "L3_cond_Wv",
          "L3_cond_Wo", "L3_cond_q_norm_w", "L3_cond_k_norm_w", "L3_cond_k_cache", "L3_cond_v_cache"]


def program(nc, ins, freq, out):
    (x, cond, subj, table, seqlens, w0, w1, w2, b2, wq, wk, wv, wo, qw, kw, kc, vc) = ins

    def scratch(name, shape):
        return nc.dram_tensor(name, shape, F32, kind="Internal").ap()

    x3_dram = scratch("x3_rows", [ROWS, HID])
    x3t_dram = scratch("x3_cols", [P, IC, ROWS])
    kt_dram = scratch("k_cache_t", [PAGES, D, HK, PSIZE])
    vn_dram = scratch("v_new", [ROWS, KVD])
    kn_dram = scratch("k_new_t", [B, D, HK, S])
    qt_dram = scratch("q_t", [HK, D, B, REP * S])
    ot_dram = scratch("o_t", [B, D, HK, REP * S])

    with ExitStack() as ctx:
        ident = ctx.enter_context(nc.sbuf_tensor("ident", [P, P], F32))
        with nc.sbuf_tensor("adapters", [P, CONDS * IC, HID], F32) as adapters:
            stage_prep(nc, w1, ident, adapters)
            stage_maps(nc, x, cond, subj, w0, w2, b2, kc, ident, adapters, x3_dram, x3t_dram, kt_dram)
        with nc.sbuf_tensor("stat", [P, B, HK + 1], F32) as stat, nc.sbuf_tensor("v_index", [P, B, PPT], I32) as v_index:
            with (nc.sbuf_tensor("x3t_hi", [P, IC, ROWS], F32R) as x3t_hi, nc.sbuf_tensor("x3t_lo", [P, IC, ROWS], F32R) as x3t_lo,
                  nc.sbuf_tensor("rope", [P, 4, ROWS], F32) as rope):
                stage_values(nc, wv, table, seqlens, freq, qw, kw, ident, x3t_hi, x3t_lo, rope, stat, v_index, x3t_dram, vn_dram)
                stage_projection(nc, wq, wk, ident, x3t_hi, x3t_lo, rope, stat, qt_dram, kn_dram)
            stage_attention(nc, table, vc, ident, stat, v_index, kt_dram, kn_dram, qt_dram, vn_dram, ot_dram)
        stage_output(nc, wo, ident, ot_dram, x3_dram, out.rearrange("b s t -> (b s) t"))


def kernel(**inputs):
    import concourse.bacc as bacc
    from concourse.bass_utils import run_bass_kernel_spmd

    nc = bacc.Bacc("TRN2", target_bir_lowering=False, num_devices=1)
    arrays, ins = {}, []
    for name in INPUTS:
        a = np.ascontiguousarray(inputs[name])
        arrays[name] = a
        ins.append(nc.dram_tensor(name, a.shape, mybir.dt.from_np(a.dtype), kind="ExternalInput").ap())
    arrays["rope_freq"] = rope_frequencies()
    freq = nc.dram_tensor("rope_freq", (P, 1), F32, kind="ExternalInput").ap()
    out = nc.dram_tensor("out", (B, S, HID), F32, kind="ExternalOutput").ap()
    program(nc, ins, freq, out)
    r = run_bass_kernel_spmd(nc, [arrays], core_ids=[0])
    return r.results[0]["out"]
```

```python
from contextlib import ExitStack

import numpy as np

import concourse.bass as bass
import concourse.mybir as mybir

ALU = mybir.AluOpType
ACT = mybir.ActivationFunctionType
F32 = mybir.dt.float32
F32R = mybir.dt.float32r
I32 = mybir.dt.int32

P = 128
B, S, HID = 64, 32, 512
ROWS = B * S
GB = P // S
G = B // GB
IC = HID // P
CONDS, SUBJ = 16, 32
D, HQ, HK = 128, 32, 8
REP = HQ // HK
PAGES, PSIZE, NPP = 64, 32, 16
L = NPP * PSIZE
KEYS = L + S
PPT = P // PSIZE
KVD = HK * D
RC = ROWS // 512
CB = B // RC
WV_EARLY = 1 + REP
THETA, EPS = 10000.0, 1e-6
SCALE = 1.0 / float(np.sqrt(D))
MASKED = -1e30
PI = float(np.float32(3.1415925))
TWO_PI = (6.28125, float(np.float32(0.0019353071795864769 // 2**-21 * 2**-21)))
TWO_PI += (2 * np.pi - TWO_PI[0] - TWO_PI[1],)
ROUND = 1.5 * 2**23


def rope_frequencies():
    exponent = np.arange(0, D, 2, dtype=np.float32) / np.float32(D)
    f = (1.0 / THETA ** exponent.astype(np.float64)).astype(np.float32)
    return np.concatenate([f, f]).reshape(P, 1)


class Alloc:

    def __init__(self, nc, ctx, stage):
        self.nc, self.ctx, self.stage = nc, ctx, stage

    def sb(self, name, shape, dt=F32):
        return self.ctx.enter_context(self.nc.sbuf_tensor(f"{self.stage}_{name}", shape, dt))

    def ps(self, name, cols=512):
        return self.ctx.enter_context(self.nc.psum_tensor(f"{self.stage}_{name}", [P, cols], F32))

    def sem(self, name, n=None):
        if n is None:
            return self.ctx.enter_context(self.nc.semaphore(f"{self.stage}_{name}"))
        return [self.ctx.enter_context(self.nc.semaphore(f"{self.stage}_{name}{i}")) for i in range(n)]


def f32(ap):
    return ap.bitcast(F32)




def stage_prep(nc, weight1, cond, subj, w0, w2, bias2, ident, adapters, tables):
    cond_sb, subj_sb, w0_all, w2_all, bias_rows = tables
    R = 4
    with ExitStack() as ctx:
        a_ = Alloc(nc, ctx, "prep")
        natural = [a_.sb(f"natural{r}", [P, IC, HID]) for r in range(R)]
        turned = [a_.ps(f"turned{c}") for c in range(IC)]
        ident_steps = a_.sem("ident_steps")
        loaded = a_.sem("loaded", R)
        tables_loaded = a_.sem("tables_loaded")
        transposed = a_.sem("transposed")
        evacuated = a_.sem("evacuated", IC)
        block = ctx.enter_context(nc.Block())

        def load(sp, r, a):
            sp.dma_start(natural[r][:], weight1[bass.ds(a, 1)].rearrange(
                "a (oc p) i -> p (a oc) i", p=P)).then_inc(loaded[r], 16)

        @block.sync
        def _(sp):
            for r in range(R):
                load(sp, r, r)
            with sp.Fori(0, CONDS // R - 1) as i:
                for r in range(R):
                    sp.wait_ge(transposed, (i * R + (r + 1)) * IC)
                    load(sp, r, i * R + (r + R))
            sp.dma_start(cond_sb[:], cond.rearrange("(o b) -> o b", o=1)).then_inc(tables_loaded, 16)
            sp.dma_start(subj_sb[:], subj.rearrange("(o b) -> o b", o=1)).then_inc(tables_loaded, 16)
            for q in range(GB):
                sp.dma_start(w0_all[q * S:(q + 1) * S], w0.rearrange("n c d -> c n d")).then_inc(tables_loaded, 16)
                sp.dma_start(w2_all[q * S:(q + 1) * S], w2.rearrange("n c d -> c n d")).then_inc(tables_loaded, 16)
                sp.dma_start(bias_rows[:, q, :], bias2.rearrange("n o d -> n (o d)")).then_inc(tables_loaded, 16)
            sp.wait_ge(tables_loaded, 16 * (2 + 3 * GB))

        @block.gpsimd
        def _(pool):
            nc.gpsimd.memset(ident[:], 0.0).then_inc(ident_steps, 1)
            pool.wait_ge(ident_steps, 1)
            nc.gpsimd.affine_select(out=ident[:], in_=ident[:], compare_op=ALU.not_equal, fill=1.0,
                                    base=0, pattern=[[-1, P]], channel_multiplier=1).then_inc(ident_steps, 1)

        @block.tensor
        def _(pe):
            pe.wait_ge(ident_steps, 2)

            def adapters_of(i, first):
                for r in range(R):
                    pe.wait_ge(loaded[r], i * 16 + 16)
                    for c in range(IC):
                        if r or not first:
                            pe.wait_ge(evacuated[c], i * R + r)
                        for oc in range(IC):
                            last = nc.tensor.transpose(turned[c][:, oc * P:(oc + 1) * P],
                                                       natural[r][:, oc, c * P:(c + 1) * P], ident[:])
                        last.then_inc(transposed, 1)

            adapters_of(0, True)
            with pe.Fori(1, CONDS // R) as i:
                adapters_of(i, False)

        @block.vector
        def _(dve):
            with dve.Fori(0, CONDS) as a:
                for c in (0, 2):
                    dve.wait_ge(transposed, a * IC + (c + 1))
                    nc.vector.tensor_copy(adapters[:, bass.ds(a * IC + c, 1), :].rearrange("p a o -> p (a o)"),
                                          turned[c][:]).then_inc(evacuated[c], 1)

        @block.scalar
        def _(act):
            with act.Fori(0, CONDS) as a:
                for c in (1, 3):
                    act.wait_ge(transposed, a * IC + (c + 1))
                    nc.scalar.activation(adapters[:, bass.ds(a * IC + c, 1), :].rearrange("p a o -> p (a o)"),
                                         turned[c][:], ACT.Copy).then_inc(evacuated[c], 1)


def load_wv(sp, wv, tile, heads, loaded):
    sp.dma_start(tile[:], wv.rearrange("(h p) i -> p h i", p=P)[:, heads]).then_inc(loaded, 16)


def stage_maps(nc, x, k_cache, wv, ident, adapters, tables, w_nat, x3_dram, x3t_dram, kt_dram):
    HALF = IC // 2
    with ExitStack() as ctx:
        a_ = Alloc(nc, ctx, "maps")
        cond_sb, subj_sb, w0_all, w2_all, bias_rows = tables
        bias_all = a_.sb("bias_all", [P, SUBJ])
        diag0 = [a_.sb(f"diag0_{u}", [P, P]) for u in range(2)]
        diag2 = [a_.sb(f"diag2_{u}", [P, P]) for u in range(2)]
        bias = [a_.sb(f"bias{u}", [P, 1]) for u in range(2)]
        slots = a_.sb("slots", [P, GB, IC, HID])
        xin = [a_.sb(f"xin{u}", [P, HID]) for u in range(2)]
        x12 = [a_.sb(f"x12_{u}", [P, HID]) for u in range(2)]
        x1t = [a_.sb(f"x1t{u}", [P, IC, P]) for u in range(2)]
        x3 = [a_.sb(f"x3_{u}", [P, HID]) for u in range(2)]
        x3t = [a_.sb(f"x3t{u}", [P, IC, P]) for u in range(2)]
        k_nat = a_.sb("k_nat", [P, KVD])
        k_turned = [a_.sb(f"k_turned{q}", [P, PPT, HK // 2, PSIZE]) for q in range(2)]
        l0_ps, l1_ps, l2_ps = (a_.ps(f"l{n}") for n in range(3))
        x1t_ps = a_.ps("x1t_bank")
        x3t_ps = a_.ps("x3t_bank")
        k_ps = [a_.ps(f"k{q}") for q in range(2)]

        bias_steps = a_.sem("bias_steps")
        diag_zero = a_.sem("diag_zero")
        diag0_ready = a_.sem("diag0_ready")
        diag2_ready = a_.sem("diag2_ready")
        xin_loaded = a_.sem("xin_loaded", 2)
        l0_done = a_.sem("l0_done")
        x1_ready = a_.sem("x1_ready")
        x1_turned = a_.sem("x1_turned")
        x1t_ready = a_.sem("x1t_ready")
        slots_by_dve = a_.sem("slots_by_dve")
        slots_by_act = a_.sem("slots_by_act")
        l1_halves = a_.sem("l1_halves")
        x2_ready = a_.sem("x2_ready")
        l2_done = a_.sem("l2_done")
        x3_ready = a_.sem("x3_ready")
        x3_turned = a_.sem("x3_turned")
        x3t_ready = a_.sem("x3t_ready")
        x3_stored = a_.sem("x3_stored", 2)
        k_loaded = a_.sem("k_loaded")
        k_transposed = a_.sem("k_transposed")
        k_evacuated = a_.sem("k_evacuated", 2)
        k_stored = a_.sem("k_stored", 2)
        wv_loaded = a_.sem("wv_loaded")
        block = ctx.enter_context(nc.Block())

        x_rows = x.rearrange("b s t -> (b s) t")
        k_rows = k_cache.rearrange("n k h d -> (n k) (h d)")

        def groups(engine, step):
            for i in range(2):
                for u in range(2):
                    step(i, u, i == 0 and u == 0, False)
            with engine.Fori(2, G // 2 - 1) as i:
                for u in range(2):
                    step(i, u, False, False)
            for u in range(2):
                step(G // 2 - 1, u, False, u == 1)

        @block.sync
        def _(sp):
            for u in range(2):
                sp.dma_start(xin[u][:], x_rows[u * P:(u + 1) * P]).then_inc(xin_loaded[u], 16)
            sp.dma_start(k_nat[:], k_rows[0:P]).then_inc(k_loaded, 16)
            load_wv(sp, wv, w_nat, slice(0, WV_EARLY), wv_loaded)
            sp.wait_ge(k_loaded, 16)

            def store_x3(i, u):
                g = i * 2 + u
                sp.wait_ge(k_loaded, 16)
                sp.wait_ge(x3_ready, g + 1)
                sp.dma_start(x3_dram[bass.ds(g * P, P)], x3[u % 2][:]).then_inc(x3_stored[u % 2], 16)
                sp.wait_ge(k_loaded, 16)
                sp.wait_ge(x3t_ready, g + 1)
                sp.dma_start(x3t_dram[:, :, bass.ds(g * P, P)], x3t[u % 2][:]).then_inc(x3_stored[u % 2], 16)

            def step(i, u, first, last, last_pair=False):
                g = i * 2 + u
                if not last_pair:
                    sp.wait_ge(k_loaded, 16)
                    sp.wait_ge(x1_ready, g + 1)
                    sp.dma_start(xin[u][:], x_rows[bass.ds((g + 2) * P, P)]).then_inc(xin_loaded[u], 16)
                if not first:
                    store_x3(i, u - 1)
                if not last:
                    sp.wait_ge(k_loaded, 16)
                    sp.wait_ge(k_transposed, g * 2 + 2)
                    sp.dma_start(k_nat[:], k_rows[bass.ds((g + 1) * P, P)]).then_inc(k_loaded, 16)
                for q in range(2):
                    sp.wait_ge(k_loaded, 16)
                    sp.wait_ge(k_evacuated[q], g + 1)
                    sp.dma_start(
                        kt_dram[bass.ds(g * PPT, PPT), :, q * (HK // 2):(q + 1) * (HK // 2), :]
                        .rearrange("n d h k -> d n (h k)"),
                        k_turned[q].rearrange("d n h k -> d n (h k)")).then_inc(k_stored[q], 16)

            for u in range(2):
                step(0, u, u == 0, False)
            with sp.Fori(1, G // 2 - 1) as i:
                for u in range(2):
                    step(i, u, False, False)
            for u in range(2):
                step(G // 2 - 1, u, False, u == 1, True)
            store_x3(G // 2, -1)
            sp.wait_ge(wv_loaded, 16)
            for u in range(2):
                sp.wait_ge(x3_stored[u], 16 * G)
            for q in range(2):
                sp.wait_ge(k_stored[q], 16 * G)

        @block.gpsimd
        def _(pool):
            for t in (diag0[0], diag0[1], diag2[0], diag2[1]):
                nc.gpsimd.memset(t[:], 0.0).then_inc(diag_zero, 1)
            pool.wait_ge(diag_zero, 4)
            pool.wait_ge(bias_steps, 2)

            def diagonals(i, u, first):
                g = i * 2 + u
                _, ids = nc.values_load_multi_w_load_instructions(
                    cond_sb[0:1, bass.ds(g * GB, GB)], engines=(mybir.EngineType.Pool,), min_val=0, max_val=CONDS - 1)
                _, subs = nc.values_load_multi_w_load_instructions(
                    subj_sb[0:1, bass.ds(g * GB, GB)], engines=(mybir.EngineType.Pool,), min_val=0, max_val=SUBJ - 1)
                if not first:
                    pool.wait_ge(l0_done, g - 1)
                for q in range(GB):
                    rows = slice(q * S, (q + 1) * S)
                    last = nc.gpsimd.tensor_copy(diag0[u][rows, q * S:(q + 1) * S],
                                                 w0_all[rows, bass.ds(ids[q], 1), :].rearrange("p n d -> p (n d)"))
                last.then_inc(diag0_ready, 1)
                if not first:
                    pool.wait_ge(x3_ready, g - 1)
                for q in range(GB):
                    rows = slice(q * S, (q + 1) * S)
                    nc.gpsimd.tensor_copy(diag2[u][rows, q * S:(q + 1) * S],
                                          w2_all[rows, bass.ds(subs[q], 1), :].rearrange("p n d -> p (n d)"))
                    last = nc.gpsimd.tensor_copy(bias[u][rows, :], bias_all[rows, bass.ds(subs[q], 1)])
                last.then_inc(diag2_ready, 1)

            for u in range(2):
                diagonals(0, u, True)
            with pool.Fori(1, G // 2) as i:
                for u in range(2):
                    diagonals(i, u, False)

        def adapters_of(etype, g, qs):
            _, ids = nc.values_load_multi_w_load_instructions(
                cond_sb[0:1, bass.ds(g * GB + qs[0], len(qs))], engines=(etype,), min_val=0, max_val=CONDS - 1)
            return zip(ids, qs)

        def fill_slots(copy, done, ids, half):
            for a, q in ids:
                copy(slots[:, q, half * HALF:(half + 1) * HALF].rearrange("p c o -> p (c o)"),
                     adapters[:, bass.ds(a * IC + half * HALF, HALF), :].rearrange("p c o -> p (c o)")).then_inc(done, 1)

        @block.vector
        def _(dve):
            dve.wait_ge(bias_steps, 1)
            nc.vector.tensor_copy(bias_all[:], k_ps[0][:, 0:SUBJ]).then_inc(bias_steps, 1)
            copy = nc.vector.tensor_copy

            def add_x(i, u, first):
                g = i * 2 + u
                dve.wait_ge(l0_done, g + 1)
                dve.wait_ge(xin_loaded[u % 2], i * 16 + (16 if u < 2 else 32))
                if not first:
                    dve.wait_ge(x3_ready, g - 1)
                nc.vector.tensor_tensor(x12[u % 2][:], l0_ps[:], xin[u % 2][:], ALU.add).then_inc(x1_ready, 1)

            def add_layer2(i, u):
                v = u % 2
                dve.wait_ge(l2_done, i * 2 + (u + 1))
                dve.wait_ge(x3_stored[v], i * 32 if u >= 0 else (i - 1) * 32)
                nc.vector.scalar_tensor_tensor(x3[v][:], l2_ps[:], bias[v][:, 0:1], x12[v][:],
                                               ALU.add, ALU.add).then_inc(x3_ready, 1)

            def step(i, u, first, last):
                g = i * 2 + u
                if not first:
                    add_layer2(i, u - 1)
                if not last:
                    add_x(i, u + 1, first)
                    ids = list(adapters_of(mybir.EngineType.DVE, g + 1, (0, 1)))
                    dve.wait_ge(l1_halves, g * 2 + 1)
                    fill_slots(copy, slots_by_dve, ids, 0)
                dve.wait_ge(l1_halves, g * 2 + 2)
                dve.wait_ge(x1_ready, g + 1)
                nc.vector.tensor_tensor(x12[u][:], l1_ps[:], x12[u][:], ALU.add).then_inc(x2_ready, 1)
                if not last:
                    fill_slots(copy, slots_by_dve, ids, 1)
                dve.wait_ge(k_transposed, g * 2 + 1)
                dve.wait_ge(k_stored[0], g * 16)
                nc.vector.tensor_copy(k_turned[0].rearrange("d n h k -> d h n k"),
                                      k_ps[0].rearrange("d (h n k) -> d h n k", h=HK // 2, n=PPT)
                                      ).then_inc(k_evacuated[0], 1)

            ids = list(adapters_of(mybir.EngineType.DVE, 0, (0, 1)))
            for half in range(2):
                fill_slots(copy, slots_by_dve, ids, half)
            add_x(0, 0, True)
            groups(dve, step)
            add_layer2(G // 2, -1)

        @block.scalar
        def _(act):

            def copy(out, in_):
                return nc.scalar.activation(out, in_, ACT.Copy)

            def keep_x1t(i, u):
                act.wait_ge(x1_turned, i * 2 + (u + 1))
                copy(x1t[u % 2].rearrange("p c r -> p (c r)"), x1t_ps[:]).then_inc(x1t_ready, 1)

            def keep_x3t(i, u):
                v = u % 2
                act.wait_ge(x3_turned, i * 2 + (u + 1))
                act.wait_ge(x3_stored[v], i * 32 if u >= 0 else (i - 1) * 32)
                copy(x3t[v].rearrange("p c r -> p (c r)"), x3t_ps[:]).then_inc(x3t_ready, 1)

            def step(i, u, first, last):
                g = i * 2 + u
                if not last:
                    ids = list(adapters_of(mybir.EngineType.Activation, g + 1, (2, 3)))
                    act.wait_ge(l1_halves, g * 2 + 1)
                    fill_slots(copy, slots_by_act, ids, 0)
                if not first:
                    keep_x3t(i, u - 1)
                if not last:
                    keep_x1t(i, u + 1)
                    act.wait_ge(l1_halves, g * 2 + 2)
                    fill_slots(copy, slots_by_act, ids, 1)
                act.wait_ge(k_transposed, g * 2 + 2)
                act.wait_ge(k_stored[1], g * 16)
                copy(k_turned[1].rearrange("d n h k -> d h n k"),
                     k_ps[1].rearrange("d (h n k) -> d h n k", h=HK // 2, n=PPT)).then_inc(k_evacuated[1], 1)

            ids = list(adapters_of(mybir.EngineType.Activation, 0, (2, 3)))
            for half in range(2):
                fill_slots(copy, slots_by_act, ids, half)
            keep_x1t(0, 0)
            groups(act, step)
            keep_x3t(G // 2, -1)

        @block.tensor
        def _(pe):
            nc.tensor.transpose(k_ps[0][:, 0:SUBJ], bias_rows.rearrange("n q d -> n (q d)"),
                                ident[0:SUBJ, 0:SUBJ]).then_inc(bias_steps, 1)
            pe.wait_ge(bias_steps, 2)

            def turn(bank, rows, done):
                for c in range(IC):
                    last = nc.tensor.transpose(bank[:, c * P:(c + 1) * P], rows[:, c * P:(c + 1) * P], ident[:])
                last.then_inc(done, 1)

            def layer0(i, u):
                g = i * 2 + u
                pe.wait_ge(diag0_ready, g + 1)
                pe.wait_ge(xin_loaded[u % 2], i * 16 + (16 if u < 2 else 32))
                pe.wait_ge(x1_ready, g)
                nc.tensor.matmul(l0_ps[:], diag0[u % 2][:], xin[u % 2][:], start=True, stop=True).then_inc(l0_done, 1)

            def layer1(g, u, half):
                for filled in (slots_by_dve, slots_by_act):
                    pe.wait_ge(filled, g * 4 + (half * 2 + 2))
                for c in range(half * HALF, (half + 1) * HALF):
                    for q in range(GB):
                        last = nc.tensor.matmul(l1_ps[q * S:(q + 1) * S, :], x1t[u][:, c, q * S:(q + 1) * S],
                                                slots[:, q, c, :], start=(c == 0), stop=(c == IC - 1))
                last.then_inc(l1_halves, 1)

            def turn_x1(i, u):
                g = i * 2 + u
                pe.wait_ge(x1_ready, g + 1)
                pe.wait_ge(x1t_ready, g)
                turn(x1t_ps, x12[u % 2], x1_turned)

            def turn_x3(i, u):
                g = i * 2 + u
                pe.wait_ge(x3_ready, g + 1)
                pe.wait_ge(x3t_ready, g)
                turn(x3t_ps, x3[u % 2], x3_turned)

            def step(i, u, first, last):
                g = i * 2 + u
                if not last:
                    layer0(i, u + 1)
                pe.wait_ge(x1t_ready, g + 1)
                pe.wait_ge(x2_ready, g)
                layer1(g, u, 0)
                if not first:
                    turn_x3(i, u - 1)
                layer1(g, u, 1)
                if not last:
                    turn_x1(i, u + 1)
                pe.wait_ge(k_loaded, g * 16 + 16)
                for q in range(2):
                    pe.wait_ge(k_evacuated[q], g)
                    for h in range(HK // 2):
                        col = (q * (HK // 2) + h) * D
                        turned = nc.tensor.transpose(k_ps[q][:, h * P:(h + 1) * P], k_nat[:, col:col + D], ident[:])
                    turned.then_inc(k_transposed, 1)
                pe.wait_ge(x2_ready, g + 1)
                pe.wait_ge(diag2_ready, g + 1)
                pe.wait_ge(x3_ready, g)
                nc.tensor.matmul(l2_ps[:], diag2[u][:], x12[u][:], start=True, stop=True).then_inc(l2_done, 1)

            layer0(0, 0)
            turn_x1(0, 0)
            groups(pe, step)
            turn_x3(G // 2, -1)


def stage_values(nc, wv, wq, wk, table, seqlens, freq, qw, kw, ident, x3t_hi, x3t_lo, rope, w_nat, stat, v_index,
                 x3t_dram, vn_dram):
    U = 2
    GC = G // RC
    BANKS = 4
    with ExitStack() as ctx:
        a_ = Alloc(nc, ctx, "values")
        wv_nat = a_.sb("wv_nat", [P, HK - WV_EARLY, HID])
        wvt_hi = a_.sb("wvt_hi", [P, IC, KVD], F32R)
        wvt_lo = a_.sb("wvt_lo", [P, IC, KVD], F32R)
        slot_hi = [a_.sb(f"slot_hi{u}", [P, IC, P], F32R) for u in range(U)]
        slot_lo = [a_.sb(f"slot_lo{u}", [P, IC, P], F32R) for u in range(U)]
        v_out = [a_.sb(f"v_out{u}", [P, KVD]) for u in range(U)]
        freq_sb = a_.sb("freq", [P, 1])
        wcol = a_.sb("wcol", [P, 4])
        seq_i = a_.sb("seq_i", [P, B], I32)
        seq_f = a_.sb("seq_f", [P, B])
        step_i = a_.sb("step_i", [P, S], I32)
        step_f = a_.sb("step_f", [P, S])
        turns, angle, cosine, sine = (rope[:, n, :] for n in range(4))
        pages_i = a_.sb("pages_i", [P, B, NPP], I32)
        row_i = a_.sb("row_i", [P, 1], I32)
        row_f = a_.sb("row_f", [P, 1])
        w_ps = [a_.ps(f"w{n}") for n in range(BANKS)]
        v_ps = [a_.ps(f"v{u}{n}") for u in range(U) for n in range(2)]

        wv_loaded = a_.sem("wv_loaded")
        w_nat_loaded = a_.sem("w_nat_loaded")
        x3t_loaded = a_.sem("x3t_loaded", RC)
        x3t_hi_ready = a_.sem("x3t_hi_ready")
        x3t_lo_ready = a_.sem("x3t_lo_ready")
        wv_hi_ready = a_.sem("wv_hi_ready")
        small_loaded = a_.sem("small_loaded")
        w_turned = a_.sem("w_turned")
        w_ready = a_.sem("w_ready")
        slot_ready = a_.sem("slot_ready", U)
        v_done = a_.sem("v_done", U)
        v_ready = a_.sem("v_ready", U)
        v_stored = a_.sem("v_stored", U)
        iotas = a_.sem("iotas")
        chain = a_.sem("chain")
        reduced = a_.sem("reduced")
        sines = a_.sem("sines")
        block = ctx.enter_context(nc.Block())

        def split_all(split_weights, split_rows):
            for h in range(WV_EARLY):
                split_weights(h)
            split_rows(0)
            for h in range(WV_EARLY, HK):
                split_weights(h)
            for rc in range(1, RC):
                split_rows(rc)

        @block.sync
        def _(sp):
            for rc in range(RC):
                rows = slice(rc * 512, (rc + 1) * 512)
                sp.dma_start(f32(x3t_lo[:, :, rows]), x3t_dram[:, :, rows]).then_inc(x3t_loaded[rc], 16)
                if rc == 0:
                    load_wv(sp, wv, wv_nat, slice(WV_EARLY, HK), wv_loaded)
            sp.dma_start(seq_i[:], seqlens.rearrange("(o b) -> o b", o=1).to_broadcast([P, B])).then_inc(small_loaded, 16)
            sp.dma_start(pages_i[:], table.rearrange("(o b) n -> o b n", o=1).to_broadcast([P, B, NPP])).then_inc(small_loaded, 16)
            sp.dma_start(freq_sb[:], freq).then_inc(small_loaded, 16)
            sp.dma_start(wcol[:, 0:1], qw.rearrange("(p o) -> p o", o=1)).then_inc(small_loaded, 16)
            sp.dma_start(wcol[:, 1:2], kw.rearrange("(p o) -> p o", o=1)).then_inc(small_loaded, 16)
            for half in (slice(0, 64), slice(64, P)):
                partner = slice(64 - half.start, P - half.start)
                sp.dma_start(wcol[half, 2:3], qw.rearrange("(p o) -> p o", o=1)[partner]).then_inc(small_loaded, 16)
                sp.dma_start(wcol[half, 3:4], kw.rearrange("(p o) -> p o", o=1)[partner]).then_inc(small_loaded, 16)
            sp.wait_ge(w_turned, WV_EARLY)
            load_head_weights(sp, wq, wk, w_nat, 0, w_nat_loaded)
            with sp.Fori(0, G // U) as i:
                for u in range(U):
                    sp.wait_ge(v_ready[u], (i + 1) * 2)
                    sp.dma_start(vn_dram[bass.ds((i * U + u) * P, P)], v_out[u][:]).then_inc(v_stored[u], 16)
            for u in range(U):
                sp.wait_ge(v_stored[u], 16 * (G // U))
            sp.wait_ge(w_nat_loaded, 32)

        @block.gpsimd
        def _(pool):
            nc.gpsimd.iota(step_i[:], pattern=[[1, S]], base=0, channel_multiplier=0).then_inc(iotas, 1)
            pool.wait_ge(iotas, 1)
            for c in range(PPT):
                nc.gpsimd.iota(row_i[c * PSIZE:(c + 1) * PSIZE], pattern=[[1, 1]], base=0,
                               channel_multiplier=1).then_inc(iotas, 1)
            pool.wait_ge(iotas, 1 + PPT)

            def chunk(rc, first):
                pool.wait_ge(x3t_lo_ready, rc + 1)
                for gg in range(GC):
                    u = gg % U
                    if gg >= U or not first:
                        pool.wait_ge(v_done[u], rc * (GC // U) + gg // U)
                    for part, x in ((slot_hi, x3t_hi), (slot_lo, x3t_lo)):
                        nc.gpsimd.tensor_copy(part[u][:], f32(x[:, :, bass.ds((rc * GC + gg) * P, P)])).then_inc(slot_ready[u], 1)

            chunk(0, True)
            with pool.Fori(1, RC) as rc:
                chunk(rc, False)

        @block.tensor
        def _(pe):
            for h in range(HK):
                if h == WV_EARLY:
                    pe.wait_ge(wv_loaded, 16)
                rows = w_nat[:, h] if h < WV_EARLY else wv_nat[:, h - WV_EARLY]
                if h >= BANKS:
                    pe.wait_ge(w_ready, h - BANKS + 1)
                for c in range(IC):
                    last = nc.tensor.transpose(w_ps[h % BANKS][:, c * P:(c + 1) * P], rows[:, c * P:(c + 1) * P], ident[:])
                last.then_inc(w_turned, 1)
            pe.wait_ge(w_ready, HK)

            def chunk(rc, first):
                for gg in range(GC):
                    u, before = gg % U, rc * (GC // U) + gg // U
                    pe.wait_ge(slot_ready[u], before * 2 + 2)
                    if gg >= U or not first:
                        pe.wait_ge(v_ready[u], before * 2)
                    for n in range(2):
                        for c in range(IC):
                            for k, (x, w) in enumerate(((slot_hi, wvt_hi), (slot_hi, wvt_lo), (slot_lo, wvt_hi))):
                                last = nc.tensor.matmul(v_ps[2 * u + n][:], x[u][:, c, :], w[:, c, n * 512:(n + 1) * 512],
                                                        start=(c == 0 and k == 0), stop=(c == IC - 1 and k == 2))
                    last.then_inc(v_done[u], 1)

            chunk(0, True)
            with pe.Fori(1, RC) as rc:
                chunk(rc, False)

        @block.scalar
        def _(act):
            def split_weights(h):
                act.wait_ge(w_turned, h + 1)
                nc.scalar.activation(wvt_hi[:, :, h * D:(h + 1) * D], w_ps[h % BANKS].rearrange("p (c e) -> p c e", c=IC),
                                     ACT.Copy).then_inc(wv_hi_ready, 1)

            def split_rows(rc):
                rows = slice(rc * 512, (rc + 1) * 512)
                act.wait_ge(x3t_loaded[rc], 16)
                nc.scalar.activation(x3t_hi[:, :, rows], f32(x3t_lo[:, :, rows]), ACT.Copy).then_inc(x3t_hi_ready, 1)

            split_all(split_weights, split_rows)

            def chunk(rc, first):
                for gg in range(GC):
                    u, before = gg % U, rc * (GC // U) + gg // U
                    act.wait_ge(v_done[u], before + 1)
                    if gg >= U or not first:
                        act.wait_ge(v_stored[u], before * 16)
                    for n in range(2):
                        nc.scalar.activation(v_out[u][:, n * 512:(n + 1) * 512], v_ps[2 * u + n][:],
                                             ACT.Copy).then_inc(v_ready[u], 1)

            chunk(0, True)
            chunk(1, False)
            act.wait_ge(reduced, 2)
            nc.scalar.activation(sine, angle, ACT.Sin).then_inc(sines, 1)
            nc.scalar.activation(cosine, turns, ACT.Sin).then_inc(sines, 1)
            with act.Fori(2, RC) as rc:
                chunk(rc, False)

        @block.vector
        def _(dve):
            def split_weights(h):
                dve.wait_ge(wv_hi_ready, h + 1)
                cols = slice(h * D, (h + 1) * D)
                nc.vector.tensor_tensor(wvt_lo[:, :, cols], w_ps[h % BANKS].rearrange("p (c e) -> p c e", c=IC),
                                        f32(wvt_hi[:, :, cols]), ALU.subtract).then_inc(w_ready, 1)

            def split_rows(rc):
                rows = slice(rc * 512, (rc + 1) * 512)
                dve.wait_ge(x3t_hi_ready, rc + 1)
                nc.vector.tensor_tensor(x3t_lo[:, :, rows], f32(x3t_lo[:, :, rows]), f32(x3t_hi[:, :, rows]),
                                        ALU.subtract).then_inc(x3t_lo_ready, 1)

            split_all(split_weights, split_rows)
            dve.wait_ge(small_loaded, 16 * 9)
            dve.wait_ge(iotas, 1 + PPT)
            steps = [0]

            def then(instruction):
                steps[0] += 1
                instruction.then_inc(chain, 1)
                dve.wait_ge(chain, steps[0])

            nc_v = nc.vector
            then(nc_v.tensor_copy(seq_f[:], seq_i[:]))
            then(nc_v.tensor_copy(step_f[:], step_i[:]))
            then(nc_v.tensor_copy(row_f[:], row_i[:]))
            then(nc_v.tensor_scalar(wcol[0:64, 2:4], wcol[0:64, 2:4], -1.0, None, ALU.mult))
            shape = [P, B, S]
            then(nc_v.tensor_tensor(angle.rearrange("p (b s) -> p b s", b=B), seq_f.rearrange("p (b o) -> p b o", o=1).to_broadcast(shape),
                                    step_f.rearrange("p (o s) -> p o s", o=1).to_broadcast(shape), ALU.add))
            then(nc_v.tensor_scalar(angle, angle, freq_sb[:, 0:1], None, ALU.mult))
            then(nc_v.tensor_scalar(turns, angle, float(1 / (2 * np.pi)), ROUND, ALU.mult, ALU.add))
            then(nc_v.tensor_scalar(turns, turns, ROUND, None, ALU.subtract))
            for part in TWO_PI:
                then(nc_v.scalar_tensor_tensor(angle, turns, -part, angle, ALU.mult, ALU.add))
            then(nc_v.tensor_scalar(turns, angle, float(np.pi / 2), float(-2 * np.pi), ALU.is_gt, ALU.mult))
            then(nc_v.scalar_tensor_tensor(turns, angle, float(np.pi / 2), turns, ALU.add, ALU.add))
            for t in (angle, turns):
                steps[0] += 1
                nc_v.tensor_scalar(t, t, PI, -PI, ALU.min, ALU.max).then_inc(chain, 1)
                dve.wait_ge(chain, steps[0])
                dve.sem_inc(reduced, 1)
            for c in range(PPT):
                rows = slice(c * PSIZE, (c + 1) * PSIZE)
                then(nc_v.tensor_scalar(v_index[rows, :, :], pages_i[rows, :, :].rearrange("p b (t c) -> p b t c", c=PPT)[:, :, :, c],
                                        float(PSIZE), row_f[rows, 0:1], ALU.mult, ALU.add))
            then(nc_v.tensor_copy(stat[:, :, HK], seq_f[:]))
            dve.wait_ge(sines, 2)
            for n, (src, w) in enumerate(((cosine, 0), (sine, 2), (cosine, 1), (sine, 3))):
                then(nc_v.tensor_scalar(rope[:, n, :], src, wcol[:, w:w + 1], None, ALU.mult))


def load_head_weights(sp, wq, wk, w_nat, h, loaded):
    sp.dma_start(w_nat[:, 0, :], wk[bass.ds(h * D, D)]).then_inc(loaded, 16)
    sp.dma_start(w_nat[:, 1:, :], wq[bass.ds(h * (REP * D), REP * D)].rearrange("(m p) i -> p m i", p=P)).then_inc(loaded, 16)


def stage_projection(nc, wq, wk, ident, x3t_hi, x3t_lo, rope, w_nat, stat, qt_dram, kn_dram):
    with ExitStack() as ctx:
        a_ = Alloc(nc, ctx, "proj")
        M = 1 + REP
        TPH = RC * M
        RING = 4
        w_hi = [a_.sb(f"w_hi{u}", [P, M, IC, P], F32R) for u in range(2)]
        w_lo = [a_.sb(f"w_lo{u}", [P, M, IC, P], F32R) for u in range(2)]
        ones = a_.sb("ones", [P, P])
        raw = [a_.sb(f"raw{n}", [P, 512]) for n in range(2)]
        q_squares = [[a_.sb(f"q_squares{v}{r}", [P, 512]) for r in range(REP)] for v in range(2)]
        k_squares = a_.sb("k_squares", [P, 512])
        by_cos = [a_.sb(f"by_cos{n}", [P, 512]) for n in range(2)]
        by_sin = [a_.sb(f"by_sin{n}", [P, 512]) for n in range(2)]
        q_out = [a_.sb(f"q_out{n}", [P, CB, REP, S]) for n in range(2)]
        k_out = [a_.sb(f"k_out{n}", [P, CB, S]) for n in range(2)]
        k_rms = a_.sb("k_rms", [P, 512])
        stat_t = a_.sb("stat_t", [P, CB, S])
        w_ps = [a_.ps(f"w{n}") for n in range(2)]
        proj_ps = [a_.ps(f"proj{k}") for k in range(RING)]
        ksum_ps = a_.ps("ksum")
        qsum_ps = a_.ps("qsum")

        w_loaded = a_.sem("w_loaded")
        w_turned = a_.sem("w_turned")
        w_hi_ready = a_.sem("w_hi_ready")
        w_ready = a_.sem("w_ready")
        ones_ready = a_.sem("ones_ready")
        proj_done = a_.sem("proj_done")
        raw_ready = a_.sem("raw_ready")
        swapped = a_.sem("swapped")
        squared = a_.sem("squared")
        ksum_done = a_.sem("ksum_done")
        qsum_done = a_.sem("qsum_done")
        k_mean = a_.sem("k_mean")
        k_root = a_.sem("k_root")
        k_scaled = a_.sem("k_scaled")
        inverted = a_.sem("inverted")
        stat_turned = a_.sem("stat_turned")
        stat_ready = a_.sem("stat_ready")
        products = a_.sem("products")
        rotated = a_.sem("rotated")
        q_stored = a_.sem("q_stored", 2)
        k_stored = a_.sem("k_stored", 2)
        block = ctx.enter_context(nc.Block())

        def heads(engine, head):
            for u in range(2):
                head(u, u, u == 0, False)
            with engine.Fori(1, HK // 2 - 1) as i:
                for u in range(2):
                    head(i * 2 + u, u, False, False)
            for u in range(2):
                head(HK - 2 + u, u, False, u == 1)

        @block.sync
        def _(sp):
            def head(h, u, first, last):
                if not last:
                    sp.wait_ge(w_turned, M)
                    sp.wait_ge(w_turned, h * M + M)
                    load_head_weights(sp, wq, wk, w_nat, h + 1, w_loaded)
                for rc in range(RC):
                    sp.wait_ge(rotated, h * TPH + (rc + 1) * M)
                    sp.dma_start(qt_dram[bass.ds(h, 1), :, rc * CB:(rc + 1) * CB, :].rearrange("h d b n -> d (h b n)"),
                                 q_out[rc % 2].rearrange("d b r s -> d (b r s)")).then_inc(q_stored[rc % 2], 16)
                    sp.wait_ge(k_scaled, h * RC + (rc + 1))
                    sp.dma_start(kn_dram[rc * CB:(rc + 1) * CB, :, bass.ds(h, 1), :].rearrange("b d h s -> d b (h s)"),
                                 k_out[rc % 2][:]).then_inc(k_stored[rc % 2], 16)

            heads(sp, head)
            for n in range(2):
                sp.wait_ge(q_stored[n], 16 * HK * (RC // 2))
                sp.wait_ge(k_stored[n], 16 * HK * (RC // 2))

        @block.tensor
        def _(pe):
            def turn_weights(h, u, m, first=False):
                if m == 0 and not first:
                    pe.wait_ge(w_loaded, h * 32)
                n = (u * M + m) % 2
                if m >= 2 or not first:
                    pe.wait_ge(w_ready, h * M + (m - 1))
                for c in range(IC):
                    last = nc.tensor.transpose(w_ps[n][:, c * P:(c + 1) * P], w_nat[:, m, c * P:(c + 1) * P], ident[:])
                last.then_inc(w_turned, 1)

            def sum_k(h, rc):
                chunk = h * RC + rc
                pe.wait_ge(squared, chunk * M + 1)
                pe.wait_ge(k_mean, chunk)
                nc.tensor.matmul(ksum_ps[:], ones[:], k_squares[:], start=True, stop=True).then_inc(ksum_done, 1)

            def sum_q(h, rc):
                chunk = h * RC + rc
                pe.wait_ge(squared, (chunk + 1) * M)
                pe.wait_ge(stat_turned, chunk)
                for r in range(REP):
                    last = nc.tensor.matmul(qsum_ps[r * S:(r + 1) * S, :], ones[:, 0:S], q_squares[rc % 2][r][:],
                                            start=True, stop=True)
                last.then_inc(qsum_done, 1)

            def head(h, u, first, last_head):
                for t in range(TPH):
                    rc, m = divmod(t, M)
                    if rc == 0:
                        pe.wait_ge(w_ready, h * M + (m + 1))
                    if t >= RING or not first:
                        pe.wait_ge(squared, h * TPH + (t - RING + 1))
                    for c in range(IC):
                        for k, (w, x) in enumerate(((w_hi, x3t_hi), (w_hi, x3t_lo), (w_lo, x3t_hi))):
                            last = nc.tensor.matmul(proj_ps[t % RING][:], w[u][:, m, c, :], x[:, c, rc * 512:(rc + 1) * 512],
                                                    start=(c == 0 and k == 0), stop=(c == IC - 1 and k == 2))
                    last.then_inc(proj_done, 1)
                    if m == 2:
                        sum_k(h, rc)
                    if m == 1 and (rc or not first):
                        sum_q(h, rc - 1)
                    if rc == 1 and not last_head:
                        turn_weights(h + 1, 1 - u, m)

            for m in range(M):
                turn_weights(0, 0, m, True)
            pe.wait_ge(ones_ready, 1)
            heads(pe, head)
            sum_q(HK, -1)

        @block.scalar
        def _(act):
            def split_weights(h, u, m):
                act.wait_ge(w_turned, h * M + (m + 1))
                nc.scalar.activation(w_hi[u][:, m].rearrange("p c e -> p (c e)"), w_ps[(u * M + m) % 2][:],
                                     ACT.Copy).then_inc(w_hi_ready, 1)

            def head(h, u, first, last):
                for t in range(TPH):
                    rc, m = divmod(t, M)
                    act.wait_ge(proj_done, h * TPH + (t + 1))
                    if t >= 2 or not first:
                        act.wait_ge(products, h * TPH + (t - 1))
                    product = proj_ps[t % RING]
                    chunk = h * RC + rc
                    nc.scalar.activation(raw[t % 2][:], product[:], ACT.Copy).then_inc(raw_ready, 1)
                    if t >= 2 or not first:
                        act.wait_ge(rotated, h * TPH + (t - 1))
                    nc.scalar.activation(by_sin[t % 2][0:64], product[64:P], ACT.Copy)
                    nc.scalar.activation(by_sin[t % 2][64:P], product[0:64], ACT.Copy).then_inc(swapped, 1)
                    if m == 0:
                        if rc or not first:
                            act.wait_ge(ksum_done, chunk)
                        nc.scalar.activation(k_squares[:], product[:], ACT.Square).then_inc(squared, 1)
                    else:
                        if rc >= 2 or not first:
                            act.wait_ge(qsum_done, chunk - 1)
                        nc.scalar.activation(q_squares[rc % 2][m - 1][:], product[:], ACT.Square).then_inc(squared, 1)
                    if rc == 1 and not last:
                        split_weights(h + 1, 1 - u, m)
                    if m == 3:
                        act.wait_ge(k_mean, h * RC + (rc + 1))
                        nc.scalar.activation(k_rms[:], k_rms[:], ACT.Sqrt).then_inc(k_root, 1)

            for m in range(M):
                split_weights(0, 0, m)
            heads(act, head)
            act.wait_ge(k_mean, HK * RC + 1)
            nc.scalar.activation(stat[:, :, 0:HK], stat[:, :, 0:HK], ACT.Sqrt).then_inc(k_root, 1)

        @block.vector
        def _(dve):
            def split_weights(h, u, m):
                dve.wait_ge(w_hi_ready, h * M + (m + 1))
                nc.vector.tensor_tensor(w_lo[u][:, m].rearrange("p c e -> p (c e)"), w_ps[(u * M + m) % 2][:],
                                        f32(w_hi[u][:, m]).rearrange("p c e -> p (c e)"), ALU.subtract).then_inc(w_ready, 1)

            def rotate(h, t, first):
                rc, m = divmod(t, M)
                cols = slice(rc * 512, (rc + 1) * 512)
                cos, sin = (2, 3) if m == 0 else (0, 1)
                n = t % 2
                dve.wait_ge(raw_ready, h * TPH + (t + 1))
                if t >= 2 or not first:
                    dve.wait_ge(rotated, h * TPH + (t - 1))
                nc.vector.tensor_tensor(by_cos[n][:], raw[n][:], rope[:, cos, cols], ALU.mult)
                dve.wait_ge(swapped, h * TPH + (t + 1))
                nc.vector.tensor_tensor(by_sin[n][:], by_sin[n][:], rope[:, sin, cols], ALU.mult).then_inc(products, 1)

            def mean_k(h, rc, first):
                dve.wait_ge(ksum_done, h * RC + (rc + 1))
                if rc or not first:
                    dve.wait_ge(k_scaled, h * RC + rc)
                nc.vector.tensor_scalar(k_rms[:], ksum_ps[:], 1.0 / D, EPS, ALU.mult, ALU.add).then_inc(k_mean, 1)

            def scale_k(h, rc):
                dve.wait_ge(k_root, h * RC + (rc + 1))
                nc.vector.reciprocal(k_rms[:], k_rms[:]).then_inc(inverted, 1)
                dve.wait_ge(inverted, h * RC + (rc + 1))
                dve.wait_ge(rotated, h * TPH + (rc * M + 1))
                kf = k_out[rc % 2].rearrange("d b s -> d (b s)")
                nc.vector.tensor_tensor(kf, kf, k_rms[:], ALU.mult).then_inc(k_scaled, 1)

            def keep_q(h, rc, first):
                dve.wait_ge(qsum_done, h * RC + (rc + 1))
                if rc or not first:
                    dve.wait_ge(stat_ready, h * RC + rc)
                nc.vector.transpose(stat_t.rearrange("p b s -> p (b s)"), qsum_ps[:]).then_inc(stat_turned, 1)
                dve.wait_ge(stat_turned, h * RC + (rc + 1))
                c = rc % RC
                nc.vector.tensor_copy(stat[:, c * CB:(c + 1) * CB, bass.ds(h if rc >= 0 else h - 1, 1)],
                                      stat_t[:, :, 0:1]).then_inc(stat_ready, 1)

            def head(h, u, first, last):
                for t in range(TPH):
                    rc, m = divmod(t, M)
                    if m == 2 and (rc or not first):
                        keep_q(h, rc - 1, first)
                    if m == 3:
                        mean_k(h, rc, first)
                    rotate(h, t, first)
                    if rc == 1 and not last:
                        split_weights(h + 1, 1 - u, m)
                    if m == 4:
                        scale_k(h, rc)

            for m in range(M):
                split_weights(0, 0, m)
            heads(dve, head)
            keep_q(HK, -1, False)
            dve.wait_ge(stat_ready, HK * RC)
            qs = stat[:, :, 0:HK]
            nc.vector.tensor_scalar(qs, qs, 1.0 / D, EPS, ALU.mult, ALU.add).then_inc(k_mean, 1)
            dve.wait_ge(k_root, HK * RC + 1)
            nc.vector.tensor_scalar(qs, qs, -1.0 / SCALE, None, ALU.mult).then_inc(inverted, 1)

        @block.gpsimd
        def _(pool):
            def head(h, u, first, last):
                for t in range(TPH):
                    rc, m = divmod(t, M)
                    n = t % 2
                    pool.wait_ge(products, h * TPH + (t + 1))
                    if m == 0:
                        if rc >= 2 or not first:
                            pool.wait_ge(k_stored[rc % 2], h * 32 + (rc // 2) * 16)
                        out = k_out[rc % 2][:]
                    else:
                        if m == 1 and (rc >= 2 or not first):
                            pool.wait_ge(q_stored[rc % 2], h * 32 + (rc // 2) * 16)
                        out = q_out[rc % 2][:, :, m - 1, :]
                    nc.gpsimd.tensor_tensor(out, by_cos[n].rearrange("d (b s) -> d b s", s=S),
                                            by_sin[n].rearrange("d (b s) -> d b s", s=S), ALU.add).then_inc(rotated, 1)

            nc.gpsimd.memset(ones[:], 1.0).then_inc(ones_ready, 1)
            heads(pool, head)


def stage_attention(nc, table, v_cache, ident, stat, v_index, kt_dram, kn_dram, qt_dram, vn_dram, ot_dram):
    N = 2 * HK
    RING = 4
    PAIRS = B // 2
    PAGE_CHUNKS = [slice(0, 2), slice(2, 4), slice(4, 6), slice(6, 9), slice(9, 12), slice(12, 15), slice(15, NPP + 1)]
    QUERY_CHUNKS = [slice(0, 3), slice(3, 6), slice(6, HK)]
    CHUNKS, QCHUNKS = len(PAGE_CHUNKS), len(QUERY_CHUNKS)
    FIRST = NPP // 2 + 1
    LEFT = 512 - FIRST * PSIZE
    with ExitStack() as ctx:
        a_ = Alloc(nc, ctx, "att")
        pages_sb = a_.sb("pages", [1, B * NPP], I32)
        keys_raw = a_.sb("keys_raw", [P, NPP + 1, HK, PSIZE])
        queries_raw = a_.sb("queries_raw", [P, HK, P])
        keys_hi = [a_.sb(f"keys_hi{v}", [P, NPP + 1, HK, PSIZE], F32R) for v in range(2)]
        keys_lo = [a_.sb(f"keys_lo{v}", [P, NPP + 1, HK, PSIZE], F32R) for v in range(2)]
        queries_hi = [a_.sb(f"queries_hi{v}", [P, HK, P], F32R) for v in range(2)]
        queries_lo = [a_.sb(f"queries_lo{v}", [P, HK, P], F32R) for v in range(2)]
        values = [a_.sb(f"values{v}", [P, PPT, KVD]) for v in range(2)]
        new_values = [a_.sb(f"new_values{v}", [P, KVD]) for v in range(2)]
        v_rows_of = [a_.sb(f"v_rows_of{v}", [P, PPT], I32) for v in range(2)]
        key_no_i = a_.sb("key_no_i", [P, L], I32)
        key_no = a_.sb("key_no", [P, L])
        batch_cols = [a_.sb(f"batch_cols{v}", [P, HK + 1]) for v in range(2)]
        mask = [a_.sb(f"mask{v}", [P, KEYS]) for v in range(2)]
        probs = [a_.sb(f"probs{k}", [P, KEYS]) for k in range(RING)]
        low = [a_.sb(f"low{k}", [P, 1]) for k in range(RING)]
        total = [a_.sb(f"total{k}", [P, 1]) for k in range(RING)]
        inverse = [a_.sb(f"inverse{k}", [P, 1]) for k in range(RING)]
        probs_t = [a_.sb(f"probs_t{n}", [P, L]) for n in range(2)]
        new_probs_t = [a_.sb(f"new_probs_t{n}", [P, P]) for n in range(2)]
        heads_out = [a_.sb(f"heads_out{v}", [P, HK, P]) for v in range(2)]
        score_ps = [a_.ps(f"score{n}", 1024) for n in range(2)]
        turn_ps = [a_.ps(f"turn{n}") for n in range(2)]
        o_ps = a_.ps("o")
        new_ps = a_.ps("new")

        pages_loaded = a_.sem("pages_loaded")
        raw_loaded = a_.sem("raw_loaded", CHUNKS)
        queries_loaded = a_.sem("queries_loaded")
        hi_ready = a_.sem("hi_ready")
        queries_hi_ready = a_.sem("queries_hi_ready")
        lo_ready = a_.sem("lo_ready")
        queries_lo_ready = a_.sem("queries_lo_ready")
        v_loaded = a_.sem("v_loaded", 2)
        zeroed = a_.sem("zeroed")
        index_ready = a_.sem("index_ready")
        iota_done = a_.sem("iota_done")
        setup = a_.sem("setup")
        cols_ready = a_.sem("cols_ready")
        mask_ready = a_.sem("mask_ready")
        scores_done = a_.sem("scores_done", 2)
        scores_masked = a_.sem("scores_masked", 2)
        exp_done = a_.sem("exp_done")
        inverse_ready = a_.sem("inverse_ready")
        probs_ready = a_.sem("probs_ready")
        main_turned = a_.sem("main_turned", 2)
        all_turned = a_.sem("all_turned", RING)
        main_ready = a_.sem("main_ready", 2)
        new_ready = a_.sem("new_ready")
        o_done = a_.sem("o_done", 2)
        o_ready = a_.sem("o_ready")
        o_stored = a_.sem("o_stored", 2)
        block = ctx.enter_context(nc.Block())

        VN = 16 * (PPT + 1)

        @block.sync
        def _(sp):
            sp.dma_start(pages_sb[:], table.rearrange("(o b) n -> o (b n)", o=1)).then_inc(pages_loaded, 16)
            sp.wait_ge(pages_loaded, 16)

            def load(b, first):
                _, pages = nc.values_load_multi_w_load_instructions(
                    pages_sb[0:1, bass.ds(b * NPP, NPP)], engines=(mybir.EngineType.SP,), min_val=0, max_val=PAGES - 1)
                for c, chunk in enumerate(PAGE_CHUNKS):
                    if not first:
                        sp.wait_ge(pages_loaded, 16)
                        sp.wait_ge(lo_ready, (b - 1) * CHUNKS + (c + 1))
                    for n in range(chunk.start, chunk.stop):
                        if n < NPP:
                            sp.dma_start(keys_raw[:, n], kt_dram[bass.ds(pages[n], 1)].rearrange("n d h k -> d (n h) k")).then_inc(raw_loaded[c], 16)
                        elif not first:
                            sp.dma_start(keys_raw[:, NPP], kn_dram[bass.ds(b, 1)].rearrange("b d h s -> d (b h) s")).then_inc(raw_loaded[c], 16)
                    if c == QCHUNKS - 1:
                        if not first:
                            sp.wait_ge(pages_loaded, 16)
                            sp.wait_ge(queries_lo_ready, b * QCHUNKS)
                            sp.dma_start(queries_raw[:], qt_dram[:, :, bass.ds(b, 1), :].rearrange("h d b n -> d h (b n)")).then_inc(queries_loaded, 16)

            load(0, True)
            with sp.Fori(1, B) as b:
                load(b, False)

        @block.gpsimd
        def _(pool):
            nc.gpsimd.iota(key_no_i[:], pattern=[[1, L]], base=0, channel_multiplier=0).then_inc(iota_done, 1)
            for v in range(2):
                nc.gpsimd.memset(new_values[v][:], 0.0).then_inc(zeroed, 1)
                nc.gpsimd.memset(new_probs_t[v][:], 0.0).then_inc(zeroed, 1)
            pool.wait_ge(zeroed, 4)
            v_rows = v_cache.rearrange("n k h d -> (n k) (h d)")

            def load(v, b, parts):
                if 0 in parts:
                    nc.gpsimd.dma_start(new_values[v][0:S, :], vn_dram[bass.ds(b * S, S)]).then_inc(v_loaded[v], 16)
                    nc.gpsimd.tensor_copy(v_rows_of[v][:], v_index[:, bass.ds(b, 1), :].rearrange("p b t -> p (b t)")).then_inc(index_ready, 1)
                    pool.lower_val(b + 1)
                    pool.wait_ge(zeroed, 4)
                    pool.wait_ge(index_ready, b + 1)
                for t in range(PPT):
                    if t + 1 in parts:
                        nc.gpsimd.indirect_dma_start(
                            values[v][:, t, :], None, v_rows,
                            bass.IndirectOffsetOnAxis(ap=v_rows_of[v][:, t:t + 1], axis=0)).then_inc(v_loaded[v], 16)

            def split(b, c, v):
                heads = QUERY_CHUNKS[c]
                pool.wait_ge(queries_hi_ready, b * QCHUNKS + (c + 1))
                nc.gpsimd.tensor_tensor(queries_lo[v][:, heads], queries_raw[:, heads], f32(queries_hi[v][:, heads]),
                                        ALU.subtract).then_inc(queries_lo_ready, 1)

            def pair(i, first, last_pair):
                for n in range(N):
                    j, h = divmod(n, HK)
                    if h < QCHUNKS and not (last_pair and j == 1):
                        split(i * 2 + (j + 1), h, (j + 1) % 2)
                    if h >= 3 and not (last_pair and j == 1):
                        if h == 3 and (j or not first):
                            pool.wait_ge(o_done[1], i * (N // 2) + j * (HK // 2))
                        load((j + 1) % 2, i * 2 + (j + 1), [h - 3])
                    pool.wait_ge(inverse_ready, i * N + n + 1)
                    k = n % RING
                    nc.gpsimd.tensor_tensor(probs[k][:], probs[k][:], inverse[k][:, 0:1].to_broadcast([P, KEYS]),
                                            ALU.mult).then_inc(probs_ready, 1)

            pool.wait_ge(raw_loaded[1], 32)
            load(0, 0, (0, 1, 2))
            for c in range(QCHUNKS):
                split(0, c, 0)
            load(0, 0, (3, 4))
            pair(0, True, False)
            with pool.Fori(1, PAIRS - 1) as i:
                pair(i, False, False)
            pair(PAIRS - 1, False, True)

        @block.tensor
        def _(pe):
            def scores(i, n):
                j, h = divmod(n, HK)
                if h == 0:
                    pe.wait_ge(lo_ready, i * (2 * CHUNKS) + (j + 1) * CHUNKS)
                    pe.wait_ge(queries_lo_ready, i * (2 * QCHUNKS) + (j + 1) * QCHUNKS)
                pe.wait_ge(scores_masked[n % 2], i * (N // 2) + n // 2)
                for pages, cols in ((slice(0, FIRST), slice(LEFT, 512)), (slice(FIRST, NPP + 1), slice(512, LEFT + KEYS))):
                    for k, (q, kt) in enumerate(((queries_hi, keys_hi), (queries_hi, keys_lo), (queries_lo, keys_hi))):
                        last = nc.tensor.matmul(score_ps[n % 2][:, cols], q[j][:, h, :], kt[j][:, pages, h, :],
                                                start=(k == 0), stop=(k == 2))
                last.then_inc(scores_done[n % 2], 1)

            def turn(i, n):
                pe.wait_ge(probs_ready, i * N + (n + 1))
                pe.wait_ge(main_ready[n % 2], i * (N // 2) + n // 2)
                for t in range(PPT):
                    last = nc.tensor.transpose(turn_ps[n % 2][:, t * P:(t + 1) * P], probs[n % RING][:, t * P:(t + 1) * P], ident[:])
                last.then_inc(main_turned[n % 2], 1)
                pe.wait_ge(new_ready, i * N + n)
                nc.tensor.transpose(new_ps[0:S, 0:P], probs[n % RING][:, L:KEYS], ident[:]).then_inc(all_turned[n % RING], 1)

            def weigh(i, n):
                j, h = (n // HK) % 2, n % HK
                if h == 0:
                    pe.wait_ge(v_loaded[j], i * VN + VN)
                pe.wait_ge(main_ready[n % 2], i * (N // 2) + (n // 2 + 1))
                pe.wait_ge(new_ready, i * N + (n + 1))
                pe.wait_ge(o_ready, i * N + n)
                for t in range(PPT):
                    nc.tensor.matmul(o_ps[:, 0:P], values[j][:, t, h * D:(h + 1) * D], probs_t[n % 2][:, t * P:(t + 1) * P],
                                     start=(t == 0), stop=False)
                nc.tensor.matmul(o_ps[:, 0:P], new_values[j][:, h * D:(h + 1) * D], new_probs_t[n % 2][:],
                                 start=False, stop=True).then_inc(o_done[n % 2], 1)

            def pair(i, first):
                for n in range(N):
                    scores(i, n)
                    if n >= 2 or not first:
                        turn(i, n - 2)
                    if n >= 3 or not first:
                        weigh(i, n - 3)

            pair(0, True)
            with pe.Fori(1, PAIRS) as i:
                pair(i, False)
            turn(PAIRS, -2)
            weigh(PAIRS, -3)
            turn(PAIRS, -1)
            weigh(PAIRS, -2)
            weigh(PAIRS, -1)

        @block.scalar
        def _(act):
            def split(b, c, v):
                pages = PAGE_CHUNKS[c]
                full = 16 * (pages.stop - pages.start)
                act.wait_ge(raw_loaded[c], b * full + full)
                nc.scalar.activation(keys_hi[v][:, pages], keys_raw[:, pages], ACT.Copy).then_inc(hi_ready, 1)
                if c < QCHUNKS:
                    act.wait_ge(queries_loaded, b * 16 + 16)
                    nc.scalar.activation(queries_hi[v][:, QUERY_CHUNKS[c]], queries_raw[:, QUERY_CHUNKS[c]], ACT.Copy).then_inc(queries_hi_ready, 1)

            def softmax(i, n):
                act.wait_ge(scores_masked[n % 2], i * (N // 2) + (n // 2 + 1))
                k = n % RING
                nc.scalar.activation(probs[k][:], probs[k][:], ACT.Exp, bias=low[k][:, 0:1], scale=-1.0,
                                     accum_out=total[k][:, 0:1]).then_inc(exp_done, 1)

            def new_part(i, n):
                act.wait_ge(all_turned[n % RING], i * (N // RING) + (n // RING + 1))
                act.wait_ge(o_done[n % 2], i * (N // 2) + n // 2)
                nc.scalar.activation(new_probs_t[n % 2][0:S, :], new_ps[0:S, 0:P], ACT.Copy).then_inc(new_ready, 1)

            def keep_o(i, n):
                j, h = (n // HK) % 2, n % HK
                act.wait_ge(o_done[n % 2], i * (N // 2) + (n // 2 + 1))
                if h == 0:
                    act.wait_ge(o_stored[j], i * 16)
                nc.scalar.activation(heads_out[j][:, h], o_ps[:, 0:P], ACT.Copy).then_inc(o_ready, 1)
                if h == HK - 1:
                    act.wait_ge(o_ready, i * N + (n + 1))
                    act.dma_start(ot_dram[bass.ds(i * 2 + n // HK, 1)].rearrange("b d h n -> d (b h n)"),
                                  heads_out[j].rearrange("d h n -> d (h n)")).then_inc(o_stored[j], 16)

            def pair(i, first, last_pair):
                for n in range(N):
                    j, h = divmod(n, HK)
                    if h < CHUNKS and not (last_pair and j == 1):
                        if h == 0:
                            act.wait_ge(scores_done[1], i * (N // 2) + j * (HK // 2))
                        split(i * 2 + (j + 1), h, (j + 1) % 2)
                    softmax(i, n)
                    if n >= 2 or not first:
                        new_part(i, n - 2)
                    if n >= 3 or not first:
                        keep_o(i, n - 3)

            act.dma_start(queries_raw[:], qt_dram[:, :, 0, :].rearrange("h d n -> d h n")).then_inc(queries_loaded, 16)
            act.dma_start(keys_raw[:, NPP], kn_dram[0]).then_inc(raw_loaded[CHUNKS - 1], 16)
            act.wait_ge(zeroed, 4)
            for c in range(CHUNKS):
                split(0, c, 0)
            pair(0, True, False)
            with act.Fori(1, PAIRS - 1) as i:
                pair(i, False, False)
            pair(PAIRS - 1, False, True)
            new_part(PAIRS, -2)
            keep_o(PAIRS, -3)
            new_part(PAIRS, -1)
            keep_o(PAIRS, -2)
            keep_o(PAIRS, -1)
            for v in range(2):
                act.wait_ge(o_stored[v], 16 * PAIRS)

        @block.vector
        def _(dve):
            def split(b, c, v):
                pages = PAGE_CHUNKS[c]
                dve.wait_ge(hi_ready, b * CHUNKS + (c + 1))
                nc.vector.tensor_tensor(keys_lo[v][:, pages], keys_raw[:, pages], f32(keys_hi[v][:, pages]),
                                        ALU.subtract).then_inc(lo_ready, 1)

            def columns(b, v):
                cols = stat[:, bass.ds(b, 1), :].rearrange("p b c -> p (b c)")
                nc.vector.reciprocal(batch_cols[v][:, 0:HK], cols[:, 0:HK])
                nc.vector.tensor_copy(batch_cols[v][:, HK:HK + 1], cols[:, HK:HK + 1]).then_inc(cols_ready, 1)
                dve.wait_ge(cols_ready, b + 1)
                nc.vector.tensor_scalar(mask[v][:, 0:L], key_no[:], batch_cols[v][:, HK:HK + 1], MASKED, ALU.is_ge, ALU.mult).then_inc(mask_ready, 1)

            def mask_scores(i, n):
                j, h = divmod(n, HK)
                k = n % RING
                if h == 0:
                    dve.wait_ge(mask_ready, i * 2 + (j + 1))
                dve.lower_val(i * (N // 2) + (n // 2 + 1))
                dve.lower_val(i * (N // RING) + n // RING)
                dve.wait_ge(setup, 3)
                dve.wait_ge(scores_done[n % 2], i * (N // 2) + (n // 2 + 1))
                dve.wait_ge(all_turned[k], i * (N // RING) + n // RING)
                nc.vector.tensor_tensor_reduce(out=probs[k][:], in0=score_ps[n % 2][:, LEFT:LEFT + KEYS], in1=mask[j][:],
                                               scale=batch_cols[j][:, h:h + 1], scalar=3e38, op0=ALU.add, op1=ALU.min,
                                               accum_out=low[k][:, 0:1]).then_inc(scores_masked[n % 2], 1)

            def main_part(i, n):
                dve.wait_ge(main_turned[n % 2], i * (N // 2) + (n // 2 + 1))
                dve.wait_ge(o_done[n % 2], i * (N // 2) + n // 2)
                nc.vector.tensor_copy(probs_t[n % 2][:], turn_ps[n % 2][:]).then_inc(main_ready[n % 2], 1)

            def invert(i, n):
                dve.wait_ge(exp_done, i * N + (n + 1))
                nc.vector.reciprocal(inverse[n % RING][:], total[n % RING][:]).then_inc(inverse_ready, 1)

            def pair(i, first, last_pair):
                for n in range(N):
                    j, h = divmod(n, HK)
                    mask_scores(i, n)
                    if n >= 2 or not first:
                        main_part(i, n - 2)
                    if not (last_pair and j == 1):
                        if h < CHUNKS:
                            split(i * 2 + (j + 1), h, (j + 1) % 2)
                        else:
                            dve.wait_ge(scores_masked[1], i * (N // 2) + j * (HK // 2))
                            columns(i * 2 + (j + 1), (j + 1) % 2)
                    invert(i, n)

            dve.wait_ge(iota_done, 1)
            nc.vector.tensor_copy(key_no[:], key_no_i[:]).then_inc(setup, 1)
            for v in range(2):
                nc.vector.memset(mask[v][:, L:KEYS], 0.0).then_inc(setup, 1)
            dve.wait_ge(setup, 3)
            columns(0, 0)
            for c in range(CHUNKS):
                split(0, c, 0)
            pair(0, True, False)
            with dve.Fori(1, PAIRS - 1) as i:
                pair(i, False, False)
            pair(PAIRS - 1, False, True)
            main_part(PAIRS, -2)
            main_part(PAIRS, -1)


def stage_output(nc, wo, ident, ot_dram, x3_dram, out):
    STEPS = RC * HK
    GC = 512 // P
    with ExitStack() as ctx:
        a_ = Alloc(nc, ctx, "out")
        wo_nat = [a_.sb(f"wo_nat{v}", [P, IC, REP * D]) for v in range(2)]
        wot_hi = a_.sb("wot_hi", [P, HQ, HID], F32R)
        wot_lo = a_.sb("wot_lo", [P, HQ, HID], F32R)
        o_raw = [a_.sb(f"o_raw{v}", [P, CB, REP, S]) for v in range(2)]
        o_hi = [a_.sb(f"o_hi{v}", [P, REP, CB, S], F32R) for v in range(2)]
        o_lo = [a_.sb(f"o_lo{v}", [P, REP, CB, S], F32R) for v in range(2)]
        y = [a_.sb(f"y_rows{v}", [P, HID]) for v in range(2)]
        w_ps = [a_.ps(f"w{n}") for n in range(REP)]
        y_ps = [a_.ps(f"y{g}") for g in range(GC)]

        wo_loaded = a_.sem("wo_loaded", 2)
        turned = a_.sem("turned")
        w_hi_ready = a_.sem("w_hi_ready")
        w_ready = a_.sem("w_ready")
        o_loaded = a_.sem("o_loaded", 2)
        o_hi_ready = a_.sem("o_hi_ready")
        o_lo_ready = a_.sem("o_lo_ready")
        step_done = a_.sem("step_done")
        product_done = a_.sem("product_done")
        x3_loaded = a_.sem("x3_loaded", 2)
        y_ready = a_.sem("y_ready")
        y_stored = a_.sem("y_stored", 2)
        block = ctx.enter_context(nc.Block())

        @block.sync
        def _(sp):
            def load_wo(v, h):
                sp.dma_start(wo_nat[v][:], wo.rearrange("(c p) e -> p c e", p=P)[:, :, h * (REP * D):(h + 1) * (REP * D)]
                             ).then_inc(wo_loaded[v], 16)

            def load_o(rc, h):
                sp.dma_start(o_raw[h % 2].rearrange("d b r s -> d b (r s)"),
                             ot_dram[bass.ds(rc * CB, CB), :, h, :].rearrange("b d n -> d b n")).then_inc(o_loaded[h % 2], 16)

            def load_x3(rc, g):
                sp.dma_start(y[g % 2][:], x3_dram[bass.ds((rc * GC + g) * P, P)]).then_inc(x3_loaded[g % 2], 16)

            load_wo(0, 0)
            load_o(0, 0)
            load_wo(1, 1)
            load_o(0, 1)
            for g in range(2):
                load_x3(0, g)
            for h in range(2, HK):
                sp.wait_ge(turned, (h - 1) * REP)
                load_wo(h % 2, h)
                sp.wait_ge(o_lo_ready, h - 1)
                load_o(0, h)

            def next_x3(rc, g):
                sp.wait_ge(wo_loaded[0], 16)
                sp.wait_ge(y_stored[g % 2], rc * (8 * GC) + 16 * (g // 2))
                load_x3(rc + g // GC, g % GC)

            def end_chunk(rc, more):
                if more:
                    for h in range(2):
                        sp.wait_ge(wo_loaded[0], 16)
                        sp.wait_ge(o_lo_ready, rc * HK + (HK - 1 + h))
                        load_o(rc + 1, h)
                for g in range(GC):
                    if g >= 2:
                        next_x3(rc, g)
                    sp.wait_ge(wo_loaded[0], 16)
                    sp.wait_ge(y_ready, rc * GC + (g + 1))
                    sp.dma_start(out[bass.ds((rc * GC + g) * P, P)], y[g % 2][:]).then_inc(y_stored[g % 2], 16)
                for g in range(GC, GC + 2):
                    if more:
                        next_x3(rc, g)

            end_chunk(0, True)
            with sp.Fori(1, RC - 1) as rc:
                for h in range(2, HK):
                    sp.wait_ge(wo_loaded[0], 16)
                    sp.wait_ge(o_lo_ready, rc * HK + (h - 1))
                    load_o(rc, h)
                end_chunk(rc, True)
            for h in range(2, HK):
                sp.wait_ge(o_lo_ready, (RC - 1) * HK + (h - 1))
                load_o(RC - 1, h)
            end_chunk(RC - 1, False)
            for v in range(2):
                sp.wait_ge(y_stored[v], 16 * RC * (GC // 2))

        @block.tensor
        def _(pe):
            def turn_weights(h):
                pe.wait_ge(wo_loaded[h % 2], 16 * (h // 2) + 16)
                for r in range(REP):
                    if h:
                        pe.wait_ge(w_ready, (h - 1) * REP + (r + 1))
                    for c in range(IC):
                        last = nc.tensor.transpose(w_ps[r][:, c * P:(c + 1) * P], wo_nat[h % 2][:, c, r * D:(r + 1) * D], ident[:])
                    last.then_inc(turned, 1)

            def products(rc, h, first):
                pe.wait_ge(o_lo_ready, rc * HK + (h + 1))
                for g in range(GC):
                    if h == 0 and not first:
                        pe.wait_ge(y_ready, (rc - 1) * GC + (g + 1))
                    rows = slice(g * GB, (g + 1) * GB)
                    for r in range(REP):
                        hq = h * REP + r
                        for k, (o, w) in enumerate(((o_hi, wot_hi), (o_hi, wot_lo), (o_lo, wot_hi))):
                            last = nc.tensor.matmul(y_ps[g][:], o[h % 2][:, r, rows].rearrange("d b s -> d (b s)"), w[:, hq, :],
                                                    start=(hq == 0 and k == 0), stop=(hq == HQ - 1 and k == 2))
                    if h == HK - 1:
                        last.then_inc(product_done, 1)
                if h < HK - 1:
                    last.then_inc(step_done, 1)

            turn_weights(0)
            for h in range(HK):
                if h < HK - 1:
                    turn_weights(h + 1)
                pe.wait_ge(w_ready, (h + 1) * REP)
                products(0, h, True)
            with pe.Fori(1, RC) as rc:
                for h in range(HK):
                    products(rc, h, False)

        def hi_is_free(engine, rc, h, first):
            if h >= 2:
                engine.wait_ge(step_done, rc * (HK - 1) + (h - 1))
            elif not first and h == 1:
                engine.wait_ge(product_done, rc * GC)
            elif not first:
                engine.wait_ge(step_done, rc * (HK - 1))

        @block.scalar
        def _(act):
            def split_weights(h):
                for r in range(REP):
                    act.wait_ge(turned, h * REP + (r + 1))
                    nc.scalar.activation(wot_hi[:, h * REP + r, :], w_ps[r][:], ACT.Copy).then_inc(w_hi_ready, 1)

            def split(rc, h, first):
                act.wait_ge(o_loaded[h % 2], rc * (8 * HK) + (16 * (h // 2) + 16))
                hi_is_free(act, rc, h, first)
                nc.scalar.activation(o_hi[h % 2][:], o_raw[h % 2].rearrange("d b r s -> d r b s"), ACT.Copy).then_inc(o_hi_ready, 1)

            split_weights(0)
            split(0, 0, True)
            for h in range(1, HK):
                split_weights(h)
                split(0, h, True)
            with act.Fori(1, RC) as rc:
                for h in range(HK):
                    split(rc, h, False)

        @block.vector
        def _(dve):
            def split_weights(h):
                for r in range(REP):
                    dve.wait_ge(w_hi_ready, h * REP + (r + 1))
                    nc.vector.tensor_tensor(wot_lo[:, h * REP + r, :], w_ps[r][:], f32(wot_hi[:, h * REP + r, :]),
                                            ALU.subtract).then_inc(w_ready, 1)

            def split(rc, h):
                dve.wait_ge(o_hi_ready, rc * HK + (h + 1))
                nc.vector.tensor_tensor(o_lo[h % 2][:], o_raw[h % 2].rearrange("d b r s -> d r b s"), f32(o_hi[h % 2][:]),
                                        ALU.subtract).then_inc(o_lo_ready, 1)

            def finish(rc, g):
                v = g % 2
                dve.wait_ge(product_done, rc * GC + (g + 1))
                dve.wait_ge(x3_loaded[v], rc * (8 * GC) + (16 * (g // 2) + 16))
                nc.vector.tensor_tensor(y[v][:], y_ps[g][:], y[v][:], ALU.add).then_inc(y_ready, 1)

            def chunk(rc, more):
                for g in range(GC):
                    finish(rc, g)
                if more:
                    split(rc + 1, 1)

            for h in range(HK):
                split_weights(h)
                split(0, h)
            split(1, 0)
            chunk(0, True)
            with dve.Fori(1, RC - 1) as rc:
                for h in range(2, HK):
                    split(rc, h)
                split(rc + 1, 0)
                chunk(rc, True)
            for h in range(2, HK):
                split(RC - 1, h)
            chunk(RC - 1, False)


INPUTS = ["x", "itok_B_0_15", "itok_B_0_31", "itok_Bx16_0_63", "itok_B_207_1644", "L0_cond_weights",
          "L1_cond_weight", "L2_cond_weights", "L2_cond_biases", "L3_cond_Wq", "L3_cond_Wk", "L3_cond_Wv",
          "L3_cond_Wo", "L3_cond_q_norm_w", "L3_cond_k_norm_w", "L3_cond_k_cache", "L3_cond_v_cache"]


def program(nc, ins, freq, out):
    (x, cond, subj, table, seqlens, w0, w1, w2, b2, wq, wk, wv, wo, qw, kw, kc, vc) = ins

    def scratch(name, shape):
        return nc.dram_tensor(name, shape, F32, kind="Internal").ap()

    x3_dram = scratch("x3_rows", [ROWS, HID])
    x3t_dram = scratch("x3_cols", [P, IC, ROWS])
    kt_dram = scratch("k_cache_t", [PAGES, D, HK, PSIZE])
    vn_dram = scratch("v_new", [ROWS, KVD])
    kn_dram = scratch("k_new_t", [B, D, HK, S])
    qt_dram = scratch("q_t", [HK, D, B, REP * S])
    ot_dram = scratch("o_t", [B, D, HK, REP * S])

    with ExitStack() as ctx:
        ident = ctx.enter_context(nc.sbuf_tensor("ident", [P, P], F32))
        w_nat = ctx.enter_context(nc.sbuf_tensor("w_nat", [P, 1 + REP, HID], F32))
        with nc.sbuf_tensor("adapters", [P, CONDS * IC, HID], F32) as adapters, ExitStack() as ctx_tables:
            tables = [ctx_tables.enter_context(nc.sbuf_tensor(name, shape, dt)) for name, shape, dt in (
                ("cond_ids", [1, B], I32), ("subj_ids", [1, B], I32), ("w0_all", [P, CONDS, S], F32),
                ("w2_all", [P, SUBJ, S], F32), ("bias_rows", [SUBJ, GB, S], F32))]
            stage_prep(nc, w1, cond, subj, w0, w2, b2, ident, adapters, tables)
            stage_maps(nc, x, kc, wv, ident, adapters, tables, w_nat, x3_dram, x3t_dram, kt_dram)
        with nc.sbuf_tensor("stat", [P, B, HK + 1], F32) as stat, nc.sbuf_tensor("v_index", [P, B, PPT], I32) as v_index:
            with (nc.sbuf_tensor("x3t_hi", [P, IC, ROWS], F32R) as x3t_hi, nc.sbuf_tensor("x3t_lo", [P, IC, ROWS], F32R) as x3t_lo,
                  nc.sbuf_tensor("rope", [P, 4, ROWS], F32) as rope):
                stage_values(nc, wv, wq, wk, table, seqlens, freq, qw, kw, ident, x3t_hi, x3t_lo, rope, w_nat, stat, v_index,
                             x3t_dram, vn_dram)
                stage_projection(nc, wq, wk, ident, x3t_hi, x3t_lo, rope, w_nat, stat, qt_dram, kn_dram)
            stage_attention(nc, table, vc, ident, stat, v_index, kt_dram, kn_dram, qt_dram, vn_dram, ot_dram)
        stage_output(nc, wo, ident, ot_dram, x3_dram, out.rearrange("b s t -> (b s) t"))


def kernel(**inputs):
    import concourse.bacc as bacc
    from concourse.bass_utils import run_bass_kernel_spmd

    nc = bacc.Bacc("TRN2", target_bir_lowering=False, num_devices=1)
    arrays, ins = {}, []
    for name in INPUTS:
        a = np.ascontiguousarray(inputs[name])
        arrays[name] = a
        ins.append(nc.dram_tensor(name, a.shape, mybir.dt.from_np(a.dtype), kind="ExternalInput").ap())
    arrays["rope_freq"] = rope_frequencies()
    freq = nc.dram_tensor("rope_freq", (P, 1), F32, kind="ExternalInput").ap()
    out = nc.dram_tensor("out", (B, S, HID), F32, kind="ExternalOutput").ap()
    program(nc, ins, freq, out)
    r = run_bass_kernel_spmd(nc, [arrays], core_ids=[0])
    return r.results[0]["out"]
```
